# Optimizing a Trainium2 kernel written in Bass

```python
import numpy as np
import jax
import jax.numpy as jnp

def _softmax(x, axis=-1):
    return jax.nn.softmax(x, axis=axis)

def _gelu(x):
    return jax.nn.gelu(x, approximate=True)

def _silu(x):
    return jax.nn.silu(x)

def _sigmoid(x):
    return jax.nn.sigmoid(x)

def _layernorm(x, axis=-1, eps=1e-05):
    m = jnp.mean(x, axis=axis, keepdims=True)
    v = jnp.var(x, axis=axis, keepdims=True)
    return (x - m) / jnp.sqrt(v + eps)

def _scatter_add(tgt, idx, src, axis=0):
    return tgt.at[idx].add(src)

def _segment_sum(src, seg, n):
    return jax.ops.segment_sum(src, seg, n)
kernel_name = 'mk_flamingo_gated_d2_seqx_r8_11a623'

def setup_inputs(seed: int=0):
    np.random.seed(seed)
    _w = jnp.asarray

    def _rec_inputs():
        import jax
        import jax.numpy as jnp
        _rk = jax.random.key(seed)
        x = -0.0003929 + 0.9999 * jax.random.normal(jax.random.fold_in(_rk, 1), (16, 128, 128), jnp.float32)
        _lenS = 128 - jax.random.randint(jax.random.fold_in(_rk, 7), (16,), 0, max(1, 128 // 4) + 1, jnp.int32)
        _lenS2 = 128 - jax.random.randint(jax.random.fold_in(_rk, 8), (16,), 0, max(1, 128 // 4) + 1, jnp.int32)
        _ctx_1024P = jax.random.normal(jax.random.fold_in(_rk, 11), (16, 16, 128), jnp.float32)
        _ctx_1024c = jax.random.dirichlet(jax.random.fold_in(_rk, 511), 0.3 * jnp.ones((16,), jnp.float32), (16, 128))
        _ctx_1024t = jnp.einsum('bsk,bkd->bsd', _ctx_1024c, _ctx_1024P)
        _ctx_1024t = _ctx_1024t * jax.lax.rsqrt(jnp.mean(jnp.square(_ctx_1024t)) + 1e-12) * 0.953939
        ctx_1024 = 2.81802e-05 + 1.00001 * (_ctx_1024t + 0.3 * jax.random.normal(jax.random.fold_in(_rk, 611), (16, 128, 128), jnp.float32))
        _g = jax.random.normal(jax.random.fold_in(_rk, 9001), (2, 2), jnp.float32)
        _g = jnp.sign(_g) * jnp.maximum(jnp.abs(_g), 1.0) + (_g == 0) * 1.0
        g_xattn = _g[0]
        g_ffn = _g[1]
        return (x, ctx_1024, g_xattn, g_ffn)
    x, ctx_1024, g_xattn, g_ffn = _rec_inputs()

    def _L0_xattn_setup():
        import jax, jax.numpy as jnp
        import numpy as np
        from functools import partial
        FACTOR = 5
        N_HEADS = 16

        def _time_delay_agg(values, corr):
            B, H, L, C = values.shape
            top_k = int(FACTOR * np.log(L + 1)) if L > 1 else 1
            top_k = max(1, min(top_k, L))
            mean_value = corr.mean(axis=1).mean(axis=1)
            mean_across_batch = mean_value.mean(axis=0)
            actual_k = min(top_k, C)
            _, indices = jax.lax.top_k(mean_across_batch, actual_k)
            selected = mean_value[:, indices]
            weights = jax.nn.softmax(selected, axis=-1)
            t = jnp.arange(L)

            def body(acc, inp):
                d, w = inp
                idx = (t + d) % L
                acc = acc + values[:, :, idx, :] * w[:, None, None, None]
                return (acc, None)
            agg, _ = jax.lax.scan(body, jnp.zeros_like(values), (indices, weights.T))
            return agg
        key = jax.random.key(seed)
        ks = jax.random.split(key, 8)
        B, L, D = (4, 512, 128)
        scale = 0.02
        return {'q': jax.random.normal(ks[0], (B, L, D), jnp.float32), 'k': jax.random.normal(ks[1], (B, L, D), jnp.float32), 'v': jax.random.normal(ks[2], (B, L, D), jnp.float32), 'Wq': jax.random.normal(ks[3], (D, D), jnp.float32) * scale, 'bq': jnp.zeros((D,), jnp.float32), 'Wk': jax.random.normal(ks[4], (D, D), jnp.float32) * scale, 'bk': jnp.zeros((D,), jnp.float32), 'Wv': jax.random.normal(ks[5], (D, D), jnp.float32) * scale, 'bv': jnp.zeros((D,), jnp.float32), 'Wo': jax.random.normal(ks[6], (D, D), jnp.float32) * scale, 'bo': jnp.zeros((D,), jnp.float32)}
    _L0_xattn_all = _L0_xattn_setup()
    _L0_xattn_in = {k: v for k, v in _L0_xattn_all.items() if k in ('Wq', 'bq', 'Wk', 'bk', 'Wv', 'bv', 'Wo', 'bo')}
    del _L0_xattn_all

    def _L0_ffn_setup():
        import jax, jax.numpy as jnp
        import numpy as np
        B, S, DIM, FFN, E = (4, 256, 128, 512, 8)
        key = jax.random.key(seed)
        k0, k1, k2, k3 = jax.random.split(key, 4)
        scale = 0.02
        return {'hidden_states': jax.random.normal(k0, (B, S, DIM), jnp.float32), 'router_w': jax.random.normal(k1, (DIM, E), jnp.float32) * scale, 'router_b': jnp.zeros((E,), jnp.float32), 'w1': jax.random.normal(k2, (E, DIM, 2 * FFN), jnp.float32) * scale, 'w2': jax.random.normal(k3, (E, FFN, DIM), jnp.float32) * scale}
    _L0_ffn_all = _L0_ffn_setup()
    _L0_ffn_in = {k: v for k, v in _L0_ffn_all.items() if k in ('router_w', 'router_b', 'w1', 'w2')}
    del _L0_ffn_all

    def _L1_xattn_setup():
        import jax, jax.numpy as jnp
        import numpy as np
        D_MODEL = 128
        N_HEADS = 16
        HEAD_DIM = D_MODEL // N_HEADS
        key = jax.random.key(seed)
        k1, k2, k3, k4, k5, k6 = jax.random.split(key, 6)
        B, T_q, T_kv = (4, 128, 512)
        s = 1.0 / np.sqrt(D_MODEL)
        return {'query': jax.random.normal(k1, (B, T_q, D_MODEL), dtype=jnp.float32), 'kv_source': jax.random.normal(k2, (B, T_kv, D_MODEL), dtype=jnp.float32), 'w_q': jax.random.normal(k3, (D_MODEL, D_MODEL), dtype=jnp.float32) * s, 'w_k': jax.random.normal(k4, (D_MODEL, D_MODEL), dtype=jnp.float32) * s, 'w_v': jax.random.normal(k5, (D_MODEL, D_MODEL), dtype=jnp.float32) * s, 'w_o': jax.random.normal(k6, (D_MODEL, D_MODEL), dtype=jnp.float32) * s}
    _L1_xattn_all = _L1_xattn_setup()
    _L1_xattn_in = {k: v for k, v in _L1_xattn_all.items() if k in ('w_q', 'w_k', 'w_v', 'w_o')}
    del _L1_xattn_all

    def _L1_ffn_setup():
        import jax, jax.numpy as jnp
        import numpy as np
        HIDDEN = 128
        NUM_EXPERTS = 8
        TOP_K = 2
        B, S = (2, 256)
        key = jax.random.key(seed)
        k1, k2, k3, k4, k5 = jax.random.split(key, 5)
        d, dff, E = (HIDDEN, 4 * HIDDEN, NUM_EXPERTS)
        x = jax.random.normal(k1, (B, S, d), dtype=jnp.float32)
        W1 = jax.random.normal(k2, (E, d, dff), dtype=jnp.float32) * (1.0 / np.sqrt(d))
        b1 = jax.random.normal(k3, (E, dff), dtype=jnp.float32) * 0.01
        W2 = jax.random.normal(k4, (E, dff, d), dtype=jnp.float32) * (1.0 / np.sqrt(dff))
        b2 = jax.random.normal(k5, (E, d), dtype=jnp.float32) * 0.01
        return {'x': x, 'W1': W1, 'b1': b1, 'W2': W2, 'b2': b2}
    _L1_ffn_all = _L1_ffn_setup()
    _L1_ffn_in = {k: v for k, v in _L1_ffn_all.items() if k in ('W1', 'b1', 'W2', 'b2')}
    del _L1_ffn_all
    return {'x': x, 'ctx_1024': ctx_1024, 'g_xattn': g_xattn, 'g_ffn': g_ffn, 'L0_xattn_Wq': _L0_xattn_in['Wq'], 'L0_xattn_bq': _L0_xattn_in['bq'], 'L0_xattn_Wk': _L0_xattn_in['Wk'], 'L0_xattn_bk': _L0_xattn_in['bk'], 'L0_xattn_Wv': _L0_xattn_in['Wv'], 'L0_xattn_bv': _L0_xattn_in['bv'], 'L0_xattn_Wo': _L0_xattn_in['Wo'], 'L0_xattn_bo': _L0_xattn_in['bo'], 'L0_ffn_router_w': _L0_ffn_in['router_w'], 'L0_ffn_router_b': _L0_ffn_in['router_b'], 'L0_ffn_w1': _L0_ffn_in['w1'], 'L0_ffn_w2': _L0_ffn_in['w2'], 'L1_xattn_w_q': _L1_xattn_in['w_q'], 'L1_xattn_w_k': _L1_xattn_in['w_k'], 'L1_xattn_w_v': _L1_xattn_in['w_v'], 'L1_xattn_w_o': _L1_xattn_in['w_o'], 'L1_ffn_W1': _L1_ffn_in['W1'], 'L1_ffn_b1': _L1_ffn_in['b1'], 'L1_ffn_W2': _L1_ffn_in['W2'], 'L1_ffn_b2': _L1_ffn_in['b2']}

def reference(x, ctx_1024, g_xattn, g_ffn, L0_xattn_Wq, L0_xattn_bq, L0_xattn_Wk, L0_xattn_bk, L0_xattn_Wv, L0_xattn_bv, L0_xattn_Wo, L0_xattn_bo, L0_ffn_router_w, L0_ffn_router_b, L0_ffn_w1, L0_ffn_w2, L1_xattn_w_q, L1_xattn_w_k, L1_xattn_w_v, L1_xattn_w_o, L1_ffn_W1, L1_ffn_b1, L1_ffn_W2, L1_ffn_b2):
    import jax
    import jax.numpy as jnp

    def _L0_xattn_ref(q, k, v, Wq, bq, Wk, bk, Wv, bv, Wo, bo):
        import jax, jax.numpy as jnp
        import numpy as np
        from functools import partial
        FACTOR = 5
        N_HEADS = 16

        def _time_delay_agg(values, corr):
            B, H, L, C = values.shape
            top_k = int(FACTOR * np.log(L + 1)) if L > 1 else 1
            top_k = max(1, min(top_k, L))
            mean_value = corr.mean(axis=1).mean(axis=1)
            mean_across_batch = mean_value.mean(axis=0)
            actual_k = min(top_k, C)
            _, indices = jax.lax.top_k(mean_across_batch, actual_k)
            selected = mean_value[:, indices]
            weights = jax.nn.softmax(selected, axis=-1)
            t = jnp.arange(L)

            def body(acc, inp):
                d, w = inp
                idx = (t + d) % L
                acc = acc + values[:, :, idx, :] * w[:, None, None, None]
                return (acc, None)
            agg, _ = jax.lax.scan(body, jnp.zeros_like(values), (indices, weights.T))
            return agg
        B, L, D = q.shape
        H = N_HEADS
        dk = D // H

        def proj(x, W, b):
            y = x @ W.T + b
            return y.reshape(B, L, H, dk).transpose(0, 2, 1, 3)
        Q = proj(q, Wq, bq).astype(jnp.float32)
        K = proj(k, Wk, bk).astype(jnp.float32)
        V = proj(v, Wv, bv).astype(jnp.float32)
        Qf = jnp.fft.rfft(Q, axis=2)
        Kf = jnp.fft.rfft(K, axis=2)
        R = jnp.fft.irfft(Qf * jnp.conj(Kf), n=L, axis=2)
        V_agg = _time_delay_agg(V, R)
        V_agg = V_agg.transpose(0, 2, 1, 3).reshape(B, L, D)
        return V_agg @ Wo.T + bo

    def _L0_ffn_ref(hidden_states, router_w, router_b, w1, w2):
        import jax, jax.numpy as jnp
        import numpy as np
        B, S, DIM, FFN, E = (4, 256, 128, 512, 8)
        b, s, d = hidden_states.shape
        x = hidden_states.reshape(-1, d)
        logits = x @ router_w + router_b
        route = jax.nn.softmax(logits, axis=1)
        max_prob = jnp.max(route, axis=1, keepdims=True)
        max_ind = jnp.argmax(route, axis=1)
        out = jnp.zeros_like(x)
        num_experts = w1.shape[0]
        for e in range(num_experts):
            h = x @ w1[e]
            a, g = jnp.split(h, 2, axis=1)
            y = jax.nn.silu(a) * g @ w2[e]
            out = jnp.where((max_ind == e)[:, None], y, out)
        out = out * max_prob
        return out.reshape(b, s, d)

    def _L1_xattn_ref(query, kv_source, w_q, w_k, w_v, w_o):
        import jax, jax.numpy as jnp
        import numpy as np
        D_MODEL = 128
        N_HEADS = 16
        HEAD_DIM = D_MODEL // N_HEADS
        B, T_q, _ = query.shape
        T_kv = kv_source.shape[1]
        q = (query @ w_q.T).reshape(B, T_q, N_HEADS, HEAD_DIM)
        k = (kv_source @ w_k.T).reshape(B, T_kv, N_HEADS, HEAD_DIM)
        v = (kv_source @ w_v.T).reshape(B, T_kv, N_HEADS, HEAD_DIM)
        scale = HEAD_DIM ** (-0.5)
        attn = jax.nn.softmax(jnp.einsum('bqhd,bkhd->bhqk', q, k) * scale, axis=-1)
        out = jnp.einsum('bhqk,bkhd->bqhd', attn, v).reshape(B, T_q, D_MODEL)
        return out @ w_o.T

    def _L1_ffn_ref(x, W1, b1, W2, b2):
        import jax, jax.numpy as jnp
        import numpy as np
        HIDDEN = 128
        NUM_EXPERTS = 8
        TOP_K = 2
        B, S = (2, 256)
        Bm, Sm, d = x.shape
        E = W1.shape[0]
        x_flat = x.reshape(-1, d)
        h = jnp.mod(x_flat[:, :TOP_K].sum(axis=1).astype(jnp.int32), E)
        sel = jnp.stack([h, jnp.mod(h + 1, E)], axis=1)

        def step(acc, params):
            e, W1e, b1e, W2e, b2e = params
            w = jnp.any(sel == e, axis=1).astype(x.dtype) / TOP_K
            y = jnp.maximum(x_flat @ W1e + b1e, 0.0) @ W2e + b2e
            return (acc + w[:, None] * y, None)
        init = jnp.zeros_like(x_flat)
        out_flat, _ = jax.lax.scan(step, init, (jnp.arange(E), W1, b1, W2, b2))
        return out_flat.reshape(Bm, Sm, d)
    x = x + jnp.tanh(g_xattn[0]) * _L0_xattn_ref(_layernorm(x, axis=-1), ctx_1024, ctx_1024, L0_xattn_Wq, L0_xattn_bq, L0_xattn_Wk, L0_xattn_bk, L0_xattn_Wv, L0_xattn_bv, L0_xattn_Wo, L0_xattn_bo)
    x = x + jnp.tanh(g_ffn[0]) * _L0_ffn_ref(_layernorm(x, axis=-1), L0_ffn_router_w, L0_ffn_router_b, L0_ffn_w1, L0_ffn_w2)
    x = x + jnp.tanh(g_xattn[1]) * _L1_xattn_ref(_layernorm(x, axis=-1), ctx_1024, L1_xattn_w_q, L1_xattn_w_k, L1_xattn_w_v, L1_xattn_w_o)
    x = x + jnp.tanh(g_ffn[1]) * _L1_ffn_ref(_layernorm(x, axis=-1), L1_ffn_W1, L1_ffn_b1, L1_ffn_W2, L1_ffn_b2)
    return x

_drawn_inputs = setup_inputs


def setup_inputs(seed=0):
    import zlib

    import numpy as np

    out = dict(_drawn_inputs(seed))
    spreads = {'g_ffn': (-1.0, 0.6),
     'L0_xattn_bq': (0.0, 0.273),
     'L0_xattn_bk': (0.0, 0.372),
     'L0_xattn_bv': (0.0, 0.277),
     'L0_xattn_bo': (0.0, 0.1),
     'L0_ffn_router_b': (0.0, 0.8)}
    factors = {'L0_xattn_Wq': 7.523,
     'L0_xattn_Wk': 2.684,
     'L0_ffn_router_w': 4.844,
     'L0_ffn_w1': 4.907,
     'L0_ffn_w2': 4.055,
     'L1_ffn_b1': 8.0,
     'L1_ffn_b2': 8.0}
    for name, (base, spread) in spreads.items():
        noise = np.random.default_rng([zlib.crc32(name.encode()), seed]).standard_normal(out[name].shape)
        drawn = base * np.exp(spread * noise) if base else spread * noise
        out[name] = jnp.asarray(drawn.astype(out[name].dtype))
    for name, factor in factors.items():
        out[name] = (out[name] * factor).astype(out[name].dtype)
    return out
```

```python
import numpy as np
import concourse.bass as bass
from concourse import mybir
from contextlib import ExitStack

STOP = "end"


class Chain:

    def __init__(self, eng, sem):
        self.eng, self.sem, self.base, self.k, self.inside = eng, sem, 0, 0, None

    def link(self, ins):
        ins.then_inc(self.sem, 1)
        self.k += 1
        self.eng.wait_ge(self.sem, self.base + self.k)

    def enter(self, i, per):
        self.inside = (self.base + self.k, per)
        self.base, self.k = self.base + self.k + i * per, 0

    def leave(self, turns):
        start, per = self.inside
        assert self.k == per, (self.k, per)
        self.base, self.k, self.inside = start + per * turns, 0, None


def build(nc, A, out):
    f32, bf16, i32 = mybir.dt.float32, mybir.dt.bfloat16, mybir.dt.int32
    ALU, ACT, AX = mybir.AluOpType, mybir.ActivationFunctionType, mybir.AxisListType.X
    ds = bass.ds

    NB, T, D = A["x"].shape
    H, HD = 16, 8
    NE = A["rw"].shape[1]
    F0, F1 = A["w2_0"].shape[1], A["w2_1"].shape[1]
    C0, C1 = F0 // T, F1 // T
    G, GB = 4, NB // 4
    GT = GB * T
    NTOK = NB * T
    K = NTOK // T + NE - 1
    EPS = 1e-5
    ROUND = 1.5 * 2.0 ** 23
    PARTS = 3
    SK = PARTS * PARTS * HD
    HU = H // 2
    NU = 2 * NB
    VW = 32

    ctx = ExitStack()

    def sb(name, shape, dt=f32):
        return ctx.enter_context(nc.sbuf_tensor(name, shape, dt))

    def sem(name):
        return ctx.enter_context(nc.semaphore(name))

    def bc(ap, at, n):
        shape = list(ap.shape)
        return ap.unsqueeze(at).broadcast_to(shape[:at] + [n] + shape[at:])

    def scratch(name, shape, dt=f32):
        return nc.dram_tensor(name, shape, dt, kind="Internal").ap()

    with ctx:
        band_d = scratch("band_d", (NB, 2 * T))
        kstack_d = scratch("kstack_d", (PARTS, PARTS, HD * H, NTOK), bf16)
        qstack_d = scratch("qstack_d", (PARTS, PARTS, HD * H, NTOK), bf16)
        slots_d = scratch("slots_d", (K, T, D))
        slots1_d = scratch("slots1_d", (K, T, D))
        ys_d = scratch("ys_d", (K, T, D))
        ys1_d = scratch("ys1_d", (K, T, D))
        b2pair_d = scratch("b2pair_d", (NE, D))

        bank = [ctx.enter_context(nc.psum_tensor(f"bank{i}", [128, 512], f32)) for i in range(4)]
        pairA = ctx.enter_context(nc.psum_tensor("pairA", [128, 2, 512], f32))
        pairB = ctx.enter_context(nc.psum_tensor("pairB", [128, 2, 512], f32))
        bank += [pairA[:, 0, :], pairA[:, 1, :], pairB[:, 0, :], pairB[:, 1, :]]
        for i in range(4):
            bank[i] = bank[i][:, :]
        mTp = bank[0].bitcast(bf16)[0:PARTS * HU, 0:T]

        ident = sb("ident", [128, 128])
        before = sb("before", [128, 128], bf16)
        onesb = sb("onesb", [128, 128], bf16)
        onesf = sb("onesf", [128, 128])
        onehot_b = sb("onehot_b", [128, NB, NB])
        pick = sb("pick", [PARTS * HU, HU, T], bf16)
        iota_e = sb("iota_e", [128, NE])
        iota_tile = sb("iota_tile", [1, 24])
        gates = sb("gates", [128, 4])
        tg = sb("tg", [128, 4])
        wq0, wk0, wv0, wo0 = (sb(n, [128, 128]) for n in ("wq0", "wk0", "wv0", "wo0"))
        wq1, wk1, wv1, wo1 = (sb(n, [128, 128]) for n in ("wq1", "wk1", "wv1", "wo1"))
        bqk = sb("bqk", [1, 2, 128])
        bo_row = sb("bo_row", [1, 128])
        bv_col = sb("bv_col", [128, 1])
        rw = sb("rw", [128, NE])
        rb = sb("rb", [128, NE])
        len_row = sb("len_row", [1, 128])
        b2a = sb("b2a", [NE, D])
        b2b = sb("b2b", [NE, D])
        x = sb("x", [128, NB, D])
        xn = sb("xn", [128, NB, D])
        ctx_s = sb("ctx_s", [128, NB, D])
        big = sb("big", [128, NB, 128])
        ctxT = sb("ctxT", [128, NTOK])
        vals = sb("vals", [128, NB, D])
        vpad = sb("vpad", [128, 2, H, VW])
        qs = sb("qs", [SK, 2, H, 2 * T], bf16)
        ks = sb("ks", [SK, 2, H, 2 * T], bf16)
        prob = sb("prob", [128, 2, HU, T])
        negm = sb("negm", [128, 2, HU])
        mparts = sb("mparts", [128, 2, PARTS, HU], bf16)
        mrow = sb("mrow", [PARTS * HU, 2, T], bf16)
        osb = sb("osb", [128, 512])
        rl = sb("rl", [128, H])
        an = sb("an", [128, D])
        anT = sb("anT", [128, T])
        identb = sb("identb", [128, 128], bf16)
        st = sb("st", [128, NB, 6])
        lnv = sb("lnv", [128, 8, NB])
        lni = sb("lni", [128, NB], i32)
        sums = sb("sums", [NB, 2, 128])
        sumsT = sb("sumsT", [128, 2, NB])
        ks_sb = sb("ks_sb", [NB, 128])
        prod = sb("prod", [NB, 128])
        sm = sb("sm", [NB, 5, HD])
        band = sb("band", [NB, 2 * T])
        wvo = sb("wvo", [128, 128])
        bvo = sb("bvo", [128, 128])
        gt = sb("gt", [128, 2, 512])
        p1 = sb("p1", [128, PARTS, GT], bf16)
        res = sb("res", [128, 2, GT])
        logit = sb("logit", [128, NB, NE])
        lw = sb("lw", [128, 3, NB, NE])
        oh = sb("oh", [128, NB, NE])
        ohb = sb("ohb", [128, NB + 1, NE], bf16)
        r16 = sb("r16", [128, 8, NB])
        cnt = sb("cnt", [128, 3, NE])
        pre = sb("pre", [128, 4, 4 + NE])
        slot_i = sb("slot_i", [128, NB], i32)
        te_f = sb("te_f", [1, 24, NE])
        te_r = sb("te_r", [1, 3, 24])
        te_i = sb("te_i", [1, 2, 24], i32)
        maxp = sb("maxp", [128, NB])
        w1r = sb("w1r", [128, 2, 2 * F0])
        w2r = sb("w2r", [128, 2, C0, D])
        b1r = sb("b1r", [128, 2, C1])
        b2r = sb("b2r", [128, 2, D])
        xt = sb("xt", [128, 2, D])
        xtT = sb("xtT", [128, 2, T])
        sil = sb("sil", [128, 2, F0])
        act = sb("act", [128, 2, C0, T])
        ysb = sb("ysb", [128, 2, D])

        S = {}

        def s(name):
            if name not in S:
                S[name] = sem("s_" + name)
            return S[name]

        PE, DV, AC, SP, PO = [], [], [], [], []
        ch = {}

        def chain(eng, name):
            if name not in ch:
                ch[name] = Chain(eng, s("chain_" + name))
            return ch[name]

        def layernorm(tag, ready):
            def dve(eng):
                c = chain(eng, "dve")
                with eng.Fori(0, G) as g:
                    c.enter(g, 1)
                    ready(eng, g)
                    for j in range(GB):
                        i = eng.bn_stats(st[:, ds(g * GB + j, 1), :].rearrange("p a d -> p (a d)"),
                                         x[:, ds(g * GB + j, 1), :].rearrange("p a d -> p (a d)"))
                    c.link(i)
                c.leave(G)
                me, mo, ve, vo = (st[:, :, k] for k in (1, 4, 2, 5))
                diff, total, var, y, t, u, mean = (lnv[:, k, :] for k in range(7))
                eng.tensor_tensor(diff, me, mo, ALU.subtract)
                eng.tensor_tensor(total, me, mo, ALU.add)
                c.link(eng.tensor_tensor(var, ve, vo, ALU.add))
                eng.tensor_scalar(mean, total, 0.5, None, ALU.mult)
                c.link(eng.tensor_tensor(t, diff, diff, ALU.mult))
                c.link(eng.scalar_tensor_tensor(u, t, D / 4.0, var, ALU.mult, ALU.add))
                c.link(eng.tensor_scalar(var, u, 1.0 / D, EPS, ALU.mult, ALU.add))
                c.link(eng.tensor_scalar(lni[:, :], var.bitcast(i32), 1, None, ALU.logical_shift_right))
                c.link(eng.tensor_scalar(y.bitcast(i32), lni[:, :], -1.0, float(0x5F3759DF), ALU.mult, ALU.add))
                for _ in range(4):
                    c.link(eng.tensor_tensor(t, y, y, ALU.mult))
                    c.link(eng.scalar_tensor_tensor(u, t, -0.5, var, ALU.mult, ALU.mult))
                    c.link(eng.scalar_tensor_tensor(y, u, 1.5, y, ALU.add, ALU.mult))
                with eng.Fori(0, G) as g:
                    for j in range(GB):
                        i = eng.tensor_scalar(xn[:, ds(g * GB + j, 1), :].rearrange("p a d -> p (a d)"),
                                              x[:, ds(g * GB + j, 1), :].rearrange("p a d -> p (a d)"),
                                              lnv[:, 6, ds(g * GB + j, 1)], lnv[:, 3, ds(g * GB + j, 1)],
                                              ALU.subtract, ALU.mult)
                    i.then_inc(s("xn_" + tag), 1)
                eng.wait_ge(s("xn_" + tag), G)
            DV.append(dve)

        def loads_sp(eng):
            for g in range(G):
                eng.dma_start(x[:, g * GB:(g + 1) * GB, :], A["x"][g * GB:(g + 1) * GB].rearrange("b t d -> t b d")).then_inc(s("x"), 16)
            for n, t in (("wv0", wv0), ("wo0", wo0), ("wq0", wq0), ("wk0", wk0)):
                eng.dma_start(t[:, :], A[n]).then_inc(s("w0"), 16)
            eng.dma_start(bqk[:, 0, :], A["bq"]).then_inc(s("w0"), 16)
            eng.dma_start(bqk[:, 1, :], A["bk"]).then_inc(s("w0"), 16)
            eng.dma_start(bo_row[:, :], A["bo"]).then_inc(s("w0"), 16)
            eng.dma_start(bv_col[:, :], A["bv"]).then_inc(s("w0"), 16)
            for n, t in (("wk1", wk1), ("wv1", wv1), ("wq1", wq1), ("wo1", wo1)):
                eng.dma_start(t[:, :], A[n]).then_inc(s("w1"), 16)
            eng.dma_start(rw[:, :], A["rw"]).then_inc(s("w1"), 16)
            eng.dma_start(rb[:, :], A["rb"].broadcast_to((128, NE))).then_inc(s("w1"), 16)
            eng.dma_start(b2a[:, :], A["b2"]).then_inc(s("w1"), 16)
            eng.dma_start(b2b[0:NE - 1, :], A["b2"][1:NE, :]).then_inc(s("w1"), 16)
            eng.dma_start(b2b[NE - 1:NE, :], A["b2"][0:1, :]).then_inc(s("w1"), 16)
        SP.append(loads_sp)

        def loads_act(eng):
            eng.dma_start(gates[:, :], A["gates"].broadcast_to((128, 4))).then_inc(s("gates"), 16)
            for g in range(G):
                eng.dma_start(ctx_s[:, g * GB:(g + 1) * GB, :], A["ctx"][g * GB:(g + 1) * GB].rearrange("b t d -> t b d")).then_inc(s("ctx"), 16)
            eng.wait_ge(s("gates"), 16)
            eng.activation(tg[:, :], gates[:, :], ACT.Tanh).then_inc(s("tg"), 1)
        AC.append(loads_act)

        def consts(eng):
            eng.memset(ident[:, :], 0.0).then_inc(s("c0"), 1)
            eng.wait_ge(s("c0"), 1)
            eng.affine_select(out=ident[:, :], in_=ident[:, :], compare_op=ALU.not_equal, fill=1.0,
                              base=0, pattern=[[-1, 128]], channel_multiplier=1).then_inc(s("ident"), 1)
            eng.memset(onehot_b[:, :, :], 0.0).then_inc(s("c0"), 1)
            eng.memset(onesf[:, :], 1.0)
            eng.memset(len_row[:, :], float(T))
            eng.wait_ge(s("c0"), 2)
            eng.affine_select(out=onehot_b[:, :, :], in_=onehot_b[:, :, :], compare_op=ALU.not_equal, fill=1.0,
                              base=0, pattern=[[1, NB], [-1, NB]], channel_multiplier=0).then_inc(s("onehot"), 1)
            eng.memset(onesb[:, :], 1.0)
            eng.memset(before[:, :], 1.0)
            eng.memset(pick[:, :, :], 0.0)
            eng.iota(iota_e[:, :], pattern=[[1, NE]], base=0, channel_multiplier=0, allow_small_or_imprecise_dtypes=True)
            eng.iota(iota_tile[:, :], pattern=[[T, 24]], base=0, channel_multiplier=0, allow_small_or_imprecise_dtypes=True)
            eng.memset(ohb[:, :, :], 0.0)
            eng.memset(pre[:, :, :], 0.0)
            eng.memset(band[:, :], 0.0).then_inc(s("c0"), 1)
            eng.wait_ge(s("c0"), 3)
            eng.affine_select(out=before[:, :], in_=before[:, :], compare_op=ALU.is_gt, fill=0.0,
                              base=0, pattern=[[1, 128]], channel_multiplier=-1)
            for i in range(PARTS):
                eng.affine_select(out=pick[:, :, :], in_=pick[:, :, :], compare_op=ALU.not_equal, fill=1.0,
                                  base=-i * HU, pattern=[[-1, HU], [0, T]], channel_multiplier=1).then_inc(s("c0"), 1)
                eng.wait_ge(s("c0"), 4 + i)
            eng.tensor_copy(identb[:, :], ident[:, :])
            eng.memset(vpad[:, :, :, :], 0.0).then_inc(s("c0"), 1)
            eng.wait_ge(s("c0"), 4 + PARTS)
            eng.memset(vpad[:, :, :, HD:HD + 1], 1.0).then_inc(s("consts"), 1)
            eng.memset(big[:, :, :], 0.0).then_inc(s("zero"), 1)
            eng.wait_ge(s("zero"), 1)
            for dst in (slots_d, slots1_d):
                v = dst.rearrange("k t d -> t k d")
                eng.dma_start(v[:, 0:NB, :], big[:, :, :]).then_inc(s("zeroed"), 16)
                eng.dma_start(v[:, NB:K, :], big[:, 0:K - NB, :]).then_inc(s("zeroed"), 16)
            eng.wait_ge(s("w1"), 16 * 9)
            eng.tensor_tensor(b2a[:, :], b2a[:, :], b2b[:, :], ALU.add).then_inc(s("b2pair"), 1)
            eng.wait_ge(s("b2pair"), 1)
            eng.dma_start(b2pair_d, b2a[:, :]).then_inc(s("b2pair_d"), 16)
            eng.wait_ge(s("b2pair_d"), 16)
        PO.append(consts)

        layernorm("a", lambda eng, g: (eng.wait_ge(s("x"), 16 * G), eng.wait_ge(s("ident"), 1)))

        def a_pe(eng):
            eng.wait_ge(s("ident"), 1)
            eng.wait_ge(s("onehot"), 1)
            eng.wait_ge(s("ctx"), 16 * G)
            for g in range(G):
                if g >= 2:
                    eng.wait_ge(s("ctxT"), g - 1)
                for j in range(GB):
                    i = eng.transpose(bank[g % 2][:, j * T:(j + 1) * T], ctx_s[:, g * GB + j, :], ident[:, :])
                i.then_inc(s("ctxTp"), 1)
            for b in range(NB):
                i = eng.matmul(bank[2][0:NB, 0:D], onehot_b[:, b, :], ctx_s[:, b, :], start=(b == 0), stop=(b == NB - 1))
            i.then_inc(s("csum"), 1)
            eng.wait_ge(s("w0"), 16 * 8)
            eng.matmul(bank[3][:, 0:128], wv0[:, :], wo0[:, :], start=True, stop=True)
            eng.matmul(bank[3][:, 128:256], bv_col[:, 0:1].broadcast_to((128, 128)), wo0[:, :], start=True, stop=False)
            eng.matmul(bank[3][:, 128:256], onesf[0:1, :], bo_row[:, :], start=False, stop=True).then_inc(s("wvop"), 1)
            for b in range(NB):
                if b % GB == 0:
                    eng.wait_ge(s("xn_a"), b // GB + 1)
                i = eng.matmul(bank[4][0:NB, 0:D], onehot_b[:, b, :], xn[:, b, :], start=(b == 0), stop=(b == NB - 1))
            i.then_inc(s("xsum"), 1)
            eng.wait_ge(s("sums"), 2)
            for j in range(2):
                i = eng.transpose(bank[5][:, j * NB:(j + 1) * NB], sums[:, j, :], ident[0:NB, 0:NB])
            i.then_inc(s("sumsTp"), 1)
            eng.wait_ge(s("sumsT"), 1)
            for j, w in enumerate((wq0, wk0)):
                eng.matmul(bank[6 + j][0:NB, 0:128], sumsT[:, j, :], w[:, :], start=True, stop=False)
                i = eng.matmul(bank[6 + j][0:NB, 0:128], len_row[0:1, 0:NB], bqk[0:1, j, :], start=False, stop=True)
            i.then_inc(s("qksum"), 1)
        PE.append(a_pe)

        def a_act(eng):
            for g in range(G):
                eng.wait_ge(s("ctxTp"), g + 1)
                eng.activation(ctxT[:, g * GT:(g + 1) * GT], bank[g % 2], ACT.Copy).then_inc(s("ctxT"), 1)
            eng.wait_ge(s("csum"), 1)
            eng.activation(sums[:, 1, :], bank[2][0:NB, 0:D], ACT.Copy).then_inc(s("sums"), 1)
            eng.wait_ge(s("wvop"), 1)
            eng.wait_ge(s("tg"), 1)
            eng.wait_ge(s("w1"), 16 * 9)
            eng.activation(wvo[:, :], bank[3][:, 0:128], ACT.Copy, scale=tg[:, 0:1])
            eng.activation(wo1[:, :], wo1[:, :], ACT.Copy, scale=tg[:, 1:2])
            eng.activation(bvo[:, :], bank[3][:, 128:256], ACT.Copy, scale=tg[:, 0:1]).then_inc(s("wvo"), 1)
            eng.wait_ge(s("xsum"), 1)
            eng.activation(sums[:, 0, :], bank[4][0:NB, 0:D], ACT.Copy).then_inc(s("sums"), 1)
            eng.wait_ge(s("sumsTp"), 1)
            eng.activation(sumsT[:, :, :], bank[5][:, 0:2 * NB].rearrange("p (j b) -> p j b", j=2), ACT.Copy).then_inc(s("sumsT"), 1)
            eng.wait_ge(s("corr"), 1)
            eng.activation(sm[:, 3, :], sm[:, 0, :], ACT.Exp, bias=sm[:, 2, 0:1], scale=1.0 / (H * T)).then_inc(s("corre"), 1)
        AC.append(a_act)

        def a_dve(eng):
            c = chain(eng, "dve")
            eng.wait_ge(s("qksum"), 1)
            c.link(eng.tensor_copy(ks_sb[:, :], bank[7][0:NB, 0:128]))
            c.link(eng.tensor_tensor(prod[:, :], bank[6][0:NB, 0:128], ks_sb[:, :], ALU.mult))
            c.link(eng.reduce_sum(sm[:, 0, :], prod[:, :].rearrange("p (h c) -> p c h", c=HD), AX))
            c.link(eng.reduce_max(sm[:, 1, 0:1], sm[:, 0, :], AX))
            eng.tensor_scalar(sm[:, 2, 0:1], sm[:, 1, 0:1], -1.0 / (H * T), None, ALU.mult).then_inc(s("corr"), 1)
            eng.wait_ge(s("corre"), 1)
            c.link(eng.reduce_sum(sm[:, 4, 0:1], sm[:, 3, :], AX))
            c.link(eng.reciprocal(sm[:, 4, 1:2], sm[:, 4, 0:1]))
            eng.wait_ge(s("consts"), 1)
            eng.tensor_scalar(band[:, T - HD:T], sm[:, 3, :], sm[:, 4, 1:2], None, ALU.mult)
            eng.tensor_scalar(band[:, 2 * T - HD:2 * T - 1], sm[:, 3, 0:HD - 1], sm[:, 4, 1:2], None, ALU.mult).then_inc(s("band"), 1)
        DV.append(a_dve)

        def a_pool(eng):
            eng.wait_ge(s("wvo"), 1)
            eng.wait_ge(s("xn_a"), G)
            eng.tensor_tensor(x[:, :, :], x[:, :, :], bc(bvo[:, :], 1, NB), ALU.add).then_inc(s("xb"), 1)
        PO.append(a_pool)

        def a_sp(eng):
            eng.wait_ge(s("band"), 1)
            eng.dma_start(band_d, band[:, :]).then_inc(s("band_d"), 16)
            eng.wait_ge(s("band_d"), 16)
            eng.wait_ge(s("zeroed"), 64)
            src = bass.AP(band_d.tensor, 0, [[1, T], [2 * T, NB], [1, T]])
            for g in range(G):
                eng.dma_start(big[:, g * GB:(g + 1) * GB, :], src[:, g * GB:(g + 1) * GB, :]).then_inc(s(f"C{g}"), 16)
        SP.append(a_sp)

        def split(tag, wait_psum, psum, scale, free, done):
            pass

        def kv_pe(eng):
            eng.wait_ge(s("w1"), 16 * 9)
            for g in range(G):
                eng.wait_ge(s("ctxT"), G)
                if g >= 1:
                    eng.wait_ge(s("kp"), g)
                eng.matmul(bank[0], wk1[:, :], ctxT[:, g * GT:(g + 1) * GT], start=True, stop=True).then_inc(s("kproj"), 1)
                if g >= 1:
                    eng.wait_ge(s("v"), g)
                for j in range(GB):
                    i = eng.matmul(bank[1][:, j * 128:(j + 1) * 128], ctxT[:, g * GT + j * T:g * GT + (j + 1) * T], wv1[:, :],
                                   start=True, stop=True)
                i.then_inc(s("vproj"), 1)
        PE.append(kv_pe)

        def kv_act(eng):
            for g in range(G):
                eng.wait_ge(s("kproj"), g + 1)
                if g >= 1:
                    eng.wait_ge(s("kstack_d"), 16 * PARTS * g)
                eng.activation(p1[:, 0, :], bank[0], ACT.Copy).then_inc(s("k1"), 1)
                eng.wait_ge(s("vproj"), g + 1)
                eng.activation(vals[:, g * GB:(g + 1) * GB, :],
                               bank[1].rearrange("p (b d) -> p b d", b=GB), ACT.Copy).then_inc(s("v"), 1)
                eng.wait_ge(s("kr1"), g + 1)
                eng.activation(p1[:, 1, :], res[:, 0, :], ACT.Copy).then_inc(s("k2"), 1)
                eng.wait_ge(s("kp"), g + 1)
                for i in range(PARTS):
                    eng.dma_start(kstack_d[:, i, :, g * GT:(g + 1) * GT].rearrange("j p t -> p j t"), p1[:, :, :])\
                       .then_inc(s("kstack_d"), 16)
        AC.append(kv_act)

        def kv_dve(eng):
            for g in range(G):
                eng.wait_ge(s("k1"), g + 1)
                eng.tensor_tensor(res[:, 0, :], bank[0], p1[:, 0, :], ALU.subtract).then_inc(s("kr1"), 1)
                eng.wait_ge(s("k2"), g + 1)
                eng.tensor_tensor(p1[:, 2, :], res[:, 0, :], p1[:, 1, :], ALU.subtract).then_inc(s("kp"), 1)
        DV.append(kv_dve)

        def ctxmix_pe(eng):
            for g in range(G):
                eng.wait_ge(s(f"C{g}"), 16)
                if g >= 2:
                    eng.wait_ge(s("gt"), g - 1)
                for j in range(GB):
                    b = g * GB + j
                    i = eng.matmul(bank[2 + g % 2][:, j * T:(j + 1) * T], ctx_s[:, b, :], big[:, b, :], start=True, stop=True)
                i.then_inc(s("gtp"), 1)
                eng.wait_ge(s("gt"), g + 1)
                if g >= 2:
                    eng.wait_ge(s("x1"), g - 1)
                for j in range(GB):
                    i = eng.matmul(bank[4 + g % 2][:, j * D:(j + 1) * D], gt[:, g % 2, j * T:(j + 1) * T], wvo[:, :], start=True, stop=True)
                i.then_inc(s("mix"), 1)
        PE.append(ctxmix_pe)

        def ctxmix_act(eng):
            for g in range(G):
                eng.wait_ge(s("gtp"), g + 1)
                if g >= 2:
                    eng.wait_ge(s("mix"), g - 1)
                eng.activation(gt[:, g % 2, :], bank[2 + g % 2], ACT.Copy).then_inc(s("gt"), 1)
        AC.append(ctxmix_act)

        def ctxmix_dve(eng):
            eng.wait_ge(s("xb"), 1)
            for g in range(G):
                eng.wait_ge(s("mix"), g + 1)
                v = x[:, g * GB:(g + 1) * GB, :].rearrange("p b d -> p (b d)")
                eng.tensor_tensor(v, bank[4 + g % 2], v, ALU.add).then_inc(s("x1"), 1)
        DV.append(ctxmix_dve)

        def finish(eng):
            eng.wait_ge(s("final"), 1)
            eng.dma_start(out.rearrange("b t d -> t b d"), x[:, :, :]).then_inc(s("out"), 16)
            eng.wait_ge(s("out"), 16)

        def done():
            def last(eng):
                eng.wait_ge(s("out"), 16)
            DV.append(lambda eng: chain(eng, "dve").link(eng.tensor_copy(lnv[:, 0, 0:1], ident[:, 0:1])))
            DV.append(lambda eng: eng.tensor_copy(lnv[:, 1, 0:1], ident[:, 0:1]).then_inc(s("final"), 1))
            SP.append(finish)

        def emit():
            with nc.Block() as block:
                for deco, steps in ((block.tensor, PE), (block.vector, DV), (block.scalar, AC), (block.sync, SP), (block.gpsimd, PO)):
                    def body(eng, steps=steps):
                        for f in steps:
                            f(eng)
                    deco(body)

        if STOP == "A":
            DV.append(lambda eng: eng.wait_ge(s("x1"), G))
            SP.append(lambda eng: [eng.wait_ge(s("kstack_d"), 16 * G * PARTS)])
            done()
            emit()
            return

        def nearest(eng, c, dst, src):
            c.link(eng.tensor_scalar(dst, src, ROUND, None, ALU.add))
            c.link(eng.tensor_scalar(dst, dst, -ROUND, None, ALU.add))

        def route(tag):
            def pe(eng):
                eng.wait_ge(s("oh_" + tag), 1)
                eng.matmul(bank[3][:, 0:(NB + 1) * NE], before[:, :], ohb[:, :, :].rearrange("p b e -> p (b e)"), start=True, stop=False)
                for b in range(NB):
                    i = eng.matmul(bank[3][:, (b + 1) * NE:(NB + 1) * NE].rearrange("p (b e) -> p b e", e=NE), onesb[:, :],
                                   bc(ohb[:, b, :], 1, NB - b), start=False, stop=(b == NB - 1))
                i.then_inc(s("rank_" + tag), 1)
            PE.append(pe)

            def dve(eng):
                c = chain(eng, "dve")
                eng.wait_ge(s("rank_" + tag), 1)
                c.link(eng.tensor_scalar(cnt[:, 0, :], bank[3][:, NB * NE:(NB + 1) * NE], 1.0 / T, None, ALU.mult))
                nearest(eng, c, cnt[:, 1, :], cnt[:, 0, :])
                c.link(eng.tensor_tensor(cnt[:, 2, :], cnt[:, 1, :], cnt[:, 0, :], ALU.is_lt))
                c.link(eng.tensor_tensor(cnt[:, 0, :], cnt[:, 1, :], cnt[:, 2, :], ALU.add))
                c.link(eng.tensor_scalar(pre[:, 0, 4:4 + NE], cnt[:, 0, :], float(T), None, ALU.mult))
                for n, d in enumerate((1, 2, 4)):
                    c.link(eng.tensor_tensor(pre[:, n + 1, 4:4 + NE], pre[:, n, 4:4 + NE], pre[:, n, 4 - d:4 + NE - d], ALU.add))
                c.link(eng.tensor_tensor(cnt[:, 2, :], pre[:, 3, 4:4 + NE], pre[:, 0, 4:4 + NE], ALU.subtract))
                c.link(eng.tensor_tensor(lw[:, 0, :, :], bank[3][:, 0:NB * NE].rearrange("p (b e) -> p b e", e=NE),
                                         bc(cnt[:, 2, :], 1, NB), ALU.add))
                c.link(eng.tensor_tensor(lw[:, 1, :, :], lw[:, 0, :, :], oh[:, :, :], ALU.mult))
                c.link(eng.reduce_sum(r16[:, 0, :], lw[:, 1, :, :], AX))
                eng.tensor_copy(slot_i[:, :], r16[:, 0, :]).then_inc(s("slot_" + tag), 1)
                c.link(eng.tensor_tensor(te_f[:, :, :], bc(pre[0:1, 3, 4:4 + NE], 1, 24), bc(iota_tile[:, :], 2, NE), ALU.is_le))
                c.link(eng.reduce_sum(te_r[:, 0, :], te_f[:, :, :], AX))
                c.link(eng.tensor_scalar(te_r[:, 1, :], te_r[:, 0, :], float(NE - 1), None, ALU.min))
                c.link(eng.tensor_scalar(te_r[:, 0, :], te_r[:, 1, :], float(NE - 1), -float(NE), ALU.is_ge, ALU.mult))
                c.link(eng.scalar_tensor_tensor(te_r[:, 2, :], te_r[:, 1, :], 1.0, te_r[:, 0, :], ALU.add, ALU.add))
                eng.tensor_copy(te_i[:, 0, :], te_r[:, 1, :])
                eng.tensor_copy(te_i[:, 1, :], te_r[:, 2, :]).then_inc(s("te_" + tag), 1)
            DV.append(dve)

            def pool(eng):
                eng.wait_ge(s("slot_" + tag), 1)
                eng.wait_ge(s("zeroed"), 64)
                dst = (slots_d if tag == "b" else slots1_d).rearrange("k t d -> (k t) d")
                for b in range(NB):
                    eng.indirect_dma_start(out=dst, out_offset=bass.IndirectOffsetOnAxis(ap=slot_i[:, b:b + 1], axis=0),
                                           in_=xn[:, b, :], in_offset=None).then_inc(s("scattered_" + tag), 16)
            PO.append(pool)

        def collect(tag, src, sems):
            def pool(eng):
                sems(eng)
                for b in range(NB):
                    eng.indirect_dma_start(out=ctx_s[:, b, :], out_offset=None, in_=src.rearrange("k t d -> (k t) d"),
                                           in_offset=bass.IndirectOffsetOnAxis(ap=slot_i[:, b:b + 1], axis=0))\
                       .then_inc(s(f"back_{tag}{b // GB}"), 16)
            PO.append(pool)

        def w(eng, sem_, v):
            if not (isinstance(v, int) and v <= 0):
                eng.wait_ge(sem_, v)

        def tiles(eng, step):
            step(0, 0, 0)
            step(1, 0, 1)
            with eng.Fori(1, K // 2) as i:
                step(2 * i, i, 0)
                step(2 * i + 1, i, 1)
            assert K % 2
            step(K - 1, K // 2, 0)

        layernorm("b", lambda eng, g: eng.wait_ge(s("x1"), g + 1))

        def b_pe(eng):
            eng.wait_ge(s("v"), G)
            for g in range(G):
                eng.wait_ge(s("xn_b"), g + 1)
                if g >= 2:
                    eng.wait_ge(s("xbT"), g - 1)
                for j in range(GB):
                    i = eng.transpose(bank[g % 2][:, j * T:(j + 1) * T], xn[:, g * GB + j, :], ident[:, :])
                i.then_inc(s("xbTp"), 1)
                eng.wait_ge(s("xbT"), g + 1)
                for j in range(GB):
                    b = g * GB + j
                    i = eng.matmul(bank[6][:, b * NE:(b + 1) * NE], big[:, b, :], rw[:, :], start=True, stop=True)
            i.then_inc(s("logit"), 1)
        PE.append(b_pe)

        def b_act(eng):
            for g in range(G):
                eng.wait_ge(s("xbTp"), g + 1)
                eng.wait_ge(s("gtp"), G)
                eng.activation(big[:, g * GB:(g + 1) * GB, :], bank[g % 2].rearrange("p (b t) -> p b t", b=GB), ACT.Copy)\
                   .then_inc(s("xbT"), 1)
            eng.wait_ge(s("shifted"), 1)
            eng.activation(lw[:, 1, :, :], lw[:, 0, :, :], ACT.Exp).then_inc(s("lexp"), 1)
        AC.append(b_act)

        def b_dve(eng):
            c = chain(eng, "dve")
            eng.wait_ge(s("logit"), 1)
            c.link(eng.tensor_tensor(logit[:, :, :], bank[6][:, 0:NB * NE].rearrange("p (b e) -> p b e", e=NE), bc(rb[:, :], 1, NB), ALU.add))
            c.link(eng.reduce_max(r16[:, 1, :], logit[:, :, :], AX))
            eng.tensor_tensor(lw[:, 0, :, :], logit[:, :, :], bc(r16[:, 1, :], 2, NE), ALU.subtract).then_inc(s("shifted"), 1)
            eng.wait_ge(s("consts"), 1)
            c.link(eng.tensor_tensor(oh[:, :, :], logit[:, :, :], bc(r16[:, 1, :], 2, NE), ALU.is_equal))
            c.link(eng.scalar_tensor_tensor(lw[:, 2, :, :], oh[:, :, :], -float(NE), bc(iota_e[:, :], 1, NB), ALU.mult, ALU.add))
            c.link(eng.tensor_reduce(r16[:, 2, :], lw[:, 2, :, :], AX, ALU.min))
            c.link(eng.tensor_scalar(r16[:, 3, :], r16[:, 2, :], float(NE), None, ALU.add))
            c.link(eng.tensor_tensor(oh[:, :, :], bc(iota_e[:, :], 1, NB), bc(r16[:, 3, :], 2, NE), ALU.is_equal))
            eng.tensor_copy(ohb[:, 0:NB, :], oh[:, :, :]).then_inc(s("oh_b"), 1)
            eng.wait_ge(s("lexp"), 1)
            c.link(eng.reduce_sum(r16[:, 4, :], lw[:, 1, :, :], AX))
            c.link(eng.reciprocal(r16[:, 5, :], r16[:, 4, :]))
            eng.tensor_scalar(maxp[:, :], r16[:, 5, :], tg[:, 2:3], None, ALU.mult)
        DV.append(b_dve)
        route("b")

        def experts(tag, src, dst, w1, w2, b1, steps):
            gated = b1 is None
            CH = C0 if gated else C1
            n = {k: s(f"{k}_{tag}") for k in ("xTp", "xT", "h", "half", "act", "yp", "y")}
            xt_in = [s(f"xt_in_{tag}{i}") for i in range(2)]
            w1_in = [s(f"w1_in_{tag}{i}") for i in range(2)]
            w2_in = [s(f"w2_in_{tag}{i}") for i in range(2)]
            b1_in = [s(f"b1_in_{tag}{i}") for i in range(2)]
            b2_in = [s(f"b2_in_{tag}{i}") for i in range(2)]
            y_out = [s(f"y_out_{tag}{i}") for i in range(2)]

            def sp(eng):
                eng.wait_ge(s("te_" + tag), 1)
                eng.wait_ge(s("scattered_" + tag), 16 * NB)
                if not gated:
                    eng.wait_ge(s("b2pair_d"), 16)

                def load_x(k, slot):
                    w(eng, n["xTp"], k - 1)
                    eng.dma_start(xt[:, slot, :], src[ds(k, 1)].rearrange("a t d -> (a t) d")).then_inc(xt_in[slot], 16)
                load_x(0, 0)

                def step(k, turn, slot):
                    if not (isinstance(k, int) and k == K - 1):
                        load_x(k + 1, 1 - slot)
                    for j in range(steps):
                        e = eng.value_load(te_i[0:1, j, ds(k, 1)], min_val=0, max_val=NE - 1)
                        q = steps * k + j
                        ws = slot if steps == 1 else j
                        w(eng, n["h"], q - 1)
                        wide = 2 * F0 if gated else F1
                        eng.dma_start(w1r[:, ws, 0:wide], w1[ds(e, 1)].rearrange("a d f -> (a d) f")).then_inc(w1_in[ws], 16)
                        w(eng, n["yp"], q - 1)
                        if not gated:
                            eng.dma_start(b1r[:, ws, :], b1[ds(e, 1)].rearrange("a p c -> (a p) c")).then_inc(b1_in[ws], 16)
                        eng.dma_start(w2r[:, ws, :, :], w2[ds(e, 1)].rearrange("a (c p) d -> (a p) c d", p=128)).then_inc(w2_in[ws], 16)
                        if not gated and j == 0:
                            w(eng, n["y"], k - 1)
                            eng.dma_start(b2r[:, slot, :], b2pair_d[ds(e, 1), :].broadcast_to((128, D))).then_inc(b2_in[slot], 16)
                tiles(eng, step)
            SP.append(sp)

            def pe(eng):
                def turn_over(k, turn, slot):
                    w(eng, n["xT"], k)
                    eng.wait_ge(xt_in[slot], 16 * (turn + 1))
                    eng.transpose(bank[0][:, 0:T], xt[:, slot, :], ident[:, :]).then_inc(n["xTp"], 1)

                def up(k, turn, slot, j):
                    q = steps * k + j
                    ws = slot if steps == 1 else j
                    if j == 0:
                        eng.wait_ge(n["xT"], k + 1)
                    w(eng, n["act"], q - 1)
                    if not gated:
                        w(eng, n["half"], q - 1)
                    eng.wait_ge(w1_in[ws], 16 * (turn + 1) if gated else 16 * (k + 1))
                    P = (pairA, pairB)[ws]
                    for f in range(2 * CH if gated else CH):
                        g_, o = divmod(f, CH if gated else CH // 2)
                        i = eng.matmul(P[:, g_, o * T:(o + 1) * T], w1r[:, ws, f * 128:(f + 1) * 128], xtT[:, slot, :], start=True, stop=True)
                    i.then_inc(n["h"], 1)

                def down(k, turn, slot, j):
                    q = steps * k + j
                    ws = slot if steps == 1 else j
                    eng.wait_ge(n["act"], q + 1)
                    if not gated:
                        eng.wait_ge(n["half"], q + 1)
                    if j == 0:
                        w(eng, n["y"], k - 1)
                    eng.wait_ge(w2_in[ws], 16 * (turn + 1) if gated else 16 * (k + 1))
                    for c_ in range(CH):
                        i = eng.matmul(bank[1 + slot][:, 0:D], act[:, ws, c_, :], w2r[:, ws, c_, :],
                                       start=(j == 0 and c_ == 0), stop=(j == steps - 1 and c_ == CH - 1))
                    i.then_inc(n["yp"], 1)

                turn_over(0, 0, 0)

                def step(k, turn, slot):
                    up(k, turn, slot, 0)
                    if not (isinstance(k, int) and k == K - 1):
                        turn_over(k + 1, turn + slot, 1 - slot)
                    if not (isinstance(k, int) and k == 0):
                        down(k - 1, turn - 1 + slot, 1 - slot, steps - 1)
                    if steps == 2:
                        up(k, turn, slot, 1)
                        down(k, turn, slot, 0)
                tiles(eng, step)
                down(K - 1, K // 2, 0, steps - 1)
            PE.append(pe)

            def act_(eng):
                def out_y(k, turn, slot):
                    eng.wait_ge(n["yp"], steps * (k + 1))
                    w(eng, y_out[slot], 16 * turn)
                    if gated:
                        eng.activation(ysb[:, slot, :], bank[1 + slot][:, 0:D], ACT.Copy).then_inc(n["y"], 1)
                    eng.wait_ge(n["y"], k + 1)
                    eng.dma_start(dst[ds(k, 1)].rearrange("a t d -> (a t) d"), ysb[:, slot, :]).then_inc(y_out[slot], 16)

                def step(k, turn, slot):
                    for j in range(steps):
                        q = steps * k + j
                        ws = slot if steps == 1 else j
                        eng.wait_ge(n["h"], q + 1)
                        P = (pairA, pairB)[ws]
                        if gated:
                            w(eng, n["act"], q - 1)
                            eng.activation(sil[:, slot, :], P[:, 0, :], ACT.Silu).then_inc(n["half"], 1)
                        else:
                            w(eng, n["yp"], q - 1)
                            eng.wait_ge(b1_in[ws], 16 * (k + 1))
                            for c_ in range(CH // 2):
                                i = eng.activation(act[:, ws, c_, :], P[:, 0, c_ * T:(c_ + 1) * T], ACT.Relu, bias=b1r[:, ws, c_:c_ + 1])
                            i.then_inc(n["half"], 1)
                        if j == 0 and not (isinstance(k, int) and k == 0):
                            out_y(k - 1, turn - 1 + slot, 1 - slot)
                tiles(eng, step)
                out_y(K - 1, K // 2, 0)
            AC.append(act_)

            def dve(eng):
                def xT(k, turn, slot):
                    eng.wait_ge(n["xTp"], k + 1)
                    w(eng, n["h"], steps * (k - 1))
                    eng.tensor_copy(xtT[:, slot, :], bank[0][:, 0:T]).then_inc(n["xT"], 1)

                def y(k, turn, slot):
                    eng.wait_ge(n["yp"], steps * (k + 1))
                    eng.wait_ge(b2_in[slot], 16 * (turn + 1))
                    w(eng, y_out[slot], 16 * turn)
                    eng.tensor_tensor(ysb[:, slot, :], bank[1 + slot][:, 0:D], b2r[:, slot, :], ALU.add).then_inc(n["y"], 1)

                xT(0, 0, 0)

                def step(k, turn, slot):
                    for j in range(steps):
                        q = steps * k + j
                        ws = slot if steps == 1 else j
                        P = (pairA, pairB)[ws]
                        if gated:
                            if not (isinstance(k, int) and k == K - 1):
                                xT(k + 1, turn + slot, 1 - slot)
                            eng.wait_ge(n["half"], q + 1)
                            w(eng, n["yp"], q - 1)
                            eng.tensor_tensor(act[:, slot, :, :].rearrange("p c t -> p (c t)"), P[:, 1, :], sil[:, slot, :], ALU.mult)\
                               .then_inc(n["act"], 1)
                        else:
                            eng.wait_ge(n["h"], q + 1)
                            w(eng, n["yp"], q - 1)
                            eng.wait_ge(b1_in[ws], 16 * (k + 1))
                            for c_ in range(CH // 2, CH):
                                o = c_ - CH // 2
                                i = eng.tensor_scalar(act[:, ws, c_, :], P[:, 1, o * T:(o + 1) * T], b1r[:, ws, c_:c_ + 1], 0.0,
                                                      ALU.add, ALU.max)
                            i.then_inc(n["act"], 1)
                            if j == 0:
                                if not (isinstance(k, int) and k == K - 1):
                                    xT(k + 1, turn + slot, 1 - slot)
                                if not (isinstance(k, int) and k == 0):
                                    y(k - 1, turn - 1 + slot, 1 - slot)
                tiles(eng, step)
                if not gated:
                    y(K - 1, K // 2, 0)
            DV.append(dve)

            def back(eng):
                eng.wait_ge(y_out[0], 16 * (K // 2 + 1))
                eng.wait_ge(y_out[1], 16 * (K // 2))
            collect(tag, dst, back)

        experts("b", slots_d, ys_d, A["w1_0"], A["w2_0"], None, 1)

        def b_add(eng):
            for b in range(NB):
                if b % GB == 0:
                    eng.wait_ge(s(f"back_b{b // GB}"), 16 * GB)
                i = eng.scalar_tensor_tensor(x[:, b, :], ctx_s[:, b, :], maxp[:, b:b + 1], x[:, b, :], ALU.mult, ALU.add)
                if b % GB == GB - 1:
                    i.then_inc(s("x2"), 1)
        DV.append(b_add)

        if STOP == "B":
            DV.append(lambda eng: eng.wait_ge(s("x2"), G))
            SP.append(lambda eng: [eng.wait_ge(s("kstack_d"), 16 * G * PARTS)])
            done()
            emit()
            return

        layernorm("c", lambda eng, g: eng.wait_ge(s("x2"), g + 1))

        def q_pe(eng):
            for g in range(G):
                eng.wait_ge(s("xn_c"), g + 1)
                if g >= 2:
                    eng.wait_ge(s("xcT"), g - 1)
                for j in range(GB):
                    i = eng.transpose(bank[g % 2][:, j * T:(j + 1) * T], xn[:, g * GB + j, :], ident[:, :])
                i.then_inc(s("xcTp"), 1)
                eng.wait_ge(s("xcT"), g + 1)
                if g >= 2:
                    eng.wait_ge(s("qp"), g - 1)
                eng.matmul(bank[2 + g % 2], wq1[:, :], big[:, g * GB:(g + 1) * GB, :].rearrange("p b t -> p (b t)"), start=True, stop=True)\
                   .then_inc(s("qproj"), 1)
        PE.append(q_pe)

        QS = HD ** -0.5

        def q_act(eng):
            for g in range(G):
                eng.wait_ge(s("xcTp"), g + 1)
                eng.activation(big[:, g * GB:(g + 1) * GB, :].rearrange("p b t -> p (b t)"), bank[g % 2], ACT.Copy).then_inc(s("xcT"), 1)
                eng.wait_ge(s("qproj"), g + 1)
                eng.wait_ge(s("kstack_d"), 16 * PARTS * G)
                if g >= 1:
                    eng.wait_ge(s("qstack_d"), 16 * PARTS * g)
                eng.activation(p1[:, 0, :], bank[2 + g % 2], ACT.Copy, scale=QS).then_inc(s("q1"), 1)
                eng.wait_ge(s("qr1"), g + 1)
                eng.activation(p1[:, 1, :], res[:, 0, :], ACT.Copy).then_inc(s("q2"), 1)
                eng.wait_ge(s("qp"), g + 1)
                for j in range(PARTS):
                    eng.dma_start(qstack_d[j, :, :, g * GT:(g + 1) * GT].rearrange("i p t -> p i t"), p1[:, :, :])\
                       .then_inc(s("qstack_d"), 16)
        AC.append(q_act)

        def q_dve(eng):
            for g in range(G):
                eng.wait_ge(s("q1"), g + 1)
                eng.scalar_tensor_tensor(res[:, 0, :], bank[2 + g % 2], QS, p1[:, 0, :], ALU.mult, ALU.subtract).then_inc(s("qr1"), 1)
                eng.wait_ge(s("q2"), g + 1)
                eng.tensor_tensor(p1[:, 2, :], res[:, 0, :], p1[:, 1, :], ALU.subtract).then_inc(s("qp"), 1)
        DV.append(q_dve)

        BODY = 2 * GB
        LAG = 7

        class At:

            def __init__(self, turn, r, lo, hi):
                self.turn, self.r, self.lo, self.hi = turn, r, lo, hi

            def on(self, k):
                return self.lo - k >= 0 and self.hi - k < NU

            def unit(self, k):
                return BODY * self.turn + (self.r - k)

            def batch(self, k):
                return (BODY // 2) * self.turn + (self.r - k) // 2

            def slot(self, k):
                return (self.r - k) % 2

            def half_(self, k):
                return (self.r - k) % 2

            def bslot(self, k):
                return ((self.r - k) // 2) % 2

        def units(eng, step):
            for n in range(BODY):
                step(At(0, n, n, n))
            with eng.Fori(1, NU // BODY) as i:
                for r in range(BODY):
                    step(At(i, r, BODY + r, NU - BODY + r))
            for r in range(LAG):
                step(At(NU // BODY, r, NU + r, NU + r))

        def c_sp(eng):
            eng.wait_ge(s("kstack_d"), 16 * PARTS * G)

            def load(turn, slot):
                p = 2 * turn + slot
                if slot == 0:
                    eng.wait_ge(s("qstack_d"), 16 * PARTS * (turn + 1))
                w(eng, s("ST"), 4 * p - 4)
                for t_, d_ in ((ks, kstack_d), (qs, qstack_d)):
                    v = d_.rearrange("j i (d h) t -> (j i d) h t", h=H)
                    eng.dma_start(t_[:, slot, :, :], v[:, :, ds(p * 2 * T, 2 * T)]).then_inc(s(f"qk{slot}"), 16)
            load(0, 0)
            load(0, 1)
            with eng.Fori(1, G) as i:
                load(i, 0)
                load(i, 1)
        SP.append(c_sp)

        def c_pe(eng):
            def heads(r):
                slot, off, u = (r // 4) % 2, ((r // 2) % 2) * T, r % 2
                return [(h, qs[:, slot, u * HU + h, off:off + T], ks[:, slot, u * HU + h, off:off + T]) for h in range(HU)]

            def step(at):
                if at.on(1):
                    eng.wait_ge(s("mparts"), at.unit(0))
                    w(eng, s("mrow"), at.unit(1))
                    eng.transpose(mTp, mparts[:, at.slot(1), :, :].rearrange("p i h -> p (i h)"), identb[:, :]).then_inc(s("mT"), 1)
                if at.on(0):
                    if at.r % 4 == 0:
                        eng.wait_ge(s(f"qk{at.r // 4}"), 32 * (at.turn + 1))
                    w(eng, s("mx"), at.unit(0))
                    for h, q_, k_ in heads(at.r):
                        i = eng.matmul(pairA[:, h // 4, (h % 4) * T:(h % 4 + 1) * T], q_, k_, start=True, stop=True)
                    i.then_inc(s("S"), 1)
                if at.on(1):
                    eng.wait_ge(s("mrow"), at.unit(0))
                    w(eng, s("P"), at.unit(1))
                    for h, q_, k_ in heads((at.r - 1) % BODY):
                        o = pairB[:, h // 4, (h % 4) * T:(h % 4 + 1) * T]
                        eng.matmul(o, k_, q_, start=True, stop=False)
                        i = eng.matmul(o, pick[:, h, :], mrow[:, at.slot(1), :], start=False, stop=True)
                    i.then_inc(s("ST"), 1)
                if at.on(2):
                    u = at.half_(2)
                    eng.wait_ge(s("P"), at.unit(1))
                    if u == 0:
                        w(eng, s("osb"), at.batch(2))
                        eng.wait_ge(s("vp"), at.batch(0))
                    for h in range(HU):
                        hh = u * HU + h
                        i = eng.matmul(bank[1][32 * (hh % 4):32 * (hh % 4) + 32, (hh // 4) * T:(hh // 4 + 1) * T],
                                       vpad[:, at.bslot(2), hh, :], prob[:, at.slot(2), h, :], start=True, stop=True,
                                       tile_position=(0, 32 * (hh % 4)))
                    i.then_inc(s("O"), 1)
                if at.r % 2 == 0 and at.on(4):
                    eng.wait_ge(s("osb"), at.batch(2))
                    w(eng, s("an"), at.batch(4))
                    for j in range(4):
                        i = eng.transpose(bank[2][:, j * 128:(j + 1) * 128], osb[:, j * 128:(j + 1) * 128], ident[:, :])
                    i.then_inc(s("oT"), 1)
                if at.r % 2 == 1 and at.on(5):
                    eng.wait_ge(s("an"), at.batch(3))
                    w(eng, s("x3"), at.batch(5))
                    eng.transpose(bank[3][:, 0:T], an[:, :], ident[:, :]).then_inc(s("anTp"), 1)
                if at.r % 2 == 0 and at.on(6):
                    eng.wait_ge(s("anT"), at.batch(4))
                    eng.matmul(bank[3][:, T:T + D], anT[:, :], wo1[:, :], start=True, stop=True).then_inc(s("proj"), 1)
            units(eng, step)
        PE.append(c_pe)

        def c_act(eng):
            def step(at):
                if at.on(1):
                    eng.wait_ge(s("mT"), at.unit(0))
                    w(eng, s("ST"), at.unit(2))
                    eng.activation(mrow[:, at.slot(1), :], mTp, ACT.Copy).then_inc(s("mrow"), 1)
                if at.r % 2 == 0 and at.on(4):
                    eng.wait_ge(s("O"), at.unit(2))
                    w(eng, s("oT"), at.batch(4))
                    eng.activation(osb[:, :], bank[1], ACT.Copy).then_inc(s("osb"), 1)
                if at.on(1):
                    eng.wait_ge(s("ST"), at.unit(0))
                    w(eng, s("O"), at.unit(2))
                    eng.activation(prob[:, at.slot(1), :, :].rearrange("p h t -> p (h t)"), pairB[:, :, :].rearrange("p a t -> p (a t)"), ACT.Exp)\
                       .then_inc(s("P"), 1)
                if at.r % 2 == 1 and at.on(5):
                    eng.wait_ge(s("anTp"), at.batch(3))
                    w(eng, s("proj"), at.batch(5))
                    eng.activation(anT[:, :], bank[3][:, 0:T], ACT.Copy).then_inc(s("anT"), 1)
            units(eng, step)
        AC.append(c_act)

        def c_dve(eng):
            c = chain(eng, "dve")

            def step(at):
                if at.on(0):
                    eng.wait_ge(s("S"), at.unit(0) + 1)
                    m = negm[:, 0, :]
                    mp = mparts[:, at.slot(0), :, :]
                    w(eng, s("mT"), at.unit(1))
                    i = eng.reduce_max(m, pairA[:, :, :].rearrange("p a (h t) -> p (a h) t", t=T), AX)
                    i.then_inc(s("mx"), 1)
                    eng.wait_ge(s("mx"), at.unit(0) + 1)
                    c.link(eng.tensor_scalar(mp[:, 0, :], m, -1.0, None, ALU.mult))
                    c.link(eng.scalar_tensor_tensor(negm[:, 1, :], m, -1.0, mp[:, 0, :], ALU.mult, ALU.subtract))
                    c.link(eng.tensor_copy(mp[:, 1, :], negm[:, 1, :]))
                    eng.tensor_tensor(mp[:, 2, :], negm[:, 1, :], mp[:, 1, :], ALU.subtract).then_inc(s("mparts"), 1)
                if at.r % 2 == 0 and at.on(4):
                    eng.wait_ge(s("oT"), at.batch(2))
                    w(eng, s("anTp"), at.batch(4))
                    v = bank[2].rearrange("p (h c) -> p h c", c=VW)
                    i = eng.reciprocal(rl[:, :], v[:, :, HD])
                    i.then_inc(s("rl"), 1)
                    eng.wait_ge(s("rl"), at.batch(2))
                    eng.tensor_tensor(an[:, :].rearrange("p (h c) -> p h c", c=HD), v[:, :, 0:HD], bc(rl[:, :], 2, HD), ALU.mult)\
                       .then_inc(s("an"), 1)
                if at.r % 2 == 0 and at.on(6):
                    eng.wait_ge(s("proj"), at.batch(4))
                    xb = x[:, ds(at.batch(6), 1), :].rearrange("p a d -> p (a d)")
                    eng.tensor_tensor(xb, bank[3][:, T:T + D], xb, ALU.add).then_inc(s("x3"), 1)

            for n in range(BODY):
                step(At(0, n, n, n))
            with eng.Fori(1, G) as i:
                c.enter(i - 1, 3 * BODY)
                for r in range(BODY):
                    step(At(i, r, BODY + r, NU - BODY + r))
            c.leave(G - 1)
            for r in range(LAG):
                step(At(NU // BODY, r, NU + r, NU + r))
        DV.append(c_dve)

        def c_pool(eng):
            eng.wait_ge(s("v"), G)

            def fill(b, slot):
                w(eng, s("O"), 2 * b - 2)
                eng.tensor_copy(vpad[:, slot, :, 0:HD], vals[:, ds(b, 1), :].rearrange("p a (h d) -> p (a h) d", h=H))\
                   .then_inc(s("vp"), 1)
            fill(0, 0)
            fill(1, 1)
            with eng.Fori(1, NB // 2) as i:
                fill(2 * i, 0)
                fill(2 * i + 1, 1)
        PO.append(c_pool)

        if STOP == "C":
            DV.append(lambda eng: eng.wait_ge(s("x3"), NB))
            done()
            emit()
            return

        layernorm("d", lambda eng, g: eng.wait_ge(s("x3"), GB * g + GB))

        def d_dve(eng):
            c = chain(eng, "dve")
            a_, b_, c_, d_, e_ = (r16[:, k, :] for k in range(5))
            c.link(eng.tensor_tensor(a_, xn[:, :, 0], xn[:, :, 1], ALU.add))
            c.link(eng.tensor_scalar(b_, a_, -1.0, None, ALU.mult))
            c.link(eng.tensor_tensor(b_, a_, b_, ALU.max))
            nearest(eng, c, c_, b_)
            c.link(eng.tensor_tensor(d_, c_, b_, ALU.is_gt))
            c.link(eng.tensor_tensor(c_, c_, d_, ALU.subtract))
            c.link(eng.tensor_scalar(d_, a_, 0.0, 2.0, ALU.is_ge, ALU.mult))
            c.link(eng.scalar_tensor_tensor(e_, d_, -1.0, c_, ALU.add, ALU.mult))
            c.link(eng.tensor_scalar(b_, e_, 64.0, None, ALU.add))
            c.link(eng.tensor_scalar(a_, b_, 1.0 / NE, None, ALU.mult))
            nearest(eng, c, c_, a_)
            c.link(eng.tensor_tensor(d_, c_, a_, ALU.is_gt))
            c.link(eng.tensor_tensor(c_, c_, d_, ALU.subtract))
            c.link(eng.scalar_tensor_tensor(e_, c_, -float(NE), b_, ALU.mult, ALU.add))
            c.link(eng.tensor_tensor(oh[:, :, :], bc(iota_e[:, :], 1, NB), bc(e_, 2, NE), ALU.is_equal))
            eng.tensor_copy(ohb[:, 0:NB, :], oh[:, :, :]).then_inc(s("oh_d"), 1)
            eng.tensor_scalar(maxp[:, 0:1], tg[:, 3:4], 0.5, None, ALU.mult).then_inc(s("half_gate"), 1)
        DV.append(d_dve)
        route("d")
        experts("d", slots1_d, ys1_d, A["w1_1"], A["w2_1"], A["b1"], 2)

        def d_add(eng):
            eng.wait_ge(s("half_gate"), 1)
            for b in range(NB):
                if b % GB == 0:
                    eng.wait_ge(s(f"back_d{b // GB}"), 16 * GB)
                i = eng.scalar_tensor_tensor(x[:, b, :], ctx_s[:, b, :], maxp[:, 0:1], x[:, b, :], ALU.mult, ALU.add)
                if b % GB == GB - 1:
                    i.then_inc(s("x4"), 1)
        DV.append(d_add)

        def d_out(eng):
            o = out.rearrange("b t d -> t b d")
            for g in range(G):
                eng.wait_ge(s("x4"), g + 1)
                eng.dma_start(o[:, g * GB:(g + 1) * GB, :], x[:, g * GB:(g + 1) * GB, :]).then_inc(s("out"), 16)
            eng.wait_ge(s("out"), 16 * G)
        SP.append(d_out)
        emit()




_OUT = (16, 128, 128)


def kernel(x, ctx_1024, g_xattn, g_ffn, L0_xattn_Wq, L0_xattn_bq, L0_xattn_Wk, L0_xattn_bk, L0_xattn_Wv, L0_xattn_bv,
           L0_xattn_Wo, L0_xattn_bo, L0_ffn_router_w, L0_ffn_router_b, L0_ffn_w1, L0_ffn_w2, L1_xattn_w_q, L1_xattn_w_k,
           L1_xattn_w_v, L1_xattn_w_o, L1_ffn_W1, L1_ffn_b1, L1_ffn_W2, L1_ffn_b2):
    import concourse.bacc as bacc
    from concourse.bass_utils import run_bass_kernel_spmd

    def rev(w):
        return w.reshape(*w.shape[:-1], 16, 8)[..., ::-1].reshape(w.shape)

    def dh(w):
        return w.reshape(128, 16, 8).transpose(0, 2, 1).reshape(128, 128)

    a = {k: np.asarray(v) for k, v in locals().items() if not callable(v) and hasattr(v, "shape")}
    arrays = {
        "x": a["x"], "ctx": a["ctx_1024"][:, ::-1, :],
        "gates": np.concatenate([a["g_xattn"], a["g_ffn"]]).reshape(1, 4),
        "wq0": rev(a["L0_xattn_Wq"].T), "wk0": rev(a["L0_xattn_Wk"].T), "wv0": a["L0_xattn_Wv"], "wo0": a["L0_xattn_Wo"].T,
        "bq": rev(a["L0_xattn_bq"]).reshape(1, 128), "bk": rev(a["L0_xattn_bk"]).reshape(1, 128),
        "bv": a["L0_xattn_bv"].reshape(128, 1), "bo": a["L0_xattn_bo"].reshape(1, 128),
        "rw": a["L0_ffn_router_w"], "rb": a["L0_ffn_router_b"].reshape(1, 8),
        "w1_0": a["L0_ffn_w1"], "w2_0": a["L0_ffn_w2"],
        "wq1": dh(a["L1_xattn_w_q"].T), "wk1": dh(a["L1_xattn_w_k"].T), "wv1": a["L1_xattn_w_v"].T, "wo1": a["L1_xattn_w_o"].T,
        "w1_1": a["L1_ffn_W1"], "b1": a["L1_ffn_b1"].reshape(8, 4, 128).transpose(0, 2, 1), "w2_1": a["L1_ffn_W2"], "b2": a["L1_ffn_b2"],
    }
    arrays = {k: np.ascontiguousarray(v) for k, v in arrays.items()}
    nc = bacc.Bacc("TRN2", target_bir_lowering=False, num_devices=1)
    aps = {k: nc.dram_tensor("in_" + k, v.shape, mybir.dt.from_np(v.dtype), kind="ExternalInput").ap() for k, v in arrays.items()}
    out = nc.dram_tensor("out_x", _OUT, mybir.dt.float32, kind="ExternalOutput").ap()
    build(nc, aps, out)
    r = run_bass_kernel_spmd(nc, [{"in_" + k: v for k, v in arrays.items()}], core_ids=[0])
    return r.results[0]["out_x"]
```

```python
import numpy as np
import concourse.bass as bass
from concourse import mybir
from contextlib import ExitStack

STOP = "end"


class Chain:

    def __init__(self, eng, sem):
        self.eng, self.sem, self.base, self.k, self.inside = eng, sem, 0, 0, None

    def link(self, ins):
        ins.then_inc(self.sem, 1)
        self.k += 1
        self.eng.wait_ge(self.sem, self.base + self.k)

    def enter(self, i, per):
        self.inside = (self.base + self.k, per)
        self.base, self.k = self.base + self.k + i * per, 0

    def leave(self, turns):
        start, per = self.inside
        assert self.k == per, (self.k, per)
        self.base, self.k, self.inside = start + per * turns, 0, None


class Lin:

    def __init__(self, j, a, b):
        self.j, self.a, self.b = j, a if j is not None else 0, b

    def __add__(self, n):
        return Lin(self.j, self.a, self.b + n)

    def __sub__(self, n):
        return self + -n

    def __mul__(self, n):
        return Lin(self.j, self.a * n, self.b * n)

    def value(self):
        return self.b if self.j is None else self.j * self.a + self.b


def wait(eng, sem, count):
    if isinstance(count, Lin):
        if count.b <= 0:
            assert count.j is None
            return
        count = count.value()
    elif count <= 0:
        return
    eng.wait_ge(sem, count)


FFN = (512, 512)


def build(nc, A, out):
    f32, bf16, i32 = mybir.dt.float32, mybir.dt.bfloat16, mybir.dt.int32
    ALU, ACT, AX = mybir.AluOpType, mybir.ActivationFunctionType, mybir.AxisListType.X
    ds = bass.ds

    NB, T, D = A["x"].shape
    H, HD = 16, 8
    NE = A["rw"].shape[1]
    F0, F1 = FFN
    C0, C1 = F0 // T, F1 // T
    W0, W1 = 3 * F0, 2 * F1 + C1
    G, GB = 4, NB // 4
    GT = GB * T
    NTOK = NB * T
    K = NTOK // T + NE - 1
    KP = K + 1
    R = 4
    EPS = 1e-5
    ROUND = 1.5 * 2.0 ** 23
    PARTS = 3
    SK = PARTS * PARTS * HD
    HU = H // 2
    NU = 2 * NB
    VW = 32

    ctx = ExitStack()

    def sb(name, shape, dt=f32):
        return ctx.enter_context(nc.sbuf_tensor(name, shape, dt))

    def sem(name):
        return ctx.enter_context(nc.semaphore(name))

    def bc(ap, at, n):
        shape = list(ap.shape)
        return ap.unsqueeze(at).broadcast_to(shape[:at] + [n] + shape[at:])

    def scratch(name, shape, dt=f32):
        return nc.dram_tensor(name, shape, dt, kind="Internal").ap()

    with ctx:
        band_d = scratch("band_d", (NB, 2 * T))
        kstack_d = scratch("kstack_d", (PARTS, PARTS, HD * H, NTOK), bf16)
        qstack_d = scratch("qstack_d", (PARTS, PARTS, HD * H, NTOK), bf16)
        rows_d = {k: scratch(f"rows_{k}_d", (NTOK, D)) for k in "bd"}
        back_d = {k: scratch(f"back_{k}_d", (NTOK + K * T, D)) for k in "bd"}
        b2pair_d = scratch("b2pair_d", (NE, D))

        bank = [ctx.enter_context(nc.psum_tensor(f"bank{i}", [128, 512], f32)) for i in range(4)]
        pairA = ctx.enter_context(nc.psum_tensor("pairA", [128, 2, 512], f32))
        pairB = ctx.enter_context(nc.psum_tensor("pairB", [128, 2, 512], f32))
        bank += [pairA[:, 0, :], pairA[:, 1, :], pairB[:, 0, :], pairB[:, 1, :]]
        for i in range(4):
            bank[i] = bank[i][:, :]
        mTp = bank[0].bitcast(bf16)[0:PARTS * HU, 0:T]

        ident = sb("ident", [128, 128])
        before = sb("before", [128, 128], bf16)
        onesb = sb("onesb", [128, 128], bf16)
        onesf = sb("onesf", [128, 128])
        onehot_b = sb("onehot_b", [128, NB, NB])
        pick = sb("pick", [PARTS * HU, HU, T], bf16)
        iota_e = sb("iota_e", [128, NE])
        iota_tile = sb("iota_tile", [1, KP])
        iota_p = sb("iota_p", [128, T])
        part = sb("part", [128, 1])
        spare = sb("spare", [128, KP])
        gates = sb("gates", [128, 4])
        tg = sb("tg", [128, 4])
        wq0, wk0, wv0, wo0 = (sb(n, [128, 128]) for n in ("wq0", "wk0", "wv0", "wo0"))
        wq1, wk1, wv1, wo1 = (sb(n, [128, 128]) for n in ("wq1", "wk1", "wv1", "wo1"))
        bqk = sb("bqk", [1, 2, 128])
        bo_row = sb("bo_row", [1, 128])
        bv_col = sb("bv_col", [128, 1])
        rw = sb("rw", [128, NE])
        rb = sb("rb", [128, NE])
        len_row = sb("len_row", [1, 128])
        b2a = sb("b2a", [NE, D])
        b2b = sb("b2b", [NE, D])
        x = sb("x", [128, NB, D])
        xn = sb("xn", [128, NB, D])
        ctx_s = sb("ctx_s", [128, NB, D])
        big = sb("big", [128, NB, 128])
        ctxT = sb("ctxT", [128, NTOK])
        vals = sb("vals", [128, NB, D])
        vpad = sb("vpad", [128, 2, H, VW])
        qs = sb("qs", [SK, 2, H, 2 * T], bf16)
        ks = sb("ks", [SK, 2, H, 2 * T], bf16)
        prob = sb("prob", [128, 2, HU, T])
        negm = sb("negm", [128, 2, HU])
        mparts = sb("mparts", [128, 2, PARTS, HU], bf16)
        mrow = sb("mrow", [PARTS * HU, 2, T], bf16)
        osb = sb("osb", [128, 512])
        rl = sb("rl", [128, H])
        an = sb("an", [128, D])
        anT = sb("anT", [128, T])
        identb = sb("identb", [128, 128], bf16)
        st = sb("st", [128, NB, 6])
        lnv = sb("lnv", [128, 8, NB])
        lni = sb("lni", [128, NB], i32)
        sums = sb("sums", [NB, 2, 128])
        sumsT = sb("sumsT", [128, 2, NB])
        ks_sb = sb("ks_sb", [NB, 128])
        prod = sb("prod", [NB, 128])
        sm = sb("sm", [NB, 5, HD])
        band = sb("band", [NB, 2 * T])
        wvo = sb("wvo", [128, 128])
        bvo = sb("bvo", [128, 128])
        gt = sb("gt", [128, 2, 512])
        p1 = sb("p1", [128, PARTS, GT], bf16)
        res = sb("res", [128, 2, GT])
        logit = sb("logit", [128, NB, NE])
        lw = sb("lw", [128, 3, NB, NE])
        oh = sb("oh", [128, NB, NE])
        ohb = sb("ohb", [128, NB + 1, NE], bf16)
        r16 = sb("r16", [128, 8, NB])
        cnt = sb("cnt", [128, 3, NE])
        pre = sb("pre", [128, 4, 4 + NE])
        slot_i = sb("slot_i", [128, NB], i32)
        te_f = sb("te_f", [1, KP, NE])
        te_r = sb("te_r", [1, 3, KP])
        te_i = sb("te_i", [1, 2, KP], i32)
        maxp = sb("maxp", [128, NB])
        ohp = sb("ohp", [128, NB, T], bf16)
        ohk = sb("ohk", [128, NB, 3, KP], bf16)
        inv = sb("inv", [128, 4, KP])
        inv_i = sb("inv_i", [128, 2, KP], i32)
        wring = sb("wring", [128, R, W0])
        b2r = sb("b2r", [128, R, D])
        xt = sb("xt", [128, R, D])
        xtT = sb("xtT", [128, 2, T])
        sil = sb("sil", [128, 2, F0])
        act = sb("act", [128, 2, C0, T])
        ysb = sb("ysb", [128, R, D])

        S = {}

        def s(name):
            if name not in S:
                S[name] = sem("s_" + name)
            return S[name]

        PE, DV, AC, SP, PO = [], [], [], [], []
        ch = {}

        def chain(eng, name):
            if name not in ch:
                ch[name] = Chain(eng, s("chain_" + name))
            return ch[name]

        def layernorm(tag, ready):
            def dve(eng):
                c = chain(eng, "dve")
                with eng.Fori(0, G) as g:
                    c.enter(g, 1)
                    ready(eng, g)
                    for j in range(GB):
                        i = eng.bn_stats(st[:, ds(g * GB + j, 1), :].rearrange("p a d -> p (a d)"),
                                         x[:, ds(g * GB + j, 1), :].rearrange("p a d -> p (a d)"))
                    c.link(i)
                c.leave(G)
                me, mo, ve, vo = (st[:, :, k] for k in (1, 4, 2, 5))
                diff, total, var, y, t, u, mean = (lnv[:, k, :] for k in range(7))
                eng.tensor_tensor(diff, me, mo, ALU.subtract)
                eng.tensor_tensor(total, me, mo, ALU.add)
                c.link(eng.tensor_tensor(var, ve, vo, ALU.add))
                eng.tensor_scalar(mean, total, 0.5, None, ALU.mult)
                c.link(eng.tensor_tensor(t, diff, diff, ALU.mult))
                c.link(eng.scalar_tensor_tensor(u, t, D / 4.0, var, ALU.mult, ALU.add))
                c.link(eng.tensor_scalar(var, u, 1.0 / D, EPS, ALU.mult, ALU.add))
                c.link(eng.tensor_scalar(lni[:, :], var.bitcast(i32), 1, None, ALU.logical_shift_right))
                c.link(eng.tensor_scalar(y.bitcast(i32), lni[:, :], -1.0, float(0x5F3759DF), ALU.mult, ALU.add))
                for _ in range(4):
                    c.link(eng.tensor_tensor(t, y, y, ALU.mult))
                    c.link(eng.scalar_tensor_tensor(u, t, -0.5, var, ALU.mult, ALU.mult))
                    c.link(eng.scalar_tensor_tensor(y, u, 1.5, y, ALU.add, ALU.mult))
                with eng.Fori(0, G) as g:
                    for j in range(GB):
                        i = eng.tensor_scalar(xn[:, ds(g * GB + j, 1), :].rearrange("p a d -> p (a d)"),
                                              x[:, ds(g * GB + j, 1), :].rearrange("p a d -> p (a d)"),
                                              lnv[:, 6, ds(g * GB + j, 1)], lnv[:, 3, ds(g * GB + j, 1)],
                                              ALU.subtract, ALU.mult)
                    i.then_inc(s("xn_" + tag), 1)
                eng.wait_ge(s("xn_" + tag), G)
            DV.append(dve)

        def loads_sp(eng):
            for g in range(G):
                eng.dma_start(x[:, g * GB:(g + 1) * GB, :], A["x"][g * GB:(g + 1) * GB].rearrange("b t d -> t b d")).then_inc(s("x"), 16)
            for n, t in (("wv0", wv0), ("wo0", wo0), ("wq0", wq0), ("wk0", wk0)):
                eng.dma_start(t[:, :], A[n]).then_inc(s("w0"), 16)
            eng.dma_start(bqk[:, 0, :], A["bq"]).then_inc(s("w0"), 16)
            eng.dma_start(bqk[:, 1, :], A["bk"]).then_inc(s("w0"), 16)
            eng.dma_start(bo_row[:, :], A["bo"]).then_inc(s("w0"), 16)
            eng.dma_start(bv_col[:, :], A["bv"]).then_inc(s("w0"), 16)
            for n, t in (("wk1", wk1), ("wv1", wv1), ("wq1", wq1), ("wo1", wo1)):
                eng.dma_start(t[:, :], A[n]).then_inc(s("w1"), 16)
            eng.dma_start(rw[:, :], A["rw"]).then_inc(s("w1"), 16)
            eng.dma_start(rb[:, :], A["rb"].broadcast_to((128, NE))).then_inc(s("w1"), 16)
            eng.dma_start(b2a[:, :], A["b2"]).then_inc(s("w1"), 16)
            eng.dma_start(b2b[0:NE - 1, :], A["b2"][1:NE, :]).then_inc(s("w1"), 16)
            eng.dma_start(b2b[NE - 1:NE, :], A["b2"][0:1, :]).then_inc(s("w1"), 16)
        SP.append(loads_sp)

        def loads_act(eng):
            eng.dma_start(gates[:, :], A["gates"].broadcast_to((128, 4))).then_inc(s("gates"), 16)
            for g in range(G):
                eng.dma_start(ctx_s[:, g * GB:(g + 1) * GB, :], A["ctx"][g * GB:(g + 1) * GB].rearrange("b t d -> t b d")).then_inc(s("ctx"), 16)
            eng.wait_ge(s("gates"), 16)
            eng.activation(tg[:, :], gates[:, :], ACT.Tanh).then_inc(s("tg"), 1)
        AC.append(loads_act)

        def consts(eng):
            eng.memset(ident[:, :], 0.0).then_inc(s("c0"), 1)
            eng.wait_ge(s("c0"), 1)
            eng.affine_select(out=ident[:, :], in_=ident[:, :], compare_op=ALU.not_equal, fill=1.0,
                              base=0, pattern=[[-1, 128]], channel_multiplier=1).then_inc(s("ident"), 1)
            eng.memset(onehot_b[:, :, :], 0.0).then_inc(s("c0"), 1)
            eng.memset(onesf[:, :], 1.0)
            eng.memset(len_row[:, :], float(T))
            eng.wait_ge(s("c0"), 2)
            eng.affine_select(out=onehot_b[:, :, :], in_=onehot_b[:, :, :], compare_op=ALU.not_equal, fill=1.0,
                              base=0, pattern=[[1, NB], [-1, NB]], channel_multiplier=0).then_inc(s("onehot"), 1)
            eng.memset(onesb[:, :], 1.0)
            eng.memset(before[:, :], 1.0)
            eng.memset(pick[:, :, :], 0.0)
            eng.iota(iota_e[:, :], pattern=[[1, NE]], base=0, channel_multiplier=0, allow_small_or_imprecise_dtypes=True)
            eng.iota(iota_tile[:, :], pattern=[[T, KP]], base=0, channel_multiplier=0, allow_small_or_imprecise_dtypes=True)
            eng.iota(iota_p[:, :], pattern=[[1, T]], base=0, channel_multiplier=0, allow_small_or_imprecise_dtypes=True)
            eng.iota(part[:, :], pattern=[[0, 1]], base=0, channel_multiplier=1, allow_small_or_imprecise_dtypes=True)
            eng.iota(spare[:, :], pattern=[[T, KP]], base=NTOK, channel_multiplier=1, allow_small_or_imprecise_dtypes=True)
            eng.memset(ohb[:, :, :], 0.0)
            eng.memset(pre[:, :, :], 0.0)
            eng.memset(band[:, :], 0.0).then_inc(s("c0"), 1)
            eng.wait_ge(s("c0"), 3)
            eng.affine_select(out=before[:, :], in_=before[:, :], compare_op=ALU.is_gt, fill=0.0,
                              base=0, pattern=[[1, 128]], channel_multiplier=-1)
            for i in range(PARTS):
                eng.affine_select(out=pick[:, :, :], in_=pick[:, :, :], compare_op=ALU.not_equal, fill=1.0,
                                  base=-i * HU, pattern=[[-1, HU], [0, T]], channel_multiplier=1).then_inc(s("c0"), 1)
                eng.wait_ge(s("c0"), 4 + i)
            eng.tensor_copy(identb[:, :], ident[:, :])
            eng.memset(vpad[:, :, :, :], 0.0).then_inc(s("c0"), 1)
            eng.wait_ge(s("c0"), 4 + PARTS)
            eng.memset(vpad[:, :, :, HD:HD + 1], 1.0).then_inc(s("consts"), 1)
            eng.wait_ge(s("w1"), 16 * 9)
            eng.tensor_tensor(b2a[:, :], b2a[:, :], b2b[:, :], ALU.add).then_inc(s("b2pair"), 1)
            eng.wait_ge(s("b2pair"), 1)
            eng.dma_start(b2pair_d, b2a[:, :]).then_inc(s("b2pair_d"), 16)
            eng.wait_ge(s("b2pair_d"), 16)
        PO.append(consts)

        layernorm("a", lambda eng, g: (eng.wait_ge(s("x"), 16 * G), eng.wait_ge(s("ident"), 1)))

        def a_pe(eng):
            eng.wait_ge(s("ident"), 1)
            eng.wait_ge(s("onehot"), 1)
            eng.wait_ge(s("ctx"), 16 * G)
            for g in range(G):
                if g >= 2:
                    eng.wait_ge(s("ctxT"), g - 1)
                for j in range(GB):
                    i = eng.transpose(bank[g % 2][:, j * T:(j + 1) * T], ctx_s[:, g * GB + j, :], ident[:, :])
                i.then_inc(s("ctxTp"), 1)
            for b in range(NB):
                i = eng.matmul(bank[2][0:NB, 0:D], onehot_b[:, b, :], ctx_s[:, b, :], start=(b == 0), stop=(b == NB - 1))
            i.then_inc(s("csum"), 1)
            eng.wait_ge(s("w0"), 16 * 8)
            eng.matmul(bank[3][:, 0:128], wv0[:, :], wo0[:, :], start=True, stop=True)
            eng.matmul(bank[3][:, 128:256], bv_col[:, 0:1].broadcast_to((128, 128)), wo0[:, :], start=True, stop=False)
            eng.matmul(bank[3][:, 128:256], onesf[0:1, :], bo_row[:, :], start=False, stop=True).then_inc(s("wvop"), 1)
            for b in range(NB):
                if b % GB == 0:
                    eng.wait_ge(s("xn_a"), b // GB + 1)
                i = eng.matmul(bank[4][0:NB, 0:D], onehot_b[:, b, :], xn[:, b, :], start=(b == 0), stop=(b == NB - 1))
            i.then_inc(s("xsum"), 1)
            eng.wait_ge(s("sums"), 2)
            for j in range(2):
                i = eng.transpose(bank[5][:, j * NB:(j + 1) * NB], sums[:, j, :], ident[0:NB, 0:NB])
            i.then_inc(s("sumsTp"), 1)
            eng.wait_ge(s("sumsT"), 1)
            for j, w in enumerate((wq0, wk0)):
                eng.matmul(bank[6 + j][0:NB, 0:128], sumsT[:, j, :], w[:, :], start=True, stop=False)
                i = eng.matmul(bank[6 + j][0:NB, 0:128], len_row[0:1, 0:NB], bqk[0:1, j, :], start=False, stop=True)
            i.then_inc(s("qksum"), 1)
        PE.append(a_pe)

        def a_act(eng):
            for g in range(G):
                eng.wait_ge(s("ctxTp"), g + 1)
                eng.activation(ctxT[:, g * GT:(g + 1) * GT], bank[g % 2], ACT.Copy).then_inc(s("ctxT"), 1)
            eng.wait_ge(s("csum"), 1)
            eng.activation(sums[:, 1, :], bank[2][0:NB, 0:D], ACT.Copy).then_inc(s("sums"), 1)
            eng.wait_ge(s("wvop"), 1)
            eng.wait_ge(s("tg"), 1)
            eng.wait_ge(s("w1"), 16 * 9)
            eng.activation(wvo[:, :], bank[3][:, 0:128], ACT.Copy, scale=tg[:, 0:1])
            eng.activation(wo1[:, :], wo1[:, :], ACT.Copy, scale=tg[:, 1:2])
            eng.activation(bvo[:, :], bank[3][:, 128:256], ACT.Copy, scale=tg[:, 0:1]).then_inc(s("wvo"), 1)
            eng.wait_ge(s("xsum"), 1)
            eng.activation(sums[:, 0, :], bank[4][0:NB, 0:D], ACT.Copy).then_inc(s("sums"), 1)
            eng.wait_ge(s("sumsTp"), 1)
            eng.activation(sumsT[:, :, :], bank[5][:, 0:2 * NB].rearrange("p (j b) -> p j b", j=2), ACT.Copy).then_inc(s("sumsT"), 1)
            eng.wait_ge(s("corr"), 1)
            eng.activation(sm[:, 3, :], sm[:, 0, :], ACT.Exp, bias=sm[:, 2, 0:1], scale=1.0 / (H * T)).then_inc(s("corre"), 1)
        AC.append(a_act)

        def a_dve(eng):
            c = chain(eng, "dve")
            eng.wait_ge(s("qksum"), 1)
            c.link(eng.tensor_copy(ks_sb[:, :], bank[7][0:NB, 0:128]))
            c.link(eng.tensor_tensor(prod[:, :], bank[6][0:NB, 0:128], ks_sb[:, :], ALU.mult))
            c.link(eng.reduce_sum(sm[:, 0, :], prod[:, :].rearrange("p (h c) -> p c h", c=HD), AX))
            c.link(eng.reduce_max(sm[:, 1, 0:1], sm[:, 0, :], AX))
            eng.tensor_scalar(sm[:, 2, 0:1], sm[:, 1, 0:1], -1.0 / (H * T), None, ALU.mult).then_inc(s("corr"), 1)
            eng.wait_ge(s("corre"), 1)
            c.link(eng.reduce_sum(sm[:, 4, 0:1], sm[:, 3, :], AX))
            c.link(eng.reciprocal(sm[:, 4, 1:2], sm[:, 4, 0:1]))
            eng.wait_ge(s("consts"), 1)
            eng.tensor_scalar(band[:, T - HD:T], sm[:, 3, :], sm[:, 4, 1:2], None, ALU.mult)
            eng.tensor_scalar(band[:, 2 * T - HD:2 * T - 1], sm[:, 3, 0:HD - 1], sm[:, 4, 1:2], None, ALU.mult).then_inc(s("band"), 1)
        DV.append(a_dve)

        def a_pool(eng):
            eng.wait_ge(s("wvo"), 1)
            eng.wait_ge(s("xn_a"), G)
            eng.tensor_tensor(x[:, :, :], x[:, :, :], bc(bvo[:, :], 1, NB), ALU.add).then_inc(s("xb"), 1)
        PO.append(a_pool)

        def a_sp(eng):
            eng.wait_ge(s("band"), 1)
            eng.dma_start(band_d, band[:, :]).then_inc(s("band_d"), 16)
            eng.wait_ge(s("band_d"), 16)
            src = bass.AP(band_d.tensor, 0, [[1, T], [2 * T, NB], [1, T]])
            for g in range(G):
                eng.dma_start(big[:, g * GB:(g + 1) * GB, :], src[:, g * GB:(g + 1) * GB, :]).then_inc(s(f"C{g}"), 16)
        SP.append(a_sp)

        def split(tag, wait_psum, psum, scale, free, done):
            pass

        def kv_pe(eng):
            eng.wait_ge(s("w1"), 16 * 9)
            for g in range(G):
                eng.wait_ge(s("ctxT"), G)
                if g >= 1:
                    eng.wait_ge(s("kp"), g)
                eng.matmul(bank[0], wk1[:, :], ctxT[:, g * GT:(g + 1) * GT], start=True, stop=True).then_inc(s("kproj"), 1)
                if g >= 1:
                    eng.wait_ge(s("v"), g)
                for j in range(GB):
                    i = eng.matmul(bank[1][:, j * 128:(j + 1) * 128], ctxT[:, g * GT + j * T:g * GT + (j + 1) * T], wv1[:, :],
                                   start=True, stop=True)
                i.then_inc(s("vproj"), 1)
        PE.append(kv_pe)

        def kv_act(eng):
            for g in range(G):
                eng.wait_ge(s("kproj"), g + 1)
                if g >= 1:
                    eng.wait_ge(s("kstack_d"), 16 * PARTS * g)
                eng.activation(p1[:, 0, :], bank[0], ACT.Copy).then_inc(s("k1"), 1)
                eng.wait_ge(s("vproj"), g + 1)
                eng.activation(vals[:, g * GB:(g + 1) * GB, :],
                               bank[1].rearrange("p (b d) -> p b d", b=GB), ACT.Copy).then_inc(s("v"), 1)
                eng.wait_ge(s("kr1"), g + 1)
                eng.activation(p1[:, 1, :], res[:, 0, :], ACT.Copy).then_inc(s("k2"), 1)
                eng.wait_ge(s("kp"), g + 1)
                for i in range(PARTS):
                    eng.dma_start(kstack_d[:, i, :, g * GT:(g + 1) * GT].rearrange("j p t -> p j t"), p1[:, :, :])\
                       .then_inc(s("kstack_d"), 16)
        AC.append(kv_act)

        def kv_dve(eng):
            for g in range(G):
                eng.wait_ge(s("k1"), g + 1)
                eng.tensor_tensor(res[:, 0, :], bank[0], p1[:, 0, :], ALU.subtract).then_inc(s("kr1"), 1)
                eng.wait_ge(s("k2"), g + 1)
                eng.tensor_tensor(p1[:, 2, :], res[:, 0, :], p1[:, 1, :], ALU.subtract).then_inc(s("kp"), 1)
        DV.append(kv_dve)

        def ctxmix_pe(eng):
            for g in range(G):
                eng.wait_ge(s(f"C{g}"), 16)
                if g >= 2:
                    eng.wait_ge(s("gt"), g - 1)
                for j in range(GB):
                    b = g * GB + j
                    i = eng.matmul(bank[2 + g % 2][:, j * T:(j + 1) * T], ctx_s[:, b, :], big[:, b, :], start=True, stop=True)
                i.then_inc(s("gtp"), 1)
                eng.wait_ge(s("gt"), g + 1)
                if g >= 2:
                    eng.wait_ge(s("x1"), g - 1)
                for j in range(GB):
                    i = eng.matmul(bank[4 + g % 2][:, j * D:(j + 1) * D], gt[:, g % 2, j * T:(j + 1) * T], wvo[:, :], start=True, stop=True)
                i.then_inc(s("mix"), 1)
        PE.append(ctxmix_pe)

        def ctxmix_act(eng):
            for g in range(G):
                eng.wait_ge(s("gtp"), g + 1)
                if g >= 2:
                    eng.wait_ge(s("mix"), g - 1)
                eng.activation(gt[:, g % 2, :], bank[2 + g % 2], ACT.Copy).then_inc(s("gt"), 1)
        AC.append(ctxmix_act)

        def ctxmix_dve(eng):
            eng.wait_ge(s("xb"), 1)
            for g in range(G):
                eng.wait_ge(s("mix"), g + 1)
                v = x[:, g * GB:(g + 1) * GB, :].rearrange("p b d -> p (b d)")
                eng.tensor_tensor(v, bank[4 + g % 2], v, ALU.add).then_inc(s("x1"), 1)
        DV.append(ctxmix_dve)

        def finish(eng):
            eng.wait_ge(s("final"), 1)
            eng.dma_start(out.rearrange("b t d -> t b d"), x[:, :, :]).then_inc(s("out"), 16)
            eng.wait_ge(s("out"), 16)

        def done():
            def last(eng):
                eng.wait_ge(s("out"), 16)
            DV.append(lambda eng: chain(eng, "dve").link(eng.tensor_copy(lnv[:, 0, 0:1], ident[:, 0:1])))
            DV.append(lambda eng: eng.tensor_copy(lnv[:, 1, 0:1], ident[:, 0:1]).then_inc(s("final"), 1))
            SP.append(finish)

        def emit():
            with nc.Block() as block:
                for deco, steps in ((block.tensor, PE), (block.vector, DV), (block.scalar, AC), (block.sync, SP), (block.gpsimd, PO)):
                    def body(eng, steps=steps):
                        for f in steps:
                            f(eng)
                    deco(body)

        if STOP == "A":
            DV.append(lambda eng: eng.wait_ge(s("x1"), G))
            SP.append(lambda eng: [eng.wait_ge(s("kstack_d"), 16 * G * PARTS)])
            done()
            emit()
            return

        def nearest(eng, c, dst, src):
            c.link(eng.tensor_scalar(dst, src, ROUND, None, ALU.add))
            c.link(eng.tensor_scalar(dst, dst, -ROUND, None, ALU.add))

        def route(tag):
            def pe(eng):
                eng.wait_ge(s("oh_" + tag), 1)
                eng.matmul(bank[3][:, 0:(NB + 1) * NE], before[:, :], ohb[:, :, :].rearrange("p b e -> p (b e)"), start=True, stop=False)
                for b in range(NB):
                    i = eng.matmul(bank[3][:, (b + 1) * NE:(NB + 1) * NE].rearrange("p (b e) -> p b e", e=NE), onesb[:, :],
                                   bc(ohb[:, b, :], 1, NB - b), start=False, stop=(b == NB - 1))
                i.then_inc(s("rank_" + tag), 1)
            PE.append(pe)

            def dve(eng):
                c = chain(eng, "dve")
                eng.wait_ge(s("rank_" + tag), 1)
                c.link(eng.tensor_scalar(cnt[:, 0, :], bank[3][:, NB * NE:(NB + 1) * NE], 1.0 / T, None, ALU.mult))
                nearest(eng, c, cnt[:, 1, :], cnt[:, 0, :])
                c.link(eng.tensor_tensor(cnt[:, 2, :], cnt[:, 1, :], cnt[:, 0, :], ALU.is_lt))
                c.link(eng.tensor_tensor(cnt[:, 0, :], cnt[:, 1, :], cnt[:, 2, :], ALU.add))
                c.link(eng.tensor_scalar(pre[:, 0, 4:4 + NE], cnt[:, 0, :], float(T), None, ALU.mult))
                for n, d in enumerate((1, 2, 4)):
                    c.link(eng.tensor_tensor(pre[:, n + 1, 4:4 + NE], pre[:, n, 4:4 + NE], pre[:, n, 4 - d:4 + NE - d], ALU.add))
                c.link(eng.tensor_tensor(cnt[:, 2, :], pre[:, 3, 4:4 + NE], pre[:, 0, 4:4 + NE], ALU.subtract))
                c.link(eng.tensor_tensor(lw[:, 0, :, :], bank[3][:, 0:NB * NE].rearrange("p (b e) -> p b e", e=NE),
                                         bc(cnt[:, 2, :], 1, NB), ALU.add))
                c.link(eng.tensor_tensor(lw[:, 1, :, :], lw[:, 0, :, :], oh[:, :, :], ALU.mult))
                c.link(eng.reduce_sum(r16[:, 0, :], lw[:, 1, :, :], AX))
                c.link(eng.tensor_tensor(te_f[:, :, :], bc(pre[0:1, 3, 4:4 + NE], 1, KP), bc(iota_tile[:, :], 2, NE), ALU.is_le))
                c.link(eng.reduce_sum(te_r[:, 0, :], te_f[:, :, :], AX))
                c.link(eng.tensor_scalar(te_r[:, 1, :], te_r[:, 0, :], float(NE - 1), None, ALU.min))
                c.link(eng.tensor_scalar(te_r[:, 0, :], te_r[:, 1, :], float(NE - 1), -float(NE), ALU.is_ge, ALU.mult))
                c.link(eng.scalar_tensor_tensor(te_r[:, 2, :], te_r[:, 1, :], 1.0, te_r[:, 0, :], ALU.add, ALU.add))
                eng.tensor_copy(te_i[:, 0, :], te_r[:, 1, :])
                eng.tensor_copy(te_i[:, 1, :], te_r[:, 2, :]).then_inc(s("te_" + tag), 1)
                slot, q, tile, up, place = (r16[:, k, :] for k in (0, 6, 7, 2, 3))
                c.link(eng.tensor_scalar(q, slot, 1.0 / T, None, ALU.mult))
                nearest(eng, c, tile, q)
                c.link(eng.tensor_tensor(up, tile, q, ALU.is_gt))
                c.link(eng.tensor_tensor(tile, tile, up, ALU.subtract))
                c.link(eng.scalar_tensor_tensor(place, tile, -float(T), slot, ALU.mult, ALU.add))
                eng.tensor_tensor(ohp[:, :, :], bc(iota_p[:, :], 1, NB), bc(place, 2, T), ALU.is_equal)
                c.link(eng.tensor_tensor(ohk[:, :, 0, :], bc(iota_p[:, 0:KP], 1, NB), bc(tile, 2, KP), ALU.is_equal))
                eng.tensor_scalar(ohk[:, :, 1, :], ohk[:, :, 0, :], part[:, 0:1], None, ALU.mult)
                eng.tensor_tensor(ohk[:, :, 2, :], ohk[:, :, 0, :], bc(iota_p[:, 0:NB], 2, KP), ALU.mult).then_inc(s("hot_" + tag), 1)
                eng.wait_ge(s("inv_" + tag), 1)
                c.link(eng.tensor_copy(inv[:, 0:3, :], bank[4][:, 0:3 * KP].rearrange("p (a k) -> p a k", a=3)))
                c.link(eng.scalar_tensor_tensor(inv[:, 3, :], inv[:, 2, :], float(T), inv[:, 1, :], ALU.mult, ALU.add))
                eng.tensor_copy(inv_i[:, 0, :], inv[:, 3, :]).then_inc(s("gather_" + tag), 1)
                c.link(eng.tensor_scalar(inv[:, 1, :], inv[:, 0, :], -1.0, 1.0, ALU.mult, ALU.add))
                c.link(eng.tensor_tensor(inv[:, 2, :], inv[:, 1, :], spare[:, :], ALU.mult))
                eng.tensor_tensor(inv_i[:, 1, :], inv[:, 3, :], inv[:, 2, :], ALU.add).then_inc(s("scatter_" + tag), 1)
            DV.append(dve)

            def pe2(eng):
                eng.wait_ge(s("hot_" + tag), 1)
                for b in range(NB):
                    i = eng.matmul(bank[4][:, 0:3 * KP], ohp[:, b, :], ohk[:, b, :, :].rearrange("p a k -> p (a k)"),
                                   start=(b == 0), stop=(b == NB - 1))
                i.then_inc(s("inv_" + tag), 1)
            PE.append(pe2)

            def sp(eng):
                v = rows_d[tag].rearrange("(b t) d -> t b d", t=T)
                for g in range(G):
                    eng.wait_ge(s("xn_" + tag), g + 1)
                    eng.dma_start(v[:, g * GB:(g + 1) * GB, :], xn[:, g * GB:(g + 1) * GB, :]).then_inc(s("rows_" + tag), 16)
            SP.append(sp)

        class Tile:

            def __init__(self, j, k):
                self.j, self.at = j, k
                self.k, self.r, self.turn = Lin(j, R, k), k % R, Lin(j, 1, k // R)
                self.first, self.last = (j is None and k == n for n in (0, K - 1))
                self.bank = k % 2

            def plus(self, d):
                return Tile(self.j, self.at + d)

        PEEL = R + 1
        TURNS = (K - PEEL) // R

        def tiles(step):
            def run(eng):
                for k in range(PEEL):
                    step(eng, Tile(None, k))
                with eng.Fori(0, TURNS) as j:
                    for k in range(PEEL, PEEL + R):
                        step(eng, Tile(j, k))
                for k in range(PEEL + TURNS * R, K):
                    step(eng, Tile(None, k))
            return run

        layernorm("b", lambda eng, g: eng.wait_ge(s("x1"), g + 1))

        def b_pe(eng):
            eng.wait_ge(s("v"), G)
            for g in range(G):
                eng.wait_ge(s("xn_b"), g + 1)
                if g >= 2:
                    eng.wait_ge(s("xbT"), g - 1)
                for j in range(GB):
                    i = eng.transpose(bank[g % 2][:, j * T:(j + 1) * T], xn[:, g * GB + j, :], ident[:, :])
                i.then_inc(s("xbTp"), 1)
                eng.wait_ge(s("xbT"), g + 1)
                for j in range(GB):
                    b = g * GB + j
                    i = eng.matmul(bank[6][:, b * NE:(b + 1) * NE], big[:, b, :], rw[:, :], start=True, stop=True)
            i.then_inc(s("logit"), 1)
        PE.append(b_pe)

        def b_act(eng):
            for g in range(G):
                eng.wait_ge(s("xbTp"), g + 1)
                eng.wait_ge(s("gtp"), G)
                eng.activation(big[:, g * GB:(g + 1) * GB, :], bank[g % 2].rearrange("p (b t) -> p b t", b=GB), ACT.Copy)\
                   .then_inc(s("xbT"), 1)
            eng.wait_ge(s("shifted"), 1)
            eng.activation(lw[:, 1, :, :], lw[:, 0, :, :], ACT.Exp).then_inc(s("lexp"), 1)
        AC.append(b_act)

        def b_dve(eng):
            c = chain(eng, "dve")
            eng.wait_ge(s("logit"), 1)
            c.link(eng.tensor_tensor(logit[:, :, :], bank[6][:, 0:NB * NE].rearrange("p (b e) -> p b e", e=NE), bc(rb[:, :], 1, NB), ALU.add))
            c.link(eng.reduce_max(r16[:, 1, :], logit[:, :, :], AX))
            eng.tensor_tensor(lw[:, 0, :, :], logit[:, :, :], bc(r16[:, 1, :], 2, NE), ALU.subtract).then_inc(s("shifted"), 1)
            eng.wait_ge(s("consts"), 1)
            c.link(eng.tensor_tensor(oh[:, :, :], logit[:, :, :], bc(r16[:, 1, :], 2, NE), ALU.is_equal))
            c.link(eng.scalar_tensor_tensor(lw[:, 2, :, :], oh[:, :, :], -float(NE), bc(iota_e[:, :], 1, NB), ALU.mult, ALU.add))
            c.link(eng.tensor_reduce(r16[:, 2, :], lw[:, 2, :, :], AX, ALU.min))
            c.link(eng.tensor_scalar(r16[:, 3, :], r16[:, 2, :], float(NE), None, ALU.add))
            c.link(eng.tensor_tensor(oh[:, :, :], bc(iota_e[:, :], 1, NB), bc(r16[:, 3, :], 2, NE), ALU.is_equal))
            eng.tensor_copy(ohb[:, 0:NB, :], oh[:, :, :]).then_inc(s("oh_b"), 1)
            eng.wait_ge(s("lexp"), 1)
            c.link(eng.reduce_sum(r16[:, 4, :], lw[:, 1, :, :], AX))
            c.link(eng.reciprocal(r16[:, 5, :], r16[:, 4, :]))
            eng.tensor_scalar(maxp[:, :], r16[:, 5, :], tg[:, 2:3], None, ALU.mult)
        DV.append(b_dve)
        route("b")

        def experts(tag, wts, steps):
            gated = steps == 1
            CH = C0 if gated else C1
            UP = 2 * F0 if gated else F1
            WD = W0 if gated else W1
            n = {k: s(f"{k}_{tag}") for k in ("xTp", "xT", "h", "half", "act", "yp", "y")}
            xt_in, w_in, b2_in, y_out = ([s(f"{k}_{tag}{i}") for i in range(R)] for k in ("xt_in", "w_in", "b2_in", "y_out"))

            def ring(t, j):
                if gated:
                    return t.k, t.r, t.turn
                return t.k * 2 + j, (2 * t.r + j) % R, Lin(t.j, 2, (2 * t.at + j) // R)

            def weights(eng, t):
                for j in range(steps):
                    q, slot, use = ring(t, j)
                    e = eng.value_load(te_i[0:1, j, ds(t.k.value(), 1)], min_val=0, max_val=NE - 1)
                    wait(eng, n["yp"], q - R + 1)
                    eng.dma_start(wring[:, slot, 0:WD], wts[ds(e, 1)].rearrange("a p w -> (a p) w")).then_inc(w_in[slot], 16)
                    if not gated and j == 0:
                        wait(eng, n["y"], t.k - R + 1)
                        eng.dma_start(b2r[:, t.r, :], b2pair_d[ds(e, 1), :].broadcast_to((128, D))).then_inc(b2_in[t.r], 16)

            def sp(eng):
                eng.wait_ge(s("te_" + tag), 1)
                if not gated:
                    eng.wait_ge(s("b2pair_d"), 16)
                tiles(weights)(eng)
            SP.append(sp)

            def turn_over(eng, t):
                wait(eng, n["xT"], t.k)
                wait(eng, xt_in[t.r], (t.turn + 1) * 16)
                eng.transpose(bank[0][:, 0:T], xt[:, t.r, :], ident[:, :]).then_inc(n["xTp"], 1)

            def up(eng, t, j):
                q, slot, use = ring(t, j)
                hb = t.bank if gated else j
                if j == 0:
                    wait(eng, n["xT"], t.k + 1)
                wait(eng, n["act"], q - 1)
                if not gated:
                    wait(eng, n["half"], q - 1)
                wait(eng, w_in[slot], (use + 1) * 16)
                P = (pairA, pairB)[hb]
                for f in range(UP // 128):
                    g_, o = divmod(f, UP // 256)
                    i = eng.matmul(P[:, g_, o * T:(o + 1) * T], wring[:, slot, f * 128:(f + 1) * 128], xtT[:, t.bank, :],
                                   start=True, stop=True)
                i.then_inc(n["h"], 1)

            def down(eng, t, j):
                q, slot, use = ring(t, j)
                hb = t.bank if gated else j
                wait(eng, n["act"], q + 1)
                if not gated:
                    wait(eng, n["half"], q + 1)
                if j == 0:
                    wait(eng, n["y"], t.k - 1)
                for c_ in range(CH):
                    o = WD - CH * D + c_ * D
                    i = eng.matmul(bank[1 + t.bank][:, 0:D], act[:, hb, c_, :], wring[:, slot, o:o + D],
                                   start=(j == 0 and c_ == 0), stop=(j == steps - 1 and c_ == CH - 1))
                i.then_inc(n["yp"], 1)

            def pe_step(eng, t):
                if t.first:
                    turn_over(eng, t)
                up(eng, t, 0)
                if not t.last:
                    turn_over(eng, t.plus(1))
                if not t.first:
                    down(eng, t.plus(-1), steps - 1)
                if steps == 2:
                    up(eng, t, 1)
                    down(eng, t, 0)
                if t.last:
                    down(eng, t, steps - 1)
            PE.append(tiles(pe_step))

            def act_step(eng, t):
                for j in range(steps):
                    q, slot, use = ring(t, j)
                    hb = t.bank if gated else j
                    P = (pairA, pairB)[hb]
                    wait(eng, n["h"], q + 1)
                    if gated:
                        wait(eng, n["act"], q - 1)
                        eng.activation(sil[:, hb, :], P[:, 0, :], ACT.Silu).then_inc(n["half"], 1)
                    else:
                        wait(eng, n["yp"], q - 1)
                        wait(eng, w_in[slot], (use + 1) * 16)
                        for c_ in range(CH // 2):
                            i = eng.activation(act[:, hb, c_, :], P[:, 0, c_ * T:(c_ + 1) * T], ACT.Relu,
                                               bias=wring[:, slot, UP + c_:UP + c_ + 1])
                        i.then_inc(n["half"], 1)
                    if gated and not t.first:
                        y_copy(eng, t.plus(-1))
                if gated and t.last:
                    y_copy(eng, t)

            def y_copy(eng, t):
                wait(eng, n["yp"], (t.k + 1) * steps)
                wait(eng, y_out[t.r], t.turn * 16)
                eng.activation(ysb[:, t.r, :], bank[1 + t.bank][:, 0:D], ACT.Copy).then_inc(n["y"], 1)
            AC.append(tiles(act_step))

            def y_add(eng, t):
                wait(eng, n["yp"], (t.k + 1) * steps)
                wait(eng, b2_in[t.r], (t.turn + 1) * 16)
                wait(eng, y_out[t.r], t.turn * 16)
                eng.tensor_tensor(ysb[:, t.r, :], bank[1 + t.bank][:, 0:D], b2r[:, t.r, :], ALU.add).then_inc(n["y"], 1)

            def xT(eng, t):
                wait(eng, n["xTp"], t.k + 1)
                wait(eng, n["h"], (t.k - 1) * steps)
                eng.tensor_copy(xtT[:, t.bank, :], bank[0][:, 0:T]).then_inc(n["xT"], 1)

            def dve_step(eng, t):
                if t.first:
                    xT(eng, t)
                for j in range(steps):
                    q, slot, use = ring(t, j)
                    hb = t.bank if gated else j
                    P = (pairA, pairB)[hb]
                    if gated:
                        if not t.last:
                            xT(eng, t.plus(1))
                        wait(eng, n["half"], q + 1)
                        wait(eng, n["yp"], q - 1)
                        eng.tensor_tensor(act[:, hb, :, :].rearrange("p c t -> p (c t)"), P[:, 1, :], sil[:, hb, :], ALU.mult)\
                           .then_inc(n["act"], 1)
                    else:
                        wait(eng, n["h"], q + 1)
                        wait(eng, n["yp"], q - 1)
                        wait(eng, w_in[slot], (use + 1) * 16)
                        for c_ in range(CH // 2, CH):
                            o = c_ - CH // 2
                            i = eng.tensor_scalar(act[:, hb, c_, :], P[:, 1, o * T:(o + 1) * T],
                                                  wring[:, slot, UP + c_:UP + c_ + 1], 0.0, ALU.add, ALU.max)
                        i.then_inc(n["act"], 1)
                        if j == 0:
                            if not t.last:
                                xT(eng, t.plus(1))
                            if not t.first:
                                y_add(eng, t.plus(-1))
                if not gated and t.last:
                    y_add(eng, t)
            DV.append(tiles(dve_step))

            AHEAD = R - 1

            def gather(eng, t):
                wait(eng, n["xTp"], t.k - R + 1)
                eng.indirect_dma_start(out=xt[:, t.r, :], out_offset=None, in_=rows_d[tag],
                                       in_offset=bass.IndirectOffsetOnAxis(ap=inv_i[:, 0, t.at:t.at + 1], axis=0)).then_inc(xt_in[t.r], 16)

            def scatter(eng, t):
                wait(eng, n["y"], t.k + 1)
                eng.indirect_dma_start(out=back_d[tag], out_offset=bass.IndirectOffsetOnAxis(ap=inv_i[:, 1, t.at:t.at + 1], axis=0),
                                       in_=ysb[:, t.r, :], in_offset=None).then_inc(y_out[t.r], 16)

            def pool(eng):
                eng.wait_ge(s("gather_" + tag), 1)
                eng.wait_ge(s("rows_" + tag), 16 * G)
                every = [Tile(None, k) for k in range(K)]
                for t in every[:AHEAD]:
                    gather(eng, t)
                eng.wait_ge(s("scatter_" + tag), 1)
                for t in every:
                    if t.at + AHEAD < K:
                        gather(eng, every[t.at + AHEAD])
                    scatter(eng, t)
            PO.append(pool)

            def sp_back(eng):
                for r in range(R):
                    eng.wait_ge(y_out[r], 16 * ((K - r + R - 1) // R))
                v = back_d[tag][0:NTOK, :].rearrange("(b t) d -> t b d", t=T)
                for g in range(G):
                    eng.dma_start(ctx_s[:, g * GB:(g + 1) * GB, :], v[:, g * GB:(g + 1) * GB, :]).then_inc(s(f"back_{tag}{g}"), 16)
            SP.append(sp_back)

        experts("b", A["wts0"], 1)

        def b_add(eng):
            for b in range(NB):
                if b % GB == 0:
                    eng.wait_ge(s(f"back_b{b // GB}"), 16)
                i = eng.scalar_tensor_tensor(x[:, b, :], ctx_s[:, b, :], maxp[:, b:b + 1], x[:, b, :], ALU.mult, ALU.add)
                if b % GB == GB - 1:
                    i.then_inc(s("x2"), 1)
        DV.append(b_add)

        if STOP == "B":
            DV.append(lambda eng: eng.wait_ge(s("x2"), G))
            SP.append(lambda eng: [eng.wait_ge(s("kstack_d"), 16 * G * PARTS)])
            done()
            emit()
            return

        layernorm("c", lambda eng, g: eng.wait_ge(s("x2"), g + 1))

        def q_pe(eng):
            for g in range(G):
                eng.wait_ge(s("xn_c"), g + 1)
                if g >= 2:
                    eng.wait_ge(s("xcT"), g - 1)
                for j in range(GB):
                    i = eng.transpose(bank[g % 2][:, j * T:(j + 1) * T], xn[:, g * GB + j, :], ident[:, :])
                i.then_inc(s("xcTp"), 1)
                eng.wait_ge(s("xcT"), g + 1)
                if g >= 2:
                    eng.wait_ge(s("qp"), g - 1)
                eng.matmul(bank[2 + g % 2], wq1[:, :], big[:, g * GB:(g + 1) * GB, :].rearrange("p b t -> p (b t)"), start=True, stop=True)\
                   .then_inc(s("qproj"), 1)
        PE.append(q_pe)

        QS = HD ** -0.5

        def q_act(eng):
            for g in range(G):
                eng.wait_ge(s("xcTp"), g + 1)
                eng.activation(big[:, g * GB:(g + 1) * GB, :].rearrange("p b t -> p (b t)"), bank[g % 2], ACT.Copy).then_inc(s("xcT"), 1)
                eng.wait_ge(s("qproj"), g + 1)
                eng.wait_ge(s("kstack_d"), 16 * PARTS * G)
                if g >= 1:
                    eng.wait_ge(s("qstack_d"), 16 * PARTS * g)
                eng.activation(p1[:, 0, :], bank[2 + g % 2], ACT.Copy, scale=QS).then_inc(s("q1"), 1)
                eng.wait_ge(s("qr1"), g + 1)
                eng.activation(p1[:, 1, :], res[:, 0, :], ACT.Copy).then_inc(s("q2"), 1)
                eng.wait_ge(s("qp"), g + 1)
                for j in range(PARTS):
                    eng.dma_start(qstack_d[j, :, :, g * GT:(g + 1) * GT].rearrange("i p t -> p i t"), p1[:, :, :])\
                       .then_inc(s("qstack_d"), 16)
        AC.append(q_act)

        def q_dve(eng):
            for g in range(G):
                eng.wait_ge(s("q1"), g + 1)
                eng.scalar_tensor_tensor(res[:, 0, :], bank[2 + g % 2], QS, p1[:, 0, :], ALU.mult, ALU.subtract).then_inc(s("qr1"), 1)
                eng.wait_ge(s("q2"), g + 1)
                eng.tensor_tensor(p1[:, 2, :], res[:, 0, :], p1[:, 1, :], ALU.subtract).then_inc(s("qp"), 1)
        DV.append(q_dve)

        BODY = 2 * GB
        LAG = 7

        class At:

            def __init__(self, j, turn, r):
                self.j, self.turn, self.r = j, Lin(j, 1, turn), r
                self.lo = BODY * turn + r

            def on(self, k):
                return self.j is not None or 0 <= self.lo - k < NU

            def unit(self, k):
                return Lin(self.j, BODY, self.lo - k)

            def batch(self, k):
                return Lin(self.j, BODY // 2, (self.lo - k) // 2)

            def half(self, k):
                return (self.r - k) % 2

            def pair(self, k):
                return ((self.r - k) // 2) % 2

        def units(step):
            def run(eng):
                for r in range(BODY):
                    step(eng, At(None, 0, r))
                with eng.Fori(0, NU // BODY - 1) as j:
                    for r in range(BODY):
                        step(eng, At(j, 1, r))
                for r in range(LAG):
                    step(eng, At(None, NU // BODY, r))
            return run

        def c_sp(eng):
            eng.wait_ge(s("kstack_d"), 16 * PARTS * G)

            def load(turn, slot):
                pair = turn * 2 + slot
                if slot == 0:
                    wait(eng, s("qstack_d"), (turn + 1) * (16 * PARTS))
                wait(eng, s("ST"), (pair - 1) * 4)
                for t_, d_ in ((ks, kstack_d), (qs, qstack_d)):
                    v = d_.rearrange("j i (d h) t -> (j i d) h t", h=H)
                    eng.dma_start(t_[:, slot, :, :], v[:, :, ds((pair * (2 * T)).value(), 2 * T)]).then_inc(s(f"qk{slot}"), 16)
            load(Lin(None, 0, 0), 0)
            load(Lin(None, 0, 0), 1)
            with eng.Fori(0, G - 1) as j:
                load(Lin(j, 1, 1), 0)
                load(Lin(j, 1, 1), 1)
        SP.append(c_sp)

        def c_pe(eng):
            def heads(r):
                slot, off, u = (r // 4) % 2, ((r // 2) % 2) * T, r % 2
                return [(h, qs[:, slot, u * HU + h, off:off + T], ks[:, slot, u * HU + h, off:off + T]) for h in range(HU)]

            def step(eng, at):
                if at.on(1):
                    wait(eng, s("mparts"), at.unit(0))
                    wait(eng, s("mrow"), at.unit(1))
                    eng.transpose(mTp, mparts[:, at.half(1), :, :].rearrange("p i h -> p (i h)"), identb[:, :]).then_inc(s("mT"), 1)
                if at.on(0):
                    if at.r % 4 == 0:
                        wait(eng, s(f"qk{at.r // 4}"), (at.turn + 1) * 32)
                    wait(eng, s("mx"), at.unit(0))
                    for h, q_, k_ in heads(at.r):
                        i = eng.matmul(pairA[:, h // 4, (h % 4) * T:(h % 4 + 1) * T], q_, k_, start=True, stop=True)
                    i.then_inc(s("S"), 1)
                if at.on(1):
                    wait(eng, s("mrow"), at.unit(0))
                    wait(eng, s("P"), at.unit(1))
                    for h, q_, k_ in heads((at.r - 1) % BODY):
                        o = pairB[:, h // 4, (h % 4) * T:(h % 4 + 1) * T]
                        eng.matmul(o, k_, q_, start=True, stop=False)
                        i = eng.matmul(o, pick[:, h, :], mrow[:, at.half(1), :], start=False, stop=True)
                    i.then_inc(s("ST"), 1)
                if at.on(2):
                    u = at.half(2)
                    wait(eng, s("P"), at.unit(1))
                    if u == 0:
                        wait(eng, s("osb"), at.batch(2))
                        wait(eng, s("vp"), at.batch(0))
                    for h in range(HU):
                        hh = u * HU + h
                        i = eng.matmul(bank[1][32 * (hh % 4):32 * (hh % 4) + 32, (hh // 4) * T:(hh // 4 + 1) * T],
                                       vpad[:, at.pair(2), hh, :], prob[:, at.half(2), h, :], start=True, stop=True,
                                       tile_position=(0, 32 * (hh % 4)))
                    i.then_inc(s("O"), 1)
                if at.r % 2 == 0 and at.on(4):
                    wait(eng, s("osb"), at.batch(2))
                    wait(eng, s("an"), at.batch(4))
                    for j in range(4):
                        i = eng.transpose(bank[2][:, j * 128:(j + 1) * 128], osb[:, j * 128:(j + 1) * 128], ident[:, :])
                    i.then_inc(s("oT"), 1)
                if at.r % 2 == 1 and at.on(5):
                    wait(eng, s("an"), at.batch(3))
                    wait(eng, s("x3"), at.batch(5))
                    eng.transpose(bank[3][:, 0:T], an[:, :], ident[:, :]).then_inc(s("anTp"), 1)
                if at.r % 2 == 0 and at.on(6):
                    wait(eng, s("anT"), at.batch(4))
                    eng.matmul(bank[3][:, T:T + D], anT[:, :], wo1[:, :], start=True, stop=True).then_inc(s("proj"), 1)
            units(step)(eng)
        PE.append(c_pe)

        def c_act(eng):
            def step(eng, at):
                if at.on(1):
                    wait(eng, s("mT"), at.unit(0))
                    wait(eng, s("ST"), at.unit(2))
                    eng.activation(mrow[:, at.half(1), :], mTp, ACT.Copy).then_inc(s("mrow"), 1)
                if at.r % 2 == 0 and at.on(4):
                    wait(eng, s("O"), at.unit(2))
                    wait(eng, s("oT"), at.batch(4))
                    eng.activation(osb[:, :], bank[1], ACT.Copy).then_inc(s("osb"), 1)
                if at.on(1):
                    wait(eng, s("ST"), at.unit(0))
                    wait(eng, s("O"), at.unit(2))
                    eng.activation(prob[:, at.half(1), :, :].rearrange("p h t -> p (h t)"), pairB[:, :, :].rearrange("p a t -> p (a t)"), ACT.Exp)\
                       .then_inc(s("P"), 1)
                if at.r % 2 == 1 and at.on(5):
                    wait(eng, s("anTp"), at.batch(3))
                    wait(eng, s("proj"), at.batch(5))
                    eng.activation(anT[:, :], bank[3][:, 0:T], ACT.Copy).then_inc(s("anT"), 1)
            units(step)(eng)
        AC.append(c_act)

        def c_dve(eng):
            c = chain(eng, "dve")

            def step(eng, at):
                if at.on(0):
                    wait(eng, s("S"), at.unit(0) + 1)
                    m = negm[:, 0, :]
                    mp = mparts[:, at.half(0), :, :]
                    wait(eng, s("mT"), at.unit(1))
                    i = eng.reduce_max(m, pairA[:, :, :].rearrange("p a (h t) -> p (a h) t", t=T), AX)
                    i.then_inc(s("mx"), 1)
                    wait(eng, s("mx"), at.unit(0) + 1)
                    c.link(eng.tensor_scalar(mp[:, 0, :], m, -1.0, None, ALU.mult))
                    c.link(eng.scalar_tensor_tensor(negm[:, 1, :], m, -1.0, mp[:, 0, :], ALU.mult, ALU.subtract))
                    c.link(eng.tensor_copy(mp[:, 1, :], negm[:, 1, :]))
                    eng.tensor_tensor(mp[:, 2, :], negm[:, 1, :], mp[:, 1, :], ALU.subtract).then_inc(s("mparts"), 1)
                if at.r % 2 == 0 and at.on(4):
                    wait(eng, s("oT"), at.batch(2))
                    wait(eng, s("anTp"), at.batch(4))
                    v = bank[2].rearrange("p (h c) -> p h c", c=VW)
                    i = eng.reciprocal(rl[:, :], v[:, :, HD])
                    i.then_inc(s("rl"), 1)
                    wait(eng, s("rl"), at.batch(2))
                    eng.tensor_tensor(an[:, :].rearrange("p (h c) -> p h c", c=HD), v[:, :, 0:HD], bc(rl[:, :], 2, HD), ALU.mult)\
                       .then_inc(s("an"), 1)
                if at.r % 2 == 0 and at.on(6):
                    wait(eng, s("proj"), at.batch(4))
                    xb = x[:, ds(at.batch(6).value(), 1), :].rearrange("p a d -> p (a d)")
                    eng.tensor_tensor(xb, bank[3][:, T:T + D], xb, ALU.add).then_inc(s("x3"), 1)

            for r in range(BODY):
                step(eng, At(None, 0, r))
            with eng.Fori(0, G - 1) as j:
                c.enter(j, 3 * BODY)
                for r in range(BODY):
                    step(eng, At(j, 1, r))
            c.leave(G - 1)
            for r in range(LAG):
                step(eng, At(None, NU // BODY, r))
        DV.append(c_dve)

        def c_pool(eng):
            eng.wait_ge(s("v"), G)

            def fill(turn, slot):
                b = turn * 2 + slot
                wait(eng, s("O"), (b - 1) * 2)
                eng.tensor_copy(vpad[:, slot, :, 0:HD], vals[:, ds(b.value(), 1), :].rearrange("p a (h d) -> p (a h) d", h=H))\
                   .then_inc(s("vp"), 1)
            fill(Lin(None, 0, 0), 0)
            fill(Lin(None, 0, 0), 1)
            with eng.Fori(0, NB // 2 - 1) as j:
                fill(Lin(j, 1, 1), 0)
                fill(Lin(j, 1, 1), 1)
        PO.append(c_pool)

        if STOP == "C":
            DV.append(lambda eng: eng.wait_ge(s("x3"), NB))
            done()
            emit()
            return

        layernorm("d", lambda eng, g: eng.wait_ge(s("x3"), GB * g + GB))

        def d_dve(eng):
            c = chain(eng, "dve")
            a_, b_, c_, d_, e_ = (r16[:, k, :] for k in range(5))
            c.link(eng.tensor_tensor(a_, xn[:, :, 0], xn[:, :, 1], ALU.add))
            c.link(eng.tensor_scalar(b_, a_, -1.0, None, ALU.mult))
            c.link(eng.tensor_tensor(b_, a_, b_, ALU.max))
            nearest(eng, c, c_, b_)
            c.link(eng.tensor_tensor(d_, c_, b_, ALU.is_gt))
            c.link(eng.tensor_tensor(c_, c_, d_, ALU.subtract))
            c.link(eng.tensor_scalar(d_, a_, 0.0, 2.0, ALU.is_ge, ALU.mult))
            c.link(eng.scalar_tensor_tensor(e_, d_, -1.0, c_, ALU.add, ALU.mult))
            c.link(eng.tensor_scalar(b_, e_, 64.0, None, ALU.add))
            c.link(eng.tensor_scalar(a_, b_, 1.0 / NE, None, ALU.mult))
            nearest(eng, c, c_, a_)
            c.link(eng.tensor_tensor(d_, c_, a_, ALU.is_gt))
            c.link(eng.tensor_tensor(c_, c_, d_, ALU.subtract))
            c.link(eng.scalar_tensor_tensor(e_, c_, -float(NE), b_, ALU.mult, ALU.add))
            c.link(eng.tensor_tensor(oh[:, :, :], bc(iota_e[:, :], 1, NB), bc(e_, 2, NE), ALU.is_equal))
            eng.tensor_copy(ohb[:, 0:NB, :], oh[:, :, :]).then_inc(s("oh_d"), 1)
            eng.tensor_scalar(maxp[:, 0:1], tg[:, 3:4], 0.5, None, ALU.mult).then_inc(s("half_gate"), 1)
        DV.append(d_dve)
        route("d")
        experts("d", A["wts1"], 2)

        def d_add(eng):
            eng.wait_ge(s("half_gate"), 1)
            for b in range(NB):
                if b % GB == 0:
                    eng.wait_ge(s(f"back_d{b // GB}"), 16)
                i = eng.scalar_tensor_tensor(x[:, b, :], ctx_s[:, b, :], maxp[:, 0:1], x[:, b, :], ALU.mult, ALU.add)
                if b % GB == GB - 1:
                    i.then_inc(s("x4"), 1)
        DV.append(d_add)

        def d_out(eng):
            o = out.rearrange("b t d -> t b d")
            for g in range(G):
                eng.wait_ge(s("x4"), g + 1)
                eng.dma_start(o[:, g * GB:(g + 1) * GB, :], x[:, g * GB:(g + 1) * GB, :]).then_inc(s("out"), 16)
            eng.wait_ge(s("out"), 16 * G)
        SP.append(d_out)
        emit()




_OUT = (16, 128, 128)


def kernel(x, ctx_1024, g_xattn, g_ffn, L0_xattn_Wq, L0_xattn_bq, L0_xattn_Wk, L0_xattn_bk, L0_xattn_Wv, L0_xattn_bv,
           L0_xattn_Wo, L0_xattn_bo, L0_ffn_router_w, L0_ffn_router_b, L0_ffn_w1, L0_ffn_w2, L1_xattn_w_q, L1_xattn_w_k,
           L1_xattn_w_v, L1_xattn_w_o, L1_ffn_W1, L1_ffn_b1, L1_ffn_W2, L1_ffn_b2):
    import concourse.bacc as bacc
    from concourse.bass_utils import run_bass_kernel_spmd

    def rev(w):
        return w.reshape(*w.shape[:-1], 16, 8)[..., ::-1].reshape(w.shape)

    def dh(w):
        return w.reshape(128, 16, 8).transpose(0, 2, 1).reshape(128, 128)

    def rows(w):
        return w.reshape(8, -1, 128, 128).transpose(0, 2, 1, 3).reshape(8, 128, -1)

    a = {k: np.asarray(v) for k, v in locals().items() if not callable(v) and hasattr(v, "shape")}
    arrays = {
        "x": a["x"], "ctx": a["ctx_1024"][:, ::-1, :],
        "gates": np.concatenate([a["g_xattn"], a["g_ffn"]]).reshape(1, 4),
        "wq0": rev(a["L0_xattn_Wq"].T), "wk0": rev(a["L0_xattn_Wk"].T), "wv0": a["L0_xattn_Wv"], "wo0": a["L0_xattn_Wo"].T,
        "bq": rev(a["L0_xattn_bq"]).reshape(1, 128), "bk": rev(a["L0_xattn_bk"]).reshape(1, 128),
        "bv": a["L0_xattn_bv"].reshape(128, 1), "bo": a["L0_xattn_bo"].reshape(1, 128),
        "rw": a["L0_ffn_router_w"], "rb": a["L0_ffn_router_b"].reshape(1, 8),
        "wts0": np.concatenate([a["L0_ffn_w1"], rows(a["L0_ffn_w2"])], axis=2),
        "wq1": dh(a["L1_xattn_w_q"].T), "wk1": dh(a["L1_xattn_w_k"].T), "wv1": a["L1_xattn_w_v"].T, "wo1": a["L1_xattn_w_o"].T,
        "wts1": np.concatenate([a["L1_ffn_W1"], a["L1_ffn_b1"].reshape(8, 4, 128).transpose(0, 2, 1), rows(a["L1_ffn_W2"])], axis=2),
        "b2": a["L1_ffn_b2"],
    }
    arrays = {k: np.ascontiguousarray(v) for k, v in arrays.items()}
    nc = bacc.Bacc("TRN2", target_bir_lowering=False, num_devices=1)
    aps = {k: nc.dram_tensor("in_" + k, v.shape, mybir.dt.from_np(v.dtype), kind="ExternalInput").ap() for k, v in arrays.items()}
    out = nc.dram_tensor("out_x", _OUT, mybir.dt.float32, kind="ExternalOutput").ap()
    build(nc, aps, out)
    r = run_bass_kernel_spmd(nc, [{"in_" + k: v for k, v in arrays.items()}], core_ids=[0])
    return r.results[0]["out_x"]
```

```python
import numpy as np
import concourse.bass as bass
from concourse import mybir
from contextlib import ExitStack



class Chain:

    def __init__(self, eng, sem):
        self.eng, self.sem, self.base, self.k, self.inside = eng, sem, 0, 0, None

    def link(self, ins):
        ins.then_inc(self.sem, 1)
        self.k += 1
        self.eng.wait_ge(self.sem, self.base + self.k)

    def enter(self, i, per):
        self.inside = (self.base + self.k, per)
        self.base, self.k = self.base + self.k + i * per, 0

    def leave(self, turns):
        start, per = self.inside
        assert self.k == per, (self.k, per)
        self.base, self.k, self.inside = start + per * turns, 0, None


class Lin:

    def __init__(self, j, a, b):
        self.j, self.a, self.b = j, a if j is not None else 0, b

    def __add__(self, n):
        return Lin(self.j, self.a, self.b + n)

    def __sub__(self, n):
        return self + -n

    def __mul__(self, n):
        return Lin(self.j, self.a * n, self.b * n)

    def value(self):
        return self.b if self.j is None else self.j * self.a + self.b


def wait(eng, sem, count):
    if isinstance(count, Lin):
        if count.b <= 0:
            assert count.j is None
            return
        count = count.value()
    elif count <= 0:
        return
    eng.wait_ge(sem, count)


FFN = (512, 512)


def build(nc, A, out):
    f32, bf16, i32 = mybir.dt.float32, mybir.dt.bfloat16, mybir.dt.int32
    ALU, ACT, AX = mybir.AluOpType, mybir.ActivationFunctionType, mybir.AxisListType.X
    ds = bass.ds

    NB, T, D = A["x"].shape
    H, HD = 16, 8
    NE = A["rw"].shape[1]
    F0, F1 = FFN
    C0, C1 = F0 // T, F1 // T
    W0, W1 = 3 * F0, 2 * F1 + C1
    G, GB = 4, NB // 4
    GT = GB * T
    NTOK = NB * T
    K = NTOK // T + NE - 1
    KP = K + 1
    R = 4
    EPS = 1e-5
    NEWTON = 3
    ROUND = 1.5 * 2.0 ** 23
    PARTS = 3
    SK = PARTS * PARTS * HD
    HU = H // 2
    NU = 2 * NB
    VW = 16

    WARM = (20, 22, 30, 20, 44, 30, 4)
    ctx = ExitStack()

    def sb(name, shape, dt=f32):
        return ctx.enter_context(nc.sbuf_tensor(name, shape, dt))

    def sem(name):
        return ctx.enter_context(nc.semaphore(name))

    def bc(ap, at, n):
        shape = list(ap.shape)
        return ap.unsqueeze(at).broadcast_to(shape[:at] + [n] + shape[at:])

    def scratch(name, shape, dt=f32):
        return nc.dram_tensor(name, shape, dt, kind="Internal").ap()

    with ctx:
        band_d = scratch("band_d", (NB, 2 * T))
        kstack_d = scratch("kstack_d", (PARTS, PARTS, HD * H, NTOK), bf16)
        qparts_d = scratch("qparts_d", (PARTS, HD * H, NTOK), bf16)
        rows_d = {k: scratch(f"rows_{k}_d", (NTOK, D)) for k in "bd"}
        back_d = {k: scratch(f"back_{k}_d", (NTOK + K * T, D)) for k in "bd"}
        b2pair_d = scratch("b2pair_d", (NE, D))

        bank = [ctx.enter_context(nc.psum_tensor(f"bank{i}", [128, 512], f32)) for i in range(4)]
        pairA = ctx.enter_context(nc.psum_tensor("pairA", [128, 2, 512], f32))
        pairB = ctx.enter_context(nc.psum_tensor("pairB", [128, 2, 512], f32))
        bank += [pairA[:, 0, :], pairA[:, 1, :], pairB[:, 0, :], pairB[:, 1, :]]
        for i in range(4):
            bank[i] = bank[i][:, :]
        mTp = bank[0].bitcast(bf16)[0:PARTS * HU, 0:T]

        ident = sb("ident", [128, 128])
        before = sb("before", [128, 128], bf16)
        onesb = sb("onesb", [128, 128], bf16)
        onesf = sb("onesf", [128, 128])
        onehot_b = sb("onehot_b", [128, NB, NB])
        pick = sb("pick", [PARTS * HU, HU, T], bf16)
        iota_e = sb("iota_e", [128, NE])
        iota_tile = sb("iota_tile", [1, KP])
        iota_p = sb("iota_p", [128, T])
        part = sb("part", [128, 1])
        spare = sb("spare", [128, KP])
        gates = sb("gates", [128, 4])
        tg = sb("tg", [128, 4])
        half_gate = sb("half_gate", [128, 1])
        wq0, wk0, wv0, wo0 = (sb(n, [128, 128]) for n in ("wq0", "wk0", "wv0", "wo0"))
        wq1, wk1, wv1, wo1 = (sb(n, [128, 128]) for n in ("wq1", "wk1", "wv1", "wo1"))
        bqk = sb("bqk", [1, 2, 128])
        bo_row = sb("bo_row", [1, 128])
        bv_col = sb("bv_col", [128, 1])
        rw = sb("rw", [128, NE])
        rb = sb("rb", [128, NE])
        len_row = sb("len_row", [1, 128])
        b2a = sb("b2a", [NE, D])
        b2b = sb("b2b", [NE, D])
        x = sb("x", [128, NB, D])
        xn = sb("xn", [128, NB, D])
        ctx_s = sb("ctx_s", [128, NB, D])
        big = sb("big", [128, NB, 128])
        ctxT = sb("ctxT", [128, NTOK])
        vals = sb("vals", [128, NB, D])
        vpad = sb("vpad", [128, 2, H // 2, 2, 3 * VW])
        qs = sb("qs", [SK, 2, H, 2 * T], bf16)
        ks = sb("ks", [SK, 2, H, 2 * T], bf16)
        prob = sb("prob", [128, 2, HU, T])
        maxi = sb("maxi", [128, 2, HU])
        zeros = sb("zeros", [128, HU])
        mrest = sb("mrest", [128, 2, HU])
        mparts = sb("mparts", [128, 2, PARTS, HU], bf16)
        mrow = sb("mrow", [PARTS * HU, 2, T], bf16)
        osb = sb("osb", [128, 2 * T])
        rl = sb("rl", [128, H])
        an = sb("an", [128, D])
        anT = sb("anT", [128, T])
        identb = sb("identb", [128, 128], bf16)
        st = sb("st", [128, NB, 6])
        lnv = sb("lnv", [128, 8, NB])
        lni = sb("lni", [128, NB], i32)
        sums = sb("sums", [NB, 128])
        sumsT = sb("sumsT", [128, 2, NB])
        ks_sb = sb("ks_sb", [NB, 128])
        prod = sb("prod", [NB, 128])
        sm = sb("sm", [NB, 5, HD])
        band = sb("band", [NB, 2 * T])
        wvo = sb("wvo", [128, 128])
        bvo = sb("bvo", [128, 128])
        gt = sb("gt", [128, 2, 512])
        parts = sb("parts", [128, G, PARTS, GT], bf16)
        res = sb("res", [128, 2, GT])
        ohr = sb("ohr", [128, NB, NB])
        fill_b = sb("fill_b", [128, 512], bf16)
        logit = sb("logit", [128, NB, NE])
        lw = sb("lw", [128, 3, NB, NE])
        oh = sb("oh", [128, NB, NE])
        ohb = sb("ohb", [128, NB + 1, NE], bf16)
        r16 = sb("r16", [128, 8, NB])
        cnt = sb("cnt", [128, 3, NE])
        pre = sb("pre", [128, 4, 4 + NE])
        te_f = sb("te_f", [1, KP, NE])
        te_r = sb("te_r", [1, 3, KP])
        te_i = sb("te_i", [1, 2, KP], i32)
        maxp = sb("maxp", [128, NB])
        ohp = sb("ohp", [128, NB, T], bf16)
        ohk = sb("ohk", [128, NB, 3, KP], bf16)
        inv = sb("inv", [128, 4, KP])
        inv_i = sb("inv_i", [128, 2, KP], i32)
        wring = sb("wring", [128, R, W0])
        b2r = sb("b2r", [128, R, D])
        xt = sb("xt", [128, R, D])
        xtT = sb("xtT", [128, 2, T])
        sil = sb("sil", [128, 2, F0])
        act = sb("act", [128, 2, C0, T])
        ysb = sb("ysb", [128, R, D])

        S = {}

        def s(name):
            if name not in S:
                S[name] = sem("s_" + name)
            return S[name]

        PE, DV, AC, SP, PO = [], [], [], [], []
        ch = {}

        def chain(eng, name):
            if name not in ch:
                ch[name] = Chain(eng, s("chain_" + name))
            return ch[name]

        BY_DVE, BY_POOL = (0, 1), (2, 3)
        MEAN, RSTD, NMR = (lnv[:, k, :] for k in (6, 3, 7))

        def stats(eng, b):
            return eng.bn_stats(st[:, b, :].rearrange("p a d -> p (a d)"), x[:, b, :].rearrange("p a d -> p (a d)"))

        def rstd(tag, last):
            def dve(eng):
                c = chain(eng, "dve")
                last(eng, c)
                me, mo, ve, vo = (st[:, :, k] for k in (1, 4, 2, 5))
                diff, total, var, y, t, u, mean, nmr = (lnv[:, k, :] for k in range(8))
                eng.tensor_tensor(diff, me, mo, ALU.subtract)
                eng.tensor_tensor(total, me, mo, ALU.add)
                c.link(eng.tensor_tensor(var, ve, vo, ALU.add))
                eng.tensor_scalar(mean, total, 0.5, None, ALU.mult)
                c.link(eng.tensor_tensor(t, diff, diff, ALU.mult))
                c.link(eng.scalar_tensor_tensor(u, t, D / 4.0, var, ALU.mult, ALU.add))
                c.link(eng.tensor_scalar(var, u, 1.0 / D, EPS, ALU.mult, ALU.add))
                c.link(eng.tensor_scalar(lni[:, :], var.bitcast(i32), 1, None, ALU.logical_shift_right))
                c.link(eng.tensor_scalar(y.bitcast(i32), lni[:, :], -1.0, float(0x5F3759DF), ALU.mult, ALU.add))
                for _ in range(NEWTON):
                    c.link(eng.tensor_tensor(t, y, y, ALU.mult))
                    c.link(eng.scalar_tensor_tensor(u, t, -0.5, var, ALU.mult, ALU.mult))
                    c.link(eng.scalar_tensor_tensor(y, u, 1.5, y, ALU.add, ALU.mult))
                eng.scalar_tensor_tensor(nmr, mean, -1.0, y, ALU.mult, ALU.mult).then_inc(s("rstd"), 1)
                eng.wait_ge(s("rstd"), "abcd".index(tag) + 1)
            DV.append(dve)

        xn_made = {name: 0 for name in "DAP"}

        def normalise(tag, who):
            def dve(eng, b):
                return eng.tensor_scalar(xn[:, b, :], x[:, b, :], MEAN[:, b:b + 1], RSTD[:, b:b + 1], ALU.subtract, ALU.mult)

            def act(eng, b):
                return eng.activation(xn[:, b, :], x[:, b, :], ACT.Identity, bias=NMR[:, b:b + 1], scale=RSTD[:, b:b + 1])

            before_ = dict(xn_made)
            for queue, name, one in ((DV, "D", dve), (AC, "A", act), (PO, "P", dve)):
                mine = [j for j in range(GB) if who[j] == name]
                if not mine:
                    continue
                xn_made[name] += G

                def run(eng, mine=mine, name=name, one=one):
                    eng.wait_ge(s("rstd"), "abcd".index(tag) + 1)
                    for g in range(G):
                        for j in mine:
                            i = one(eng, g * GB + j)
                        i.then_inc(s(f"xn{name}"), 1)
                queue.append(run)

            def ready(eng, g):
                for name in sorted(set(who)):
                    eng.wait_ge(s(f"xn{name}"), before_[name] + g + 1)
            return ready

        def warm(eng, bank_, n):
            for _ in range(n):
                eng.matmul(bank_, onesb[:, :], fill_b[:, :], start=True, stop=True)

        def load_x(eng, g):
            eng.dma_start(x[:, g * GB:(g + 1) * GB, :], A["x"][g * GB:(g + 1) * GB].rearrange("b t d -> t b d")).then_inc(s(f"x_in{g}"), 16)

        def loads_sp(eng):
            for g in range(G // 2):
                load_x(eng, g)
            for n, t in (("wv0", wv0), ("wo0", wo0), ("wq0", wq0), ("wk0", wk0)):
                eng.dma_start(t[:, :], A[n]).then_inc(s("w0"), 16)
            eng.dma_start(bqk[:, 0, :], A["bq"]).then_inc(s("w0"), 16)
            eng.dma_start(bqk[:, 1, :], A["bk"]).then_inc(s("w0"), 16)
            eng.dma_start(bo_row[:, :], A["bo"]).then_inc(s("w0"), 16)
            eng.dma_start(bv_col[:, :], A["bv"]).then_inc(s("w0"), 16)
            for n, t in (("wk1", wk1), ("wv1", wv1), ("wq1", wq1), ("wo1", wo1)):
                eng.dma_start(t[:, :], A[n]).then_inc(s("w1"), 16)
            eng.dma_start(rw[:, :], A["rw"]).then_inc(s("w1"), 16)
            eng.dma_start(rb[:, :], A["rb"].broadcast_to((128, NE))).then_inc(s("w1"), 16)
            eng.dma_start(b2a[:, :], A["b2"]).then_inc(s("w1"), 16)
            eng.dma_start(b2b[0:NE - 1, :], A["b2"][1:NE, :]).then_inc(s("w1"), 16)
            eng.dma_start(b2b[NE - 1:NE, :], A["b2"][0:1, :]).then_inc(s("w1"), 16)
        SP.append(loads_sp)

        def loads_act(eng):
            for g in range(G // 2, G):
                load_x(eng, g)
            eng.dma_start(gates[:, :], A["gates"].broadcast_to((128, 4))).then_inc(s("gates"), 16)
            for g in range(G):
                eng.dma_start(ctx_s[:, g * GB:(g + 1) * GB, :], A["ctx"][g * GB:(g + 1) * GB].rearrange("b t d -> t b d")).then_inc(s(f"ctx{g}"), 16)
            eng.wait_ge(s("gates"), 16)
            eng.activation(tg[:, :], gates[:, :], ACT.Tanh).then_inc(s("tg"), 1)
        AC.append(loads_act)

        def consts(eng):
            eng.memset(onesb[:, :], 1.0)
            eng.memset(fill_b[:, :], 0.0).then_inc(s("fill"), 1)
            eng.memset(ident[:, :], 0.0).then_inc(s("c0"), 1)
            eng.wait_ge(s("c0"), 1)
            eng.affine_select(out=ident[:, :], in_=ident[:, :], compare_op=ALU.not_equal, fill=1.0,
                              base=0, pattern=[[-1, 128]], channel_multiplier=1).then_inc(s("ident"), 1)
            eng.memset(onehot_b[:, :, :], 0.0).then_inc(s("c0"), 1)
            eng.memset(onesf[:, :], 1.0)
            eng.memset(zeros[:, :], 0.0)
            eng.memset(len_row[:, :], float(T))
            eng.wait_ge(s("c0"), 2)
            eng.affine_select(out=onehot_b[:, :, :], in_=onehot_b[:, :, :], compare_op=ALU.not_equal, fill=1.0,
                              base=0, pattern=[[1, NB], [-1, NB]], channel_multiplier=0).then_inc(s("onehot"), 1)
            eng.memset(before[:, :], 1.0)
            eng.memset(pick[:, :, :], 0.0)
            eng.iota(iota_e[:, :], pattern=[[1, NE]], base=0, channel_multiplier=0, allow_small_or_imprecise_dtypes=True)
            eng.iota(iota_tile[:, :], pattern=[[T, KP]], base=0, channel_multiplier=0, allow_small_or_imprecise_dtypes=True)
            eng.iota(iota_p[:, :], pattern=[[1, T]], base=0, channel_multiplier=0, allow_small_or_imprecise_dtypes=True)
            eng.iota(part[:, :], pattern=[[0, 1]], base=0, channel_multiplier=1, allow_small_or_imprecise_dtypes=True)
            eng.iota(spare[:, :], pattern=[[T, KP]], base=NTOK, channel_multiplier=1, allow_small_or_imprecise_dtypes=True)
            eng.memset(ohb[:, :, :], 0.0)
            eng.memset(pre[:, :, :], 0.0)
            eng.memset(band[:, :], 0.0).then_inc(s("c0"), 1)
            eng.wait_ge(s("c0"), 3)
            eng.affine_select(out=before[:, :], in_=before[:, :], compare_op=ALU.is_gt, fill=0.0,
                              base=0, pattern=[[1, 128]], channel_multiplier=-1)
            for i in range(PARTS):
                eng.affine_select(out=pick[:, :, :], in_=pick[:, :, :], compare_op=ALU.not_equal, fill=1.0,
                                  base=-i * HU, pattern=[[-1, HU], [0, T]], channel_multiplier=1).then_inc(s("c0"), 1)
                eng.wait_ge(s("c0"), 4 + i)
            eng.tensor_copy(identb[:, :], ident[:, :])
            eng.memset(vpad[:, :, :, :, :], 0.0).then_inc(s("c0"), 1)
            eng.wait_ge(s("c0"), 4 + PARTS)
            eng.memset(vpad[:, :, :, :, HD:HD + 1], 1.0).then_inc(s("consts"), 1)
            eng.wait_ge(s("w1"), 16 * 9)
            eng.wait_ge(s("tg"), 1)
            eng.tensor_scalar(half_gate[:, :], tg[:, 3:4], 0.5, None, ALU.mult).then_inc(s("half_gate"), 1)
            eng.tensor_tensor(b2a[:, :], b2a[:, :], b2b[:, :], ALU.add).then_inc(s("b2pair"), 1)
            eng.wait_ge(s("half_gate"), 1)
            eng.wait_ge(s("b2pair"), 1)
            eng.tensor_scalar(b2a[:, :], b2a[:, :], half_gate[0:NE, :], None, ALU.mult).then_inc(s("b2pair"), 1)
            eng.wait_ge(s("b2pair"), 2)
            eng.dma_start(b2pair_d, b2a[:, :]).then_inc(s("b2pair_d"), 16)
            eng.wait_ge(s("b2pair_d"), 16)
        PO.append(consts)

        def a_stats(eng, c):
            for b in range(NB):
                if b % GB == 0:
                    eng.wait_ge(s(f"x_in{b // GB}"), 16)
                i = stats(eng, slice(b, b + 1))
            c.link(i)
        rstd("a", a_stats)

        def a_weights(eng):
            eng.wait_ge(s("onehot"), 1)
            eng.tensor_tensor(ohr[:, :, :], onehot_b[:, :, :], bc(RSTD, 2, NB), ALU.mult).then_inc(s("ohr"), 1)
        DV.append(a_weights)

        def a_csum(eng):
            for g in range(G):
                eng.wait_ge(s("ctxT"), g + 1)
                i = eng.reduce_sum(sumsT[:, 1, g * GB:(g + 1) * GB], ctxT[:, g * GT:(g + 1) * GT].rearrange("p (b t) -> p b t", t=T), AX)
            i.then_inc(s("csum"), 1)
        DV.append(a_csum)

        def a_pe(eng):
            eng.wait_ge(s("fill"), 1)
            warm(eng, bank[7], WARM[0])
            eng.wait_ge(s("ident"), 1)
            for g in range(G):
                eng.wait_ge(s(f"ctx{g}"), 16)
                if g >= 2:
                    eng.wait_ge(s("ctxT"), g - 1)
                for j in range(GB):
                    i = eng.transpose(bank[g % 2][:, j * T:(j + 1) * T], ctx_s[:, g * GB + j, :], ident[:, :])
                i.then_inc(s("ctxTp"), 1)
            eng.wait_ge(s("ohr"), 1)
            for b in range(NB):
                eng.matmul(bank[4][0:NB, 0:D], ohr[:, b, :], x[:, b, :], start=(b == 0), stop=False)
            i = eng.matmul(bank[4][0:NB, 0:D], NMR, onesf[:, :], start=False, stop=True)
            i.then_inc(s("xsum"), 1)
            eng.wait_ge(s("w0"), 16 * 8)
            eng.matmul(bank[3][:, 0:128], wv0[:, :], wo0[:, :], start=True, stop=True)
            eng.matmul(bank[3][:, 128:256], bv_col[:, 0:1].broadcast_to((128, 128)), wo0[:, :], start=True, stop=False)
            eng.matmul(bank[3][:, 128:256], onesf[0:1, :], bo_row[:, :], start=False, stop=True).then_inc(s("wvop"), 1)
            eng.wait_ge(s("sums"), 1)
            eng.transpose(bank[5][:, 0:NB], sums[:, :], ident[0:NB, 0:NB]).then_inc(s("sumsTp"), 1)
            eng.wait_ge(s("sumsT"), 1)
            eng.wait_ge(s("csum"), 1)
            for j, w in enumerate((wq0, wk0)):
                eng.matmul(bank[6 + j][0:NB, 0:128], sumsT[:, j, :], w[:, :], start=True, stop=False)
                i = eng.matmul(bank[6 + j][0:NB, 0:128], len_row[0:1, 0:NB], bqk[0:1, j, :], start=False, stop=True)
            i.then_inc(s("qksum"), 1)
            eng.wait_ge(s("ctxT"), G)
            eng.wait_ge(s("w1"), 16 * 9)
            eng.wait_ge(s("wvo"), 1)
            for g in range(G):
                i = eng.matmul(bank[g], wk1[:, :], ctxT[:, g * GT:(g + 1) * GT], start=True, stop=True)
                i.then_inc(s("kproj"), 1)
            warm(eng, bank[5], WARM[1])
        PE.append(a_pe)

        def a_act(eng):
            for g in range(G):
                eng.wait_ge(s("ctxTp"), g + 1)
                eng.activation(ctxT[:, g * GT:(g + 1) * GT], bank[g % 2], ACT.Copy).then_inc(s("ctxT"), 1)
            eng.wait_ge(s("xsum"), 1)
            eng.activation(sums[:, :], bank[4][0:NB, 0:D], ACT.Copy).then_inc(s("sums"), 1)
            eng.wait_ge(s("wvop"), 1)
            eng.wait_ge(s("tg"), 1)
            eng.wait_ge(s("w1"), 16 * 9)
            eng.activation(wvo[:, :], bank[3][:, 0:128], ACT.Copy, scale=tg[:, 0:1])
            eng.activation(bvo[:, :], bank[3][:, 128:256], ACT.Copy, scale=tg[:, 0:1]).then_inc(s("wvo"), 1)
            eng.wait_ge(s("sumsTp"), 1)
            eng.activation(sumsT[:, 0, :], bank[5][:, 0:NB], ACT.Copy).then_inc(s("sumsT"), 1)
            eng.activation(wo1[:, :], wo1[:, :], ACT.Copy, scale=tg[:, 1:2])
            for g in range(G):
                if g == 2:
                    eng.wait_ge(s("corr"), 1)
                    eng.activation(sm[:, 3, :], sm[:, 0, :], ACT.Exp, bias=sm[:, 2, 0:1], scale=1.0 / (H * T)).then_inc(s("corre"), 1)
                eng.wait_ge(s("kproj"), g + 1)
                eng.activation(parts[:, g, 0, :], bank[g], ACT.Copy).then_inc(s("k1"), 1)
        AC.append(a_act)

        def a_dve(eng):
            c = chain(eng, "dve")
            eng.wait_ge(s("qksum"), 1)
            c.link(eng.tensor_copy(ks_sb[:, :], bank[7][0:NB, 0:128]))
            c.link(eng.tensor_tensor(prod[:, :], bank[6][0:NB, 0:128], ks_sb[:, :], ALU.mult))
            c.link(eng.reduce_sum(sm[:, 0, :], prod[:, :].rearrange("p (h c) -> p c h", c=HD), AX))
            c.link(eng.reduce_max(sm[:, 1, 0:1], sm[:, 0, :], AX))
            eng.tensor_scalar(sm[:, 2, 0:1], sm[:, 1, 0:1], -1.0 / (H * T), None, ALU.mult).then_inc(s("corr"), 1)
            eng.wait_ge(s("corre"), 1)
            c.link(eng.reduce_sum(sm[:, 4, 0:1], sm[:, 3, :], AX))
            c.link(eng.reciprocal(sm[:, 4, 1:2], sm[:, 4, 0:1]))
            eng.wait_ge(s("consts"), 1)
            eng.tensor_scalar(band[:, T - HD:T], sm[:, 3, :], sm[:, 4, 1:2], None, ALU.mult)
            eng.tensor_scalar(band[:, 2 * T - HD:2 * T - 1], sm[:, 3, 0:HD - 1], sm[:, 4, 1:2], None, ALU.mult).then_inc(s("band"), 1)
        DV.append(a_dve)

        def a_pool(eng):
            eng.wait_ge(s("wvo"), 1)
            eng.wait_ge(s("xsum"), 1)
            eng.tensor_tensor(x[:, :, :], x[:, :, :], bc(bvo[:, :], 1, NB), ALU.add).then_inc(s("xb"), 1)
        PO.append(a_pool)

        def a_sp(eng):
            eng.wait_ge(s("band"), 1)
            eng.dma_start(band_d, band[:, :]).then_inc(s("band_d"), 16)
            eng.wait_ge(s("band_d"), 16)
            src = bass.AP(band_d.tensor, 0, [[1, T], [2 * T, NB], [1, T]])
            for g in range(G):
                eng.dma_start(big[:, g * GB:(g + 1) * GB, :], src[:, g * GB:(g + 1) * GB, :]).then_inc(s(f"C{g}"), 16)
        SP.append(a_sp)

        def k_act(eng):
            for g in range(G):
                eng.wait_ge(s("kr1"), g + 1)
                eng.activation(parts[:, g, 1, :], res[:, g % 2, :], ACT.Copy).then_inc(s("k2"), 1)
        AC.append(k_act)

        def k_dve(eng):
            def rest(g):
                eng.wait_ge(s("k2"), g + 1)
                eng.tensor_tensor(parts[:, g, 2, :], res[:, g % 2, :], parts[:, g, 1, :], ALU.subtract).then_inc(s("kp"), 1)

            for g in range(G):
                if g >= 2:
                    rest(g - 2)
                    eng.wait_ge(s("kp"), g - 1)
                eng.wait_ge(s("k1"), g + 1)
                eng.tensor_tensor(res[:, g % 2, :], bank[g], parts[:, g, 0, :], ALU.subtract).then_inc(s("kr1"), 1)
            rest(G - 2)
            rest(G - 1)
        DV.append(k_dve)

        def k_sp(eng):
            for g in range(G):
                eng.wait_ge(s("kp"), g + 1)
                for i in range(PARTS):
                    eng.dma_start(kstack_d[:, i, :, g * GT:(g + 1) * GT].rearrange("j p t -> p j t"), parts[:, g, :, :]).then_inc(s("kstack_d"), 16)
        SP.append(k_sp)

        def ctxmix_pe(eng):
            def mixed(g):
                eng.wait_ge(s("gt"), g + 1)
                if g >= 2:
                    eng.wait_ge(s("x1"), g - 1)
                for j in range(GB):
                    i = eng.matmul(bank[6 + g % 2][:, j * D:(j + 1) * D], gt[:, g % 2, j * T:(j + 1) * T], wvo[:, :], start=True, stop=True)
                i.then_inc(s("mix"), 1)

            for g in range(G):
                eng.wait_ge(s(f"C{g}"), 16)
                if g >= 2:
                    eng.wait_ge(s("gt"), g - 1)
                for j in range(GB):
                    b = g * GB + j
                    i = eng.matmul(bank[4 + g % 2][:, j * T:(j + 1) * T], ctx_s[:, b, :], big[:, b, :], start=True, stop=True)
                i.then_inc(s("gtp"), 1)
                if g >= 1:
                    mixed(g - 1)
            mixed(G - 1)
        PE.append(ctxmix_pe)

        def ctxmix_act(eng):
            for g in range(G):
                eng.wait_ge(s("gtp"), g + 1)
                if g >= 2:
                    eng.wait_ge(s("mix"), g - 1)
                eng.activation(gt[:, g % 2, :], bank[4 + g % 2], ACT.Copy).then_inc(s("gt"), 1)
        AC.append(ctxmix_act)

        def ctxmix_dve(eng):
            eng.wait_ge(s("xb"), 1)
            for g in range(G):
                eng.wait_ge(s("mix"), g + 1)
                v = x[:, g * GB:(g + 1) * GB, :].rearrange("p b d -> p (b d)")
                eng.tensor_tensor(v, bank[6 + g % 2], v, ALU.add).then_inc(s("x1"), 1)
                eng.wait_ge(s("x1"), g + 1)
                for j in range(GB):
                    i = stats(eng, slice(g * GB + j, g * GB + j + 1))
            chain(eng, "dve").link(i)
        DV.append(ctxmix_dve)

        def emit():
            with nc.Block() as block:
                for deco, steps in ((block.tensor, PE), (block.vector, DV), (block.scalar, AC), (block.sync, SP), (block.gpsimd, PO)):
                    def body(eng, steps=steps):
                        for f in steps:
                            f(eng)
                    deco(body)

        def nearest(eng, c, dst, src):
            c.link(eng.tensor_scalar(dst, src, ROUND, -ROUND, ALU.add, ALU.add))

        def floor_div(eng, c, dst, tmp, src, n, more=0):
            c.link(eng.tensor_scalar(tmp, src, 1.0 / n, (more + 0.5) / n - 0.5, ALU.mult, ALU.add))
            nearest(eng, c, dst, tmp)

        def values():
            def v_pe(eng):
                for g in range(G):
                    eng.wait_ge(s("xbT"), G)
                    if g >= 2:
                        eng.wait_ge(s("v"), g - 1)
                    for j in range(GB):
                        i = eng.matmul(bank[g % 2][:, j * 128:(j + 1) * 128], ctxT[:, g * GT + j * T:g * GT + (j + 1) * T], wv1[:, :],
                                       start=True, stop=True)
                    i.then_inc(s("vproj"), 1)
                eng.wait_ge(s("v"), G)
            PE.append(v_pe)

            def v_act(eng):
                for g in range(G):
                    eng.wait_ge(s("vproj"), g + 1)
                    eng.activation(vals[:, g * GB:(g + 1) * GB, :],
                                   bank[g % 2].rearrange("p (b d) -> p b d", b=GB), ACT.Copy).then_inc(s("v"), 1)
            AC.append(v_act)

        def route(tag, xn_ready, meanwhile=None):
            nth = "bd".index(tag) + 1
            def pe(eng):
                eng.wait_ge(s("oh"), nth)
                eng.matmul(bank[3][:, 0:(NB + 1) * NE], before[:, :], ohb[:, :, :].rearrange("p b e -> p (b e)"), start=True, stop=False)
                for b in range(NB):
                    i = eng.matmul(bank[3][:, (b + 1) * NE:(NB + 1) * NE].rearrange("p (b e) -> p b e", e=NE), onesb[:, :],
                                   bc(ohb[:, b, :], 1, NB - b), start=False, stop=(b == NB - 1))
                i.then_inc(s("rank"), 1)
            PE.append(pe)
            if meanwhile:
                meanwhile()

            def dve(eng):
                c = chain(eng, "dve")
                eng.wait_ge(s("rank"), nth)
                floor_div(eng, c, cnt[:, 0, :], cnt[:, 1, :], bank[3][:, NB * NE:(NB + 1) * NE], T, T - 1)
                c.link(eng.tensor_scalar(pre[:, 0, 4:4 + NE], cnt[:, 0, :], float(T), None, ALU.mult))
                for n, d in enumerate((1, 2, 4)):
                    c.link(eng.tensor_tensor(pre[:, n + 1, 4:4 + NE], pre[:, n, 4:4 + NE], pre[:, n, 4 - d:4 + NE - d], ALU.add))
                c.link(eng.tensor_tensor(cnt[:, 2, :], pre[:, 3, 4:4 + NE], pre[:, 0, 4:4 + NE], ALU.subtract))
                c.link(eng.tensor_tensor(lw[:, 0, :, :], bank[3][:, 0:NB * NE].rearrange("p (b e) -> p b e", e=NE),
                                         bc(cnt[:, 2, :], 1, NB), ALU.add))
                c.link(eng.tensor_tensor(lw[:, 1, :, :], lw[:, 0, :, :], oh[:, :, :], ALU.mult))
                c.link(eng.reduce_sum(r16[:, 0, :], lw[:, 1, :, :], AX))
                slot, q, tile, place = (r16[:, k, :] for k in (0, 6, 7, 3))
                floor_div(eng, c, tile, q, slot, T)
                eng.tensor_tensor(ohk[:, :, 0, :], bc(iota_p[:, 0:KP], 1, NB), bc(tile, 2, KP), ALU.is_equal).then_inc(s("tile"), 1)
                c.link(eng.scalar_tensor_tensor(place, tile, -float(T), slot, ALU.mult, ALU.add))
                for half in (slice(0, NB // 2), slice(NB // 2, NB)):
                    eng.tensor_tensor(ohp[:, half, :], bc(iota_p[:, :], 1, NB // 2), bc(place[:, half], 2, T), ALU.is_equal).then_inc(s("hot"), 1)
                c.link(eng.tensor_tensor(te_f[:, :, :], bc(pre[0:1, 3, 4:4 + NE], 1, KP), bc(iota_tile[:, :], 2, NE), ALU.is_le))
                c.link(eng.reduce_sum(te_r[:, 0, :], te_f[:, :, :], AX))
                c.link(eng.tensor_scalar(te_r[:, 1, :], te_r[:, 0, :], float(NE - 1), None, ALU.min))
                eng.wait_ge(s("inv"), nth)
                c.link(eng.tensor_copy(inv[:, 0:3, :], bank[4][:, 0:3 * KP].rearrange("p (a k) -> p a k", a=3)))
                c.link(eng.scalar_tensor_tensor(inv[:, 3, :], inv[:, 2, :], float(T), inv[:, 1, :], ALU.mult, ALU.add))
                eng.tensor_copy(inv_i[:, 0, :], inv[:, 3, :]).then_inc(s("gather"), 1)
                c.link(eng.tensor_scalar(te_r[:, 0, :], te_r[:, 1, :], float(NE - 1), -float(NE), ALU.is_ge, ALU.mult))
                c.link(eng.scalar_tensor_tensor(te_r[:, 2, :], te_r[:, 1, :], 1.0, te_r[:, 0, :], ALU.add, ALU.add))
                eng.tensor_copy(te_i[:, 0, :], te_r[:, 1, :])
                eng.tensor_copy(te_i[:, 1, :], te_r[:, 2, :]).then_inc(s("te"), 1)
                c.link(eng.tensor_scalar(inv[:, 1, :], inv[:, 0, :], -1.0, 1.0, ALU.mult, ALU.add))
                c.link(eng.tensor_tensor(inv[:, 2, :], inv[:, 1, :], spare[:, :], ALU.mult))
                eng.tensor_tensor(inv_i[:, 1, :], inv[:, 3, :], inv[:, 2, :], ALU.add).then_inc(s("scatter"), 1)
            DV.append(dve)

            def pool(eng):
                eng.wait_ge(s("tile"), nth)
                eng.tensor_tensor(ohk[:, :, 1, :], ohk[:, :, 0, :], bc(part[:, 0:1].broadcast_to((128, KP)), 1, NB), ALU.mult)
                eng.tensor_tensor(ohk[:, :, 2, :], ohk[:, :, 0, :], bc(iota_p[:, 0:NB], 2, KP), ALU.mult).then_inc(s("hotk"), 1)
            PO.append(pool)

            def pe2(eng):
                eng.wait_ge(s("hotk"), nth)
                for b in range(NB):
                    if b % (NB // 2) == 0:
                        eng.wait_ge(s("hot"), 2 * nth - 1 + b // (NB // 2))
                    i = eng.matmul(bank[4][:, 0:3 * KP], ohp[:, b, :], ohk[:, b, :, :].rearrange("p a k -> p (a k)"),
                                   start=(b == 0), stop=(b == NB - 1))
                i.then_inc(s("inv"), 1)
                warm(eng, bank[5], WARM[3])
            PE.append(pe2)

            def sp(eng):
                v = rows_d[tag].rearrange("(b t) d -> t b d", t=T)
                for g in range(G):
                    xn_ready(eng, g)
                    eng.dma_start(v[:, g * GB:(g + 1) * GB, :], xn[:, g * GB:(g + 1) * GB, :]).then_inc(s("rows_" + tag), 16)
            SP.append(sp)

        class Tile:

            def __init__(self, j, k):
                self.j, self.at = j, k
                self.k, self.r, self.turn = Lin(j, R, k), k % R, Lin(j, 1, k // R)
                self.first, self.last = (j is None and k == n for n in (0, K - 1))
                self.bank = k % 2

            def plus(self, d):
                return Tile(self.j, self.at + d)

        PEEL = R + 1
        TURNS = (K - PEEL) // R

        def tiles(step):
            def run(eng):
                for k in range(PEEL):
                    step(eng, Tile(None, k))
                with eng.Fori(0, TURNS) as j:
                    for k in range(PEEL, PEEL + R):
                        step(eng, Tile(j, k))
                for k in range(PEEL + TURNS * R, K):
                    step(eng, Tile(None, k))
            return run

        rstd("b", lambda eng, c: None)
        ready_b = normalise("b", "DDDA")

        def b_pe(eng):
            warm(eng, bank[2], WARM[2])

            def logits(g):
                eng.wait_ge(s("xbT"), g + 1)
                for b in range(g * GB, (g + 1) * GB):
                    i = eng.matmul(bank[6][:, b * NE:(b + 1) * NE], big[:, b, :], rw[:, :], start=True, stop=True)
                return i

            for g in range(G):
                ready_b(eng, g)
                if g >= 2:
                    eng.wait_ge(s("xbT"), g - 1)
                for j in range(GB):
                    i = eng.transpose(bank[g % 2][:, j * T:(j + 1) * T], xn[:, g * GB + j, :], ident[:, :])
                i.then_inc(s("xbTp"), 1)
                if g >= 1:
                    logits(g - 1)
            logits(G - 1).then_inc(s("logit"), 1)
        PE.append(b_pe)

        def b_act(eng):
            for g in range(G):
                eng.wait_ge(s("xbTp"), g + 1)
                eng.wait_ge(s("gtp"), G)
                eng.activation(big[:, g * GB:(g + 1) * GB, :], bank[g % 2].rearrange("p (b t) -> p b t", b=GB), ACT.Copy)\
                   .then_inc(s("xbT"), 1)
            eng.wait_ge(s("shifted"), 1)
            eng.activation(lw[:, 1, :, :], lw[:, 0, :, :], ACT.Exp).then_inc(s("lexp"), 1)
        AC.append(b_act)

        def b_dve(eng):
            c = chain(eng, "dve")
            eng.wait_ge(s("logit"), 1)
            c.link(eng.tensor_tensor(logit[:, :, :], bank[6][:, 0:NB * NE].rearrange("p (b e) -> p b e", e=NE), bc(rb[:, :], 1, NB), ALU.add))
            c.link(eng.reduce_max(r16[:, 1, :], logit[:, :, :], AX))
            eng.tensor_tensor(lw[:, 0, :, :], logit[:, :, :], bc(r16[:, 1, :], 2, NE), ALU.subtract).then_inc(s("shifted"), 1)
            eng.wait_ge(s("consts"), 1)
            c.link(eng.tensor_tensor(oh[:, :, :], logit[:, :, :], bc(r16[:, 1, :], 2, NE), ALU.is_equal))
            c.link(eng.scalar_tensor_tensor(lw[:, 2, :, :], oh[:, :, :], -float(NE), bc(iota_e[:, :], 1, NB), ALU.mult, ALU.add))
            c.link(eng.tensor_reduce(r16[:, 2, :], lw[:, 2, :, :], AX, ALU.min))
            c.link(eng.tensor_scalar(r16[:, 3, :], r16[:, 2, :], float(NE), None, ALU.add))
            eng.tensor_tensor(ohb[:, 0:NB, :], bc(iota_e[:, :], 1, NB), bc(r16[:, 3, :], 2, NE), ALU.is_equal).then_inc(s("oh"), 1)
            c.link(eng.tensor_tensor(oh[:, :, :], bc(iota_e[:, :], 1, NB), bc(r16[:, 3, :], 2, NE), ALU.is_equal))
            eng.wait_ge(s("lexp"), 1)
            c.link(eng.reduce_sum(r16[:, 4, :], lw[:, 1, :, :], AX))
            c.link(eng.reciprocal(r16[:, 5, :], r16[:, 4, :]))
            eng.tensor_scalar(maxp[:, :], r16[:, 5, :], tg[:, 2:3], None, ALU.mult).then_inc(s("maxp"), 1)
        DV.append(b_dve)
        route("b", ready_b, values)

        def experts(tag, wts, steps):
            gated = steps == 1
            nth = "bd".index(tag) + 1
            CH = C0 if gated else C1
            UP = 2 * F0 if gated else F1
            WD = W0 if gated else W1
            n = {k: s(f"{k}_{tag}") for k in ("xTp", "xT", "h", "half", "act", "yp", "y")}
            xt_in, w_in, y_out = ([s(f"{k}_{tag}{i}") for i in range(R)] for k in ("xt_in", "w_in", "y_out"))
            b2_in = [s(f"b2_in{i}") for i in range(R)]

            def ring(t, j):
                if gated:
                    return t.k, t.r, t.turn
                return t.k * 2 + j, (2 * t.r + j) % R, Lin(t.j, 2, (2 * t.at + j) // R)

            def weights(eng, t):
                for j in range(steps):
                    q, slot, use = ring(t, j)
                    e = eng.value_load(te_i[0:1, j, ds(t.k.value(), 1)], min_val=0, max_val=NE - 1)
                    wait(eng, n["yp"], q - R + 1)
                    eng.dma_start(wring[:, slot, 0:WD], wts[ds(e, 1)].rearrange("a p w -> (a p) w")).then_inc(w_in[slot], 16)
                    if not gated and j == 0:
                        wait(eng, n["y"], t.k - R + 1)
                        eng.dma_start(b2r[:, t.r, :], b2pair_d[ds(e, 1), :].broadcast_to((128, D))).then_inc(b2_in[t.r], 16)

            def sp(eng):
                eng.wait_ge(s("te"), nth)
                if not gated:
                    eng.wait_ge(s("b2pair_d"), 16)
                tiles(weights)(eng)
            SP.append(sp)

            def turn_over(eng, t):
                wait(eng, n["xT"], t.k)
                wait(eng, xt_in[t.r], (t.turn + 1) * 16)
                eng.transpose(bank[0][:, 0:T], xt[:, t.r, :], ident[:, :]).then_inc(n["xTp"], 1)

            def up(eng, t, j):
                q, slot, use = ring(t, j)
                hb = t.bank if gated else j
                if j == 0:
                    wait(eng, n["xT"], t.k + 1)
                wait(eng, n["act"], q - 1)
                if not gated:
                    wait(eng, n["half"], q - 1)
                wait(eng, w_in[slot], (use + 1) * 16)
                P = (pairA, pairB)[hb]
                for f in range(UP // 128):
                    g_, o = divmod(f, UP // 256)
                    i = eng.matmul(P[:, g_, o * T:(o + 1) * T], wring[:, slot, f * 128:(f + 1) * 128], xtT[:, t.bank, :],
                                   start=True, stop=True)
                i.then_inc(n["h"], 1)

            def down(eng, t, j):
                q, slot, use = ring(t, j)
                hb = t.bank if gated else j
                wait(eng, n["act"], q + 1)
                if not gated:
                    wait(eng, n["half"], q + 1)
                if j == 0:
                    wait(eng, n["y"], t.k - 1)
                for c_ in range(CH):
                    o = WD - CH * D + c_ * D
                    i = eng.matmul(bank[1 + t.bank][:, 0:D], act[:, hb, c_, :], wring[:, slot, o:o + D],
                                   start=(j == 0 and c_ == 0), stop=(j == steps - 1 and c_ == CH - 1))
                i.then_inc(n["yp"], 1)

            def pe_step(eng, t):
                if t.first:
                    turn_over(eng, t)
                up(eng, t, 0)
                if not t.last:
                    turn_over(eng, t.plus(1))
                if not t.first:
                    down(eng, t.plus(-1), steps - 1)
                if steps == 2:
                    up(eng, t, 1)
                    down(eng, t, 0)
                if t.last:
                    down(eng, t, steps - 1)
            PE.append(tiles(pe_step))

            def act_step(eng, t):
                for j in range(steps):
                    q, slot, use = ring(t, j)
                    hb = t.bank if gated else j
                    P = (pairA, pairB)[hb]
                    wait(eng, n["h"], q + 1)
                    if gated:
                        wait(eng, n["act"], q - 1)
                        eng.activation(sil[:, hb, :], P[:, 0, :], ACT.Silu).then_inc(n["half"], 1)
                    else:
                        wait(eng, n["yp"], q - 1)
                        wait(eng, w_in[slot], (use + 1) * 16)
                        for c_ in range(CH // 2):
                            i = eng.activation(act[:, hb, c_, :], P[:, 0, c_ * T:(c_ + 1) * T], ACT.Relu,
                                               bias=wring[:, slot, UP + c_:UP + c_ + 1])
                        i.then_inc(n["half"], 1)
                    if gated and not t.first:
                        y_copy(eng, t.plus(-1))
                if gated and t.last:
                    y_copy(eng, t)

            def y_copy(eng, t):
                wait(eng, n["yp"], (t.k + 1) * steps)
                wait(eng, y_out[t.r], t.turn * 16)
                eng.activation(ysb[:, t.r, :], bank[1 + t.bank][:, 0:D], ACT.Copy).then_inc(n["y"], 1)
            AC.append(tiles(act_step))

            def y_add(eng, t):
                wait(eng, n["yp"], (t.k + 1) * steps)
                wait(eng, b2_in[t.r], (t.turn + 1) * 16)
                wait(eng, y_out[t.r], t.turn * 16)
                eng.scalar_tensor_tensor(ysb[:, t.r, :], bank[1 + t.bank][:, 0:D], half_gate[:, 0:1], b2r[:, t.r, :], ALU.mult, ALU.add)\
                   .then_inc(n["y"], 1)

            def xT(eng, t):
                wait(eng, n["xTp"], t.k + 1)
                wait(eng, n["h"], (t.k - 1) * steps)
                eng.tensor_copy(xtT[:, t.bank, :], bank[0][:, 0:T]).then_inc(n["xT"], 1)

            def dve_step(eng, t):
                if t.first:
                    xT(eng, t)
                for j in range(steps):
                    q, slot, use = ring(t, j)
                    hb = t.bank if gated else j
                    P = (pairA, pairB)[hb]
                    if gated:
                        if not t.last:
                            xT(eng, t.plus(1))
                        wait(eng, n["half"], q + 1)
                        wait(eng, n["yp"], q - 1)
                        eng.tensor_tensor(act[:, hb, :, :].rearrange("p c t -> p (c t)"), P[:, 1, :], sil[:, hb, :], ALU.mult)\
                           .then_inc(n["act"], 1)
                    else:
                        wait(eng, n["h"], q + 1)
                        wait(eng, n["yp"], q - 1)
                        wait(eng, w_in[slot], (use + 1) * 16)
                        for c_ in range(CH // 2, CH):
                            o = c_ - CH // 2
                            i = eng.tensor_scalar(act[:, hb, c_, :], P[:, 1, o * T:(o + 1) * T],
                                                  wring[:, slot, UP + c_:UP + c_ + 1], 0.0, ALU.add, ALU.max)
                        i.then_inc(n["act"], 1)
                        if j == 0:
                            if not t.last:
                                xT(eng, t.plus(1))
                            if not t.first:
                                y_add(eng, t.plus(-1))
                if not gated and t.last:
                    y_add(eng, t)
            DV.append(tiles(dve_step))

            AHEAD = R

            def gather(eng, t):
                wait(eng, n["xTp"], t.k - R + 1)
                eng.indirect_dma_start(out=xt[:, t.r, :], out_offset=None, in_=rows_d[tag],
                                       in_offset=bass.IndirectOffsetOnAxis(ap=inv_i[:, 0, t.at:t.at + 1], axis=0)).then_inc(xt_in[t.r], 16)

            def scatter(eng, t):
                wait(eng, n["y"], t.k + 1)
                eng.indirect_dma_start(out=back_d[tag], out_offset=bass.IndirectOffsetOnAxis(ap=inv_i[:, 1, t.at:t.at + 1], axis=0),
                                       in_=ysb[:, t.r, :], in_offset=None).then_inc(y_out[t.r], 16)

            def pool(eng):
                eng.wait_ge(s("gather"), nth)
                eng.wait_ge(s("rows_" + tag), 16 * G)
                every = [Tile(None, k) for k in range(K)]
                for t in every[:AHEAD]:
                    gather(eng, t)
                eng.wait_ge(s("scatter"), nth)
                for t in every:
                    if t.at + AHEAD < K:
                        gather(eng, every[t.at + AHEAD])
                    scatter(eng, t)
            PO.append(pool)

            def sp_back(eng):
                for r in range(R):
                    eng.wait_ge(y_out[r], 16 * ((K - r + R - 1) // R))
                v = back_d[tag][0:NTOK, :].rearrange("(b t) d -> t b d", t=T)
                for g in range(G):
                    eng.dma_start(ctx_s[:, g * GB:(g + 1) * GB, :], v[:, g * GB:(g + 1) * GB, :]).then_inc(s(f"back{g}"), 16)
            SP.append(sp_back)

        experts("b", A["wts0"], 1)

        def b_pool(eng):
            c = chain(eng, "pool")
            eng.wait_ge(s("maxp"), 1)
            for g in range(G):
                eng.wait_ge(s(f"back{g}"), 16)
                mine = slice(g * GB + BY_POOL[0], g * GB + BY_POOL[-1] + 1)
                got = ctx_s[:, mine, :]
                c.link(eng.tensor_tensor(got, got, bc(maxp[:, mine], 2, D), ALU.mult))
                eng.tensor_tensor(x[:, mine, :], x[:, mine, :], got, ALU.add).then_inc(s("x2P"), 1)
        PO.append(b_pool)

        def b_dve2(eng):
            for g in range(G):
                eng.wait_ge(s(f"back{g}"), 16)
                for b in (g * GB + j for j in BY_DVE):
                    i = eng.scalar_tensor_tensor(x[:, b, :], ctx_s[:, b, :], maxp[:, b:b + 1], x[:, b, :], ALU.mult, ALU.add)
                i.then_inc(s("x2D"), 1)
                eng.wait_ge(s("x2D"), g + 1)
                eng.wait_ge(s("x2P"), g + 1)
                for j in range(GB):
                    i = stats(eng, slice(g * GB + j, g * GB + j + 1))
            chain(eng, "dve").link(i)
        DV.append(b_dve2)

        rstd("c", lambda eng, c: None)
        ready_c = normalise("c", "DDDA")

        def q_pe(eng):
            eng.wait_ge(s("back0"), 16)
            warm(eng, bank[7], WARM[4])

            def product(g):
                eng.wait_ge(s("xcT"), g + 1)
                if g >= 2:
                    eng.wait_ge(s("qr1"), g - 1)
                eng.matmul(bank[2 + g % 2], wq1[:, :], big[:, g * GB:(g + 1) * GB, :].rearrange("p b t -> p (b t)"), start=True, stop=True)\
                   .then_inc(s("qproj"), 1)

            for g in range(G):
                ready_c(eng, g)
                if g >= 2:
                    eng.wait_ge(s("xcT"), g - 1)
                for j in range(GB):
                    i = eng.transpose(bank[g % 2][:, j * T:(j + 1) * T], xn[:, g * GB + j, :], ident[:, :])
                i.then_inc(s("xcTp"), 1)
                if g >= 1:
                    product(g - 1)
            product(G - 1)
            warm(eng, bank[7], WARM[5])
        PE.append(q_pe)

        QS = HD ** -0.5

        def q_act(eng):
            for g in range(G + 2):
                if g < G:
                    eng.wait_ge(s("xcTp"), g + 1)
                    eng.activation(big[:, g * GB:(g + 1) * GB, :].rearrange("p b t -> p (b t)"), bank[g % 2], ACT.Copy).then_inc(s("xcT"), 1)
                if 1 <= g < G + 1:
                    eng.wait_ge(s("qproj"), g)
                    eng.activation(parts[:, g - 1, 0, :], bank[2 + (g - 1) % 2], ACT.Copy, scale=QS).then_inc(s("q1"), 1)
                if 1 <= g - 1:
                    eng.wait_ge(s("qr1"), g - 1)
                    eng.activation(parts[:, g - 2, 1, :], res[:, g % 2, :], ACT.Copy).then_inc(s("q2"), 1)
        AC.append(q_act)

        def q_dve(eng):
            def rest(g):
                eng.wait_ge(s("q2"), g + 1)
                eng.tensor_tensor(parts[:, g, 2, :], res[:, g % 2, :], parts[:, g, 1, :], ALU.subtract).then_inc(s("qp"), 1)

            for g in range(G):
                if g >= 2:
                    rest(g - 2)
                    eng.wait_ge(s("qp"), g - 1)
                eng.wait_ge(s("q1"), g + 1)
                eng.scalar_tensor_tensor(res[:, g % 2, :], bank[2 + g % 2], QS, parts[:, g, 0, :], ALU.mult, ALU.subtract).then_inc(s("qr1"), 1)
            rest(G - 2)
            rest(G - 1)
        DV.append(q_dve)

        BODY = 2 * GB
        LAG = 9

        class At:

            def __init__(self, j, turn, r):
                self.j, self.turn, self.r = j, Lin(j, 1, turn), r
                self.lo = BODY * turn + r

            def on(self, k):
                return self.j is not None or 0 <= self.lo - k < NU

            def unit(self, k):
                return Lin(self.j, BODY, self.lo - k)

            def batch(self, k):
                return Lin(self.j, BODY // 2, (self.lo - k) // 2)

            def half(self, k):
                return (self.r - k) % 2

            def pair(self, k):
                return ((self.r - k) // 2) % 2

        def units(step):
            def run(eng):
                for r in range(BODY):
                    step(eng, At(None, 0, r))
                with eng.Fori(0, NU // BODY - 1) as j:
                    for r in range(BODY):
                        step(eng, At(j, 1, r))
                for r in range(LAG + 1):
                    step(eng, At(None, NU // BODY, r))
            return run

        def c_sp(eng):
            def write(g):
                eng.wait_ge(s("qp"), g + 1)
                eng.dma_start(qparts_d[:, :, g * GT:(g + 1) * GT].rearrange("i p t -> p i t"), parts[:, g, :, :]).then_inc(s(f"qparts{g}"), 16)

            def load_keys(pair):
                v = kstack_d.rearrange("j i (d h) t -> (j i d) h t", h=H)
                eng.dma_start(ks[:, pair % 2, :, :], v[:, :, pair * 2 * T:(pair + 1) * 2 * T]).then_inc(s(f"qk{pair % 2}"), 16)

            def load_queries(pair):
                v = qparts_d.rearrange("i (d h) t -> (i d) h t", h=H)[:, :, pair * 2 * T:(pair + 1) * 2 * T]
                for j in range(PARTS):
                    eng.dma_start(qs[j * PARTS * HD:(j + 1) * PARTS * HD, pair % 2, :, :], v).then_inc(s(f"qk{pair % 2}"), 16)

            eng.wait_ge(s("kstack_d"), 16 * PARTS * G)
            load_keys(0)
            load_keys(1)
            write(0)
            eng.wait_ge(s("qparts0"), 16)
            load_queries(0)
            write(1)
            load_queries(1)
            write(2)
            write(3)
            for pair in range(2, NB // 2):
                if pair % 2 == 0:
                    eng.wait_ge(s(f"qparts{pair // 2}"), 16)
                wait(eng, s("ST"), (pair - 1) * 4)
                load_keys(pair)
                load_queries(pair)
        SP.append(c_sp)

        def c_pe(eng):
            eng.wait_ge(s("qr1"), G)
            def heads(r):
                slot, off, u = (r // 4) % 2, ((r // 2) % 2) * T, r % 2
                return [(h, qs[:, slot, u * HU + h, off:off + T], ks[:, slot, u * HU + h, off:off + T]) for h in range(HU)]

            def step(eng, at):
                if at.on(0):
                    if at.r % 4 == 0:
                        wait(eng, s(f"qk{at.r // 4}"), (at.turn + 1) * (16 * (PARTS + 1)))
                    wait(eng, s("mx"), at.unit(0))
                    for h, q_, k_ in heads(at.r):
                        i = eng.matmul(pairA[:, h // 4, (h % 4) * T:(h % 4 + 1) * T], q_, k_, start=True, stop=True)
                    i.then_inc(s("S"), 1)
                    if at.j is None and at.lo < 4:
                        warm(eng, bank[2], WARM[6])
                if at.on(2):
                    wait(eng, s("mrow"), at.unit(1))
                    wait(eng, s("P"), at.unit(2))
                    for h, q_, k_ in heads((at.r - 2) % BODY):
                        o = pairB[:, h // 4, (h % 4) * T:(h % 4 + 1) * T]
                        eng.matmul(o, k_, q_, start=True, stop=False)
                        i = eng.matmul(o, pick[:, h, :], mrow[:, at.half(2), :], start=False, stop=True)
                    i.then_inc(s("ST"), 1)
                if at.on(1):
                    wait(eng, s("mparts"), at.unit(0))
                    wait(eng, s("mrow"), at.unit(1))
                    eng.transpose(mTp, mparts[:, at.half(1), :, :].rearrange("p i h -> p (i h)"), identb[:, :]).then_inc(s("mT"), 1)
                if at.on(3):
                    u = at.half(3)
                    wait(eng, s("P"), at.unit(2))
                    if u == 0:
                        wait(eng, s("osb"), at.batch(3))
                        wait(eng, s("vp"), at.batch(1))
                    for odd in range(2):
                        for p in range(HU // 2):
                            v = vpad[:, at.pair(3), u * (HU // 2) + p, :, :].rearrange("p o w -> p (o w)")
                            i = eng.matmul(bank[1][32 * p:32 * p + 32, u * T:(u + 1) * T], v[:, 32 * odd:32 * odd + 32],
                                           prob[:, at.half(3), 2 * p + odd, :], start=(odd == 0), stop=(odd == 1),
                                           tile_position=(0, 32 * p))
                    i.then_inc(s("O"), 1)
                if at.r % 2 == 0 and at.on(6):
                    wait(eng, s("osb"), at.batch(4))
                    wait(eng, s("an"), at.batch(6))
                    for j in range(2):
                        i = eng.transpose(bank[2][:, j * 128:(j + 1) * 128], osb[:, j * 128:(j + 1) * 128], ident[:, :])
                    i.then_inc(s("oT"), 1)
                if at.r % 2 == 1 and at.on(7):
                    wait(eng, s("an"), at.batch(5))
                    wait(eng, s("x3"), at.batch(7))
                    eng.transpose(bank[3][:, 0:T], an[:, :], ident[:, :]).then_inc(s("anTp"), 1)
                if at.r % 2 == 0 and at.on(8):
                    wait(eng, s("anT"), at.batch(6))
                    eng.matmul(bank[3][:, T:T + D], anT[:, :], wo1[:, :], start=True, stop=True).then_inc(s("proj"), 1)
            units(step)(eng)
        PE.append(c_pe)

        def c_act(eng):
            def step(eng, at):
                if at.r % 2 == 1 and at.on(5):
                    wait(eng, s("O"), at.unit(3))
                    wait(eng, s("oT"), at.batch(5))
                    eng.activation(osb[:, :], bank[1][:, 0:2 * T], ACT.Copy).then_inc(s("osb"), 1)
                if at.on(2):
                    wait(eng, s("ST"), at.unit(1))
                    wait(eng, s("O"), at.unit(3))
                    eng.activation(prob[:, at.half(2), :, :].rearrange("p h t -> p (h t)"), pairB[:, :, :].rearrange("p a t -> p (a t)"), ACT.Exp)\
                       .then_inc(s("P"), 1)
                if at.on(1):
                    wait(eng, s("mT"), at.unit(0))
                    wait(eng, s("ST"), at.unit(2))
                    eng.activation(mrow[:, at.half(1), :], mTp, ACT.Copy).then_inc(s("mrow"), 1)
                if at.r % 2 == 1 and at.on(7):
                    wait(eng, s("anTp"), at.batch(5))
                    wait(eng, s("proj"), at.batch(7))
                    eng.activation(anT[:, :], bank[3][:, 0:T], ACT.Copy).then_inc(s("anT"), 1)
            units(step)(eng)
        AC.append(c_act)

        def c_dve(eng):
            def step(eng, at):
                if at.on(0):
                    wait(eng, s("S"), at.unit(0) + 1)
                    wait(eng, s("mparts"), at.unit(1))
                    eng.reduce_max(maxi[:, at.half(0), :], pairA[:, :, :].rearrange("p a (h t) -> p (a h) t", t=T), AX).then_inc(s("mx"), 1)
                if at.r % 2 == 0 and at.on(6):
                    wait(eng, s("oT"), at.batch(4))
                    wait(eng, s("anTp"), at.batch(6))
                    v = bank[2][:, 0:H * VW].rearrange("p (h c) -> p h c", c=VW)
                    eng.reciprocal(rl[:, :], v[:, :, HD]).then_inc(s("rl"), 1)
                    wait(eng, s("rl"), at.batch(4))
                    eng.tensor_tensor(an[:, :].rearrange("p (h c) -> p h c", c=HD), v[:, :, 0:HD], bc(rl[:, :], 2, HD), ALU.mult)\
                       .then_inc(s("an"), 1)
                if at.r % 2 == 0 and at.on(8):
                    wait(eng, s("proj"), at.batch(6))
                    xb = x[:, ds(at.batch(8).value(), 1), :].rearrange("p a d -> p (a d)")
                    eng.tensor_tensor(xb, bank[3][:, T:T + D], xb, ALU.add).then_inc(s("x3"), 1)
                if at.r % 2 == 1 and at.on(9):
                    wait(eng, s("x3"), at.batch(9) + 1)
                    stats(eng, ds(at.batch(9).value(), 1)).then_inc(s("st_d"), 1)
            units(step)(eng)
        DV.append(c_dve)

        def c_pool(eng):
            c = chain(eng, "pool")
            eng.wait_ge(s("v"), G)

            def step(eng, at):
                if at.on(0):
                    wait(eng, s("mx"), at.unit(0) + 1)
                    wait(eng, s("mT"), at.unit(1))
                    m, rest, mp = maxi[:, at.half(0), :], mrest[:, at.half(0), :], mparts[:, at.half(0), :, :]
                    eng.tensor_tensor(mp[:, 0, :], zeros[:, :], m, ALU.subtract)
                    c.link(eng.tensor_tensor(rest, zeros[:, :], m, ALU.subtract))
                    c.link(eng.tensor_tensor(rest, rest, mp[:, 0, :], ALU.subtract))
                    c.link(eng.tensor_tensor(mp[:, 1, :], rest, zeros[:, :], ALU.subtract))
                    eng.tensor_tensor(mp[:, 2, :], rest, mp[:, 1, :], ALU.subtract).then_inc(s("mparts"), 1)
                if at.r % 2 == 1 and at.on(1):
                    b = at.batch(1)
                    wait(eng, s("O"), (b - 1) * 2)
                    eng.tensor_copy(vpad[:, at.pair(1), :, :, 0:HD].rearrange("p q o d -> p (q o) d"),
                                    vals[:, ds(b.value(), 1), :].rearrange("p a (h d) -> p (a h) d", h=H))\
                       .then_inc(s("vp"), 1)

            for r in range(BODY):
                step(eng, At(None, 0, r))
            with eng.Fori(0, G - 1) as j:
                c.enter(j, 3 * BODY)
                for r in range(BODY):
                    step(eng, At(j, 1, r))
            c.leave(G - 1)
            step(eng, At(None, NU // BODY, 0))
        PO.append(c_pool)

        rstd("d", lambda eng, c: eng.wait_ge(s("st_d"), NB))
        ready_d = normalise("d", "AAAP")

        def d_dve(eng):
            c = chain(eng, "dve")
            a_, b_, c_, d_, e_, up = (r16[:, k, :] for k in range(6))
            first = ohr[:, :, 0:2]
            c.link(eng.tensor_tensor(first, x[:, :, 0:2], bc(MEAN, 2, 2), ALU.subtract))
            c.link(eng.tensor_tensor(first, first, bc(RSTD, 2, 2), ALU.mult))
            c.link(eng.tensor_tensor(a_, first[:, :, 0], first[:, :, 1], ALU.add))
            eng.tensor_scalar(d_, a_, 0.0, 2.0, ALU.is_ge, ALU.mult)
            c.link(eng.scalar_tensor_tensor(b_, a_, -1.0, a_, ALU.mult, ALU.max))
            nearest(eng, c, c_, b_)
            c.link(eng.tensor_tensor(up, c_, b_, ALU.is_gt))
            c.link(eng.tensor_tensor(c_, c_, up, ALU.subtract))
            c.link(eng.scalar_tensor_tensor(e_, d_, -1.0, c_, ALU.add, ALU.mult))
            floor_div(eng, c, c_, b_, e_, NE)
            c.link(eng.scalar_tensor_tensor(d_, c_, -float(NE), e_, ALU.mult, ALU.add))
            eng.tensor_tensor(ohb[:, 0:NB, :], bc(iota_e[:, :], 1, NB), bc(d_, 2, NE), ALU.is_equal).then_inc(s("oh"), 1)
            c.link(eng.tensor_tensor(oh[:, :, :], bc(iota_e[:, :], 1, NB), bc(d_, 2, NE), ALU.is_equal))
        DV.append(d_dve)
        route("d", ready_d)
        experts("d", A["wts1"], 2)

        def d_add(eng):
            for g in range(G):
                eng.wait_ge(s(f"back{g}"), 32)
                mine = slice(g * GB, (g + 1) * GB)
                eng.tensor_tensor(x[:, mine, :], x[:, mine, :], ctx_s[:, mine, :], ALU.add).then_inc(s("x4"), 1)
        DV.append(d_add)

        def d_out(eng):
            o = out.rearrange("b t d -> t b d")
            for g in range(G):
                eng.wait_ge(s("x4"), g + 1)
                eng.dma_start(o[:, g * GB:(g + 1) * GB, :], x[:, g * GB:(g + 1) * GB, :]).then_inc(s("out"), 16)
            eng.wait_ge(s("out"), 16 * G)
        SP.append(d_out)
        emit()


_OUT = (16, 128, 128)


def kernel(x, ctx_1024, g_xattn, g_ffn, L0_xattn_Wq, L0_xattn_bq, L0_xattn_Wk, L0_xattn_bk, L0_xattn_Wv, L0_xattn_bv,
           L0_xattn_Wo, L0_xattn_bo, L0_ffn_router_w, L0_ffn_router_b, L0_ffn_w1, L0_ffn_w2, L1_xattn_w_q, L1_xattn_w_k,
           L1_xattn_w_v, L1_xattn_w_o, L1_ffn_W1, L1_ffn_b1, L1_ffn_W2, L1_ffn_b2):
    import concourse.bacc as bacc
    from concourse.bass_utils import run_bass_kernel_spmd

    def rev(w):
        return w.reshape(*w.shape[:-1], 16, 8)[..., ::-1].reshape(w.shape)

    def dh(w):
        return w.reshape(128, 16, 8).transpose(0, 2, 1).reshape(128, 128)

    def rows(w):
        return w.reshape(8, -1, 128, 128).transpose(0, 2, 1, 3).reshape(8, 128, -1)

    a = {k: np.asarray(v) for k, v in locals().items() if not callable(v) and hasattr(v, "shape")}
    arrays = {
        "x": a["x"], "ctx": a["ctx_1024"][:, ::-1, :],
        "gates": np.concatenate([a["g_xattn"], a["g_ffn"]]).reshape(1, 4),
        "wq0": rev(a["L0_xattn_Wq"].T), "wk0": rev(a["L0_xattn_Wk"].T), "wv0": a["L0_xattn_Wv"], "wo0": a["L0_xattn_Wo"].T,
        "bq": rev(a["L0_xattn_bq"]).reshape(1, 128), "bk": rev(a["L0_xattn_bk"]).reshape(1, 128),
        "bv": a["L0_xattn_bv"].reshape(128, 1), "bo": a["L0_xattn_bo"].reshape(1, 128),
        "rw": a["L0_ffn_router_w"], "rb": a["L0_ffn_router_b"].reshape(1, 8),
        "wts0": np.concatenate([a["L0_ffn_w1"], rows(a["L0_ffn_w2"])], axis=2),
        "wq1": dh(a["L1_xattn_w_q"].T), "wk1": dh(a["L1_xattn_w_k"].T), "wv1": a["L1_xattn_w_v"].T, "wo1": a["L1_xattn_w_o"].T,
        "wts1": np.concatenate([a["L1_ffn_W1"], a["L1_ffn_b1"].reshape(8, 4, 128).transpose(0, 2, 1), rows(a["L1_ffn_W2"])], axis=2),
        "b2": a["L1_ffn_b2"],
    }
    arrays = {k: np.ascontiguousarray(v) for k, v in arrays.items()}
    nc = bacc.Bacc("TRN2", target_bir_lowering=False, num_devices=1)
    aps = {k: nc.dram_tensor("in_" + k, v.shape, mybir.dt.from_np(v.dtype), kind="ExternalInput").ap() for k, v in arrays.items()}
    out = nc.dram_tensor("out_x", _OUT, mybir.dt.float32, kind="ExternalOutput").ap()
    build(nc, aps, out)
    r = run_bass_kernel_spmd(nc, [{"in_" + k: v for k, v in arrays.items()}], core_ids=[0])
    return r.results[0]["out_x"]
```
